# Optimizing a Trainium2 kernel written in Bass

```python
import numpy as np
import jax
import jax.numpy as jnp

def _softmax(x, axis=-1):
    return jax.nn.softmax(x, axis=axis)

def _gelu(x):
    return jax.nn.gelu(x, approximate=True)

def _silu(x):
    return jax.nn.silu(x)

def _sigmoid(x):
    return jax.nn.sigmoid(x)

def _layernorm(x, axis=-1, eps=1e-05):
    m = jnp.mean(x, axis=axis, keepdims=True)
    v = jnp.var(x, axis=axis, keepdims=True)
    return (x - m) / jnp.sqrt(v + eps)

def _scatter_add(tgt, idx, src, axis=0):
    return tgt.at[idx].add(src)

def _segment_sum(src, seg, n):
    return jax.ops.segment_sum(src, seg, n)
kernel_name = 'mk_hybrid_d1_jaxref_r4_4eb8dd'

def setup_inputs(seed: int=0):
    np.random.seed(seed)
    _w = jnp.asarray

    def _L0_attn_a_setup():
        import jax, jax.numpy as jnp
        import numpy as np
        import math
        NUM_HEADS = 16
        D_MODEL = 256
        B, T = (1, 1024)
        key = jax.random.key(seed)
        kx, kq, kk, kv, ko = jax.random.split(key, 5)
        s = 1.0 / math.sqrt(D_MODEL)
        return {'x': jax.random.normal(kx, (B, T, D_MODEL), dtype=jnp.float32), 'Wq': jax.random.normal(kq, (D_MODEL, D_MODEL), dtype=jnp.float32) * s, 'Wk': jax.random.normal(kk, (D_MODEL, D_MODEL), dtype=jnp.float32) * s, 'Wv': jax.random.normal(kv, (D_MODEL, D_MODEL), dtype=jnp.float32) * s, 'Wo': jax.random.normal(ko, (D_MODEL, D_MODEL), dtype=jnp.float32) * s}
    _L0_attn_a_in = _L0_attn_a_setup()

    def _L0_attn_b_setup():
        import jax, jax.numpy as jnp
        import numpy as np
        DIM = 256
        B, S = (8, 512)
        LN_EPS = 1e-05
        key = jax.random.key(seed)
        k1, k2, k3 = jax.random.split(key, 3)
        x = jax.random.normal(k1, (B, S, DIM), dtype=jnp.float32)
        w_qkv = jax.random.normal(k2, (3 * DIM, DIM), dtype=jnp.float32) * np.sqrt(2.0 / (DIM + 3 * DIM))
        w_fc = jax.random.normal(k3, (DIM, DIM), dtype=jnp.float32) * np.sqrt(2.0 / (DIM + DIM))
        b_fc = jnp.zeros((DIM,), dtype=jnp.float32)
        gamma = jnp.ones((DIM,), dtype=jnp.float32)
        beta = jnp.zeros((DIM,), dtype=jnp.float32)
        return {'x': x, 'w_qkv': w_qkv, 'w_fc': w_fc, 'b_fc': b_fc, 'gamma': gamma, 'beta': beta}
    _L0_attn_b_in = _L0_attn_b_setup()

    def _L0_ffn_setup():
        import jax, jax.numpy as jnp
        import numpy as np
        B, S, D = (1, 512, 256)
        I = 512
        E = 8
        K = 2
        LIMIT = 7.0
        ALPHA = 1.702
        EPS = 1e-05

        def _swiglu(h):
            x_glu = jnp.minimum(h[..., ::2], LIMIT)
            x_lin = jnp.clip(h[..., 1::2], -LIMIT, LIMIT)
            return x_glu * jax.nn.sigmoid(ALPHA * x_glu) * (x_lin + 1.0)

        def _moe(t, gate_w, gate_b, mlp1_w, mlp1_b, mlp2_w, mlp2_b):
            T = t.shape[0]
            logits = t @ gate_w + gate_b
            top_v, top_i = jax.lax.top_k(logits, K)
            probs = jax.nn.softmax(top_v, axis=-1)
            w = jnp.zeros((T, E), t.dtype).at[jnp.arange(T)[:, None], top_i].set(probs)

            def body(acc, ew):
                w1, b1, w2, b2, we = ew
                h = _swiglu(t @ w1 + b1)
                y = h @ w2 + b2
                return (acc + we[:, None] * y, None)
            acc0 = jnp.zeros((T, t.shape[1]), t.dtype)
            acc, _ = jax.lax.scan(body, acc0, (mlp1_w, mlp1_b, mlp2_w, mlp2_b, w.T))
            return acc
        key = jax.random.key(seed)
        ks = jax.random.split(key, 4)
        s = 0.02
        return {'x': jax.random.normal(ks[0], (B, S, D), jnp.float32), 'norm_scale': jnp.ones((D,), jnp.float32), 'gate_w': jax.random.normal(ks[1], (D, E), jnp.float32) * s, 'gate_b': jnp.zeros((E,), jnp.float32), 'mlp1_w': jax.random.normal(ks[2], (E, D, 2 * I), jnp.float32) * s, 'mlp1_b': jnp.zeros((E, 2 * I), jnp.float32), 'mlp2_w': jax.random.normal(ks[3], (E, I, D), jnp.float32) * s, 'mlp2_b': jnp.zeros((E, D), jnp.float32)}
    _L0_ffn_in = _L0_ffn_setup()
    _d = {'L0_attn_a_x': _L0_attn_a_in['x'], 'L0_attn_a_Wq': _L0_attn_a_in['Wq'], 'L0_attn_a_Wk': _L0_attn_a_in['Wk'], 'L0_attn_a_Wv': _L0_attn_a_in['Wv'], 'L0_attn_a_Wo': _L0_attn_a_in['Wo'], 'L0_attn_b_w_qkv': _L0_attn_b_in['w_qkv'], 'L0_attn_b_w_fc': _L0_attn_b_in['w_fc'], 'L0_attn_b_b_fc': _L0_attn_b_in['b_fc'], 'L0_attn_b_gamma': _L0_attn_b_in['gamma'], 'L0_attn_b_beta': _L0_attn_b_in['beta'], 'L0_ffn_norm_scale': _L0_ffn_in['norm_scale'], 'L0_ffn_gate_w': _L0_ffn_in['gate_w'], 'L0_ffn_gate_b': _L0_ffn_in['gate_b'], 'L0_ffn_mlp1_w': _L0_ffn_in['mlp1_w'], 'L0_ffn_mlp1_b': _L0_ffn_in['mlp1_b'], 'L0_ffn_mlp2_w': _L0_ffn_in['mlp2_w'], 'L0_ffn_mlp2_b': _L0_ffn_in['mlp2_b']}
    _x0 = _d['L0_attn_a_x']
    _d['L0_attn_a_x'] = jax.random.normal(jax.random.fold_in(jax.random.key(seed), 1), (4, 1024, 256), dtype=_x0.dtype)
    del _x0
    return _d

def reference(L0_attn_a_x, L0_attn_a_Wq, L0_attn_a_Wk, L0_attn_a_Wv, L0_attn_a_Wo, L0_attn_b_w_qkv, L0_attn_b_w_fc, L0_attn_b_b_fc, L0_attn_b_gamma, L0_attn_b_beta, L0_ffn_norm_scale, L0_ffn_gate_w, L0_ffn_gate_b, L0_ffn_mlp1_w, L0_ffn_mlp1_b, L0_ffn_mlp2_w, L0_ffn_mlp2_b):

    def _L0_attn_a_ref(x, Wq, Wk, Wv, Wo):
        import jax, jax.numpy as jnp
        import numpy as np
        import math
        NUM_HEADS = 16
        D_MODEL = 256
        B, T = (1, 1024)
        Bx, Tx, D = x.shape
        H = NUM_HEADS
        dk = D // H
        q = (x @ Wq.T).reshape(Bx, Tx, H, dk)
        k = (x @ Wk.T).reshape(Bx, Tx, H, dk)
        v = (x @ Wv.T).reshape(Bx, Tx, H, dk)
        scores = jnp.einsum('bthd,bshd->bhts', q, k) / math.sqrt(dk)
        causal_mask = jnp.triu(jnp.ones((Tx, Tx), dtype=bool), k=1)
        scores = jnp.where(causal_mask, jnp.float32(-jnp.inf), scores).astype(jnp.float32)
        attn = jax.nn.softmax(scores, axis=-1)
        out = jnp.einsum('bhts,bshd->bthd', attn, v).reshape(Bx, Tx, D)
        return out @ Wo.T

    def _L0_attn_b_ref(x, w_qkv, w_fc, b_fc, gamma, beta):
        import jax, jax.numpy as jnp
        import numpy as np
        DIM = 256
        B, S = (8, 512)
        LN_EPS = 1e-05
        scaling = DIM ** (-0.5)
        qkv = jnp.einsum('bsd,ed->bse', x, w_qkv)
        q, k, v = jnp.split(qkv, 3, axis=-1)
        att = jax.nn.softmax(jnp.einsum('bqd,bkd->bqk', q, k) * scaling, axis=-1)
        y = jnp.einsum('bqk,bvd->bqd', att, v)
        y = jnp.einsum('bqd,ed->bqe', y, w_fc) + b_fc
        h = x + y
        mu = jnp.mean(h, axis=-1, keepdims=True)
        var = jnp.var(h, axis=-1, keepdims=True)
        return (h - mu) * jax.lax.rsqrt(var + LN_EPS) * gamma + beta

    def _L0_ffn_ref(x, norm_scale, gate_w, gate_b, mlp1_w, mlp1_b, mlp2_w, mlp2_b):
        import jax, jax.numpy as jnp
        import numpy as np
        B, S, D = (1, 512, 256)
        I = 512
        E = 8
        K = 2
        LIMIT = 7.0
        ALPHA = 1.702
        EPS = 1e-05

        def _swiglu(h):
            x_glu = jnp.minimum(h[..., ::2], LIMIT)
            x_lin = jnp.clip(h[..., 1::2], -LIMIT, LIMIT)
            return x_glu * jax.nn.sigmoid(ALPHA * x_glu) * (x_lin + 1.0)

        def _moe(t, gate_w, gate_b, mlp1_w, mlp1_b, mlp2_w, mlp2_b):
            T = t.shape[0]
            logits = t @ gate_w + gate_b
            top_v, top_i = jax.lax.top_k(logits, K)
            probs = jax.nn.softmax(top_v, axis=-1)
            w = jnp.zeros((T, E), t.dtype).at[jnp.arange(T)[:, None], top_i].set(probs)

            def body(acc, ew):
                w1, b1, w2, b2, we = ew
                h = _swiglu(t @ w1 + b1)
                y = h @ w2 + b2
                return (acc + we[:, None] * y, None)
            acc0 = jnp.zeros((T, t.shape[1]), t.dtype)
            acc, _ = jax.lax.scan(body, acc0, (mlp1_w, mlp1_b, mlp2_w, mlp2_b, w.T))
            return acc
        Bx, Sx, Dx = x.shape
        ms = jnp.mean(x * x, axis=-1, keepdims=True)
        t = (x * jax.lax.rsqrt(ms + EPS) * norm_scale).reshape(Bx * Sx, Dx)
        y = _moe(t, gate_w, gate_b, mlp1_w, mlp1_b, mlp2_w, mlp2_b)
        return x + y.reshape(Bx, Sx, Dx)
    x = L0_attn_a_x
    x = x + _L0_attn_a_ref(_layernorm(x, axis=-1), L0_attn_a_Wq, L0_attn_a_Wk, L0_attn_a_Wv, L0_attn_a_Wo)
    x = x + _L0_ffn_ref(_layernorm(x, axis=-1), L0_ffn_norm_scale, L0_ffn_gate_w, L0_ffn_gate_b, L0_ffn_mlp1_w, L0_ffn_mlp1_b, L0_ffn_mlp2_w, L0_ffn_mlp2_b)
    x = x + _L0_attn_b_ref(_layernorm(x, axis=-1), L0_attn_b_w_qkv, L0_attn_b_w_fc, L0_attn_b_b_fc, L0_attn_b_gamma, L0_attn_b_beta)
    x = x + _L0_ffn_ref(_layernorm(x, axis=-1), L0_ffn_norm_scale, L0_ffn_gate_w, L0_ffn_gate_b, L0_ffn_mlp1_w, L0_ffn_mlp1_b, L0_ffn_mlp2_w, L0_ffn_mlp2_b)
    return x

_drawn_inputs = setup_inputs


def setup_inputs(seed=0):
    import zlib

    import numpy as np

    out = dict(_drawn_inputs(seed))
    spreads = {'L0_attn_b_b_fc': (0.0, 0.8),
     'L0_attn_b_gamma': (1.0, 0.2),
     'L0_attn_b_beta': (0.0, 0.1),
     'L0_ffn_norm_scale': (1.0, 0.6),
     'L0_ffn_gate_b': (0.0, 0.1),
     'L0_ffn_mlp1_b': (0.0, 0.1),
     'L0_ffn_mlp2_b': (0.0, 0.1)}
    factors = {}
    for name, (base, spread) in spreads.items():
        noise = np.random.default_rng([zlib.crc32(name.encode()), seed]).standard_normal(out[name].shape)
        drawn = base * np.exp(spread * noise) if base else spread * noise
        out[name] = jnp.asarray(drawn.astype(out[name].dtype))
    for name, factor in factors.items():
        out[name] = (out[name] * factor).astype(out[name].dtype)
    return out
```

```python
from contextlib import ExitStack

import concourse.bass as bass
from concourse import mybir

F32 = mybir.dt.float32
BF16 = mybir.dt.bfloat16
I32 = mybir.dt.int32
ALU = mybir.AluOpType
ACT = mybir.ActivationFunctionType
AX = mybir.AxisListType

P = 128
B, S, D = 4, 1024, 256
T = B * S
NT = T // P
KD = D // P
EPS = 1e-5

H, DK = 16, 16
HG = 4
U = B * H // HG
QB = S // P
PAD = 32
NEG = -1e30
Q_PART = (0, 0, 1, 0, 2, 1)
K_PART = (0, 1, 0, 2, 0, 1)
ROWS = len(Q_PART) * DK
MROWS = 3

E, I = 8, 512
KI = I // P
LIMIT, ALPHA = 7.0, 1.702
MT = 2 * T // P + E
SLOTS = MT * P


def paired(eng, count, body, lead=1):
    pairs = count // 2
    for i in range(lead):
        for s in range(2):
            body(2 * i + s, s, i == 0, i == pairs - 1)
    if pairs > lead + 1:
        with eng.Fori(lead, pairs - 1, 1) as i:
            for s in range(2):
                body(2 * i + s, s, False, False)
    for s in range(2):
        body(count - 2 + s, s, False, True)


class Mem:

    def __init__(self, nc, ctx, tag="", spent=None, whole=None):
        self.nc, self.ctx, self.tag, self.spent, self.whole = nc, ctx, tag, spent, whole

    def sb(self, name, shape, dt=F32):
        return self.ctx.enter_context(self.nc.sbuf_tensor(self.tag + name, shape, dt))

    def ps(self, name, shape, dt=F32):
        return self.ctx.enter_context(self.nc.psum_tensor(self.tag + name, shape, dt))

    def sem(self, name):
        s = self.ctx.enter_context(self.nc.semaphore(self.tag + name))
        if self.spent is not None:
            assert s.num not in [t.num for t in self.spent], "a spent semaphore is used again"
            self.spent.append(s)
        return s

    def pool_dma_sem(self, name):
        return self.whole.enter_context(self.nc.semaphore(self.tag + name))


def project_qkv(nc, mem, g, x_dram, qk_dram, v_dram):
    CH = T // 512
    n = mem.sb("n", [P, 2, 4, D])
    nT = mem.sb("nT", [P, 2, KD, 512])
    stats = mem.sb("stats", [P, 4, 6])
    mv = mem.sb("mv", [P, 2, 4, 2])
    std = mem.sb("std", [P, 2, 4])
    rstd = mem.sb("rstd", [P, 2, 4])
    part = mem.sb("part", [P, 2, 3, 512], BF16)
    rest = mem.sb("rest", [P, 2, 512])
    vpad = mem.sb("vpad", [P, 2, 4, H, PAD])
    w3 = mem.sb("wqkv", [P, 3, KD, D])
    p_t = mem.ps("p_t", [P, KD, 512])
    p_qk = mem.ps("p_qk", [P, 2, 512])
    p_v = mem.ps("p_v", [P, 2, 2, D])

    w_in = mem.sem("w_in")
    x_in = [mem.sem(f"x_in{s}") for s in range(2)]
    stats_done, mv_done, std_done, rstd_done = (mem.sem(s) for s in ("stats_d", "mv_d", "std_d", "rstd_d"))
    n_done, t_done, nT0_done, nT1_done = (mem.sem(s) for s in ("n_d", "t_d", "nT0_d", "nT1_d"))
    qk_done, hi_done, rest_done, mid_done, lo_done = (mem.sem(s) for s in ("qk_d", "hi_d", "rest_d", "mid_d", "lo_d"))
    v0_done, v1_done, v0_copied, v1_copied = (mem.sem(s) for s in ("v0_d", "v1_d", "v0_c", "v1_c"))
    pad_done = mem.sem("pad_d")
    part_out = [mem.pool_dma_sem(f"part_out{s}") for s in range(2)]
    v_out = [mem.pool_dma_sem(f"v_out{s}") for s in range(2)]

    with nc.Block() as block:
        @block.sync
        def _(sp):
            for m, w in enumerate((g["WqT"], g["WkT"], g["WvT"])):
                sp.dma_start(w3[:, m], w.rearrange("(k p) n -> p k n", p=P)).then_inc(w_in, 16)

            def step(c, s, first, last):
                if not first:
                    sp.wait_ge(x_in[s], 8 * (c - s))
                sp.dma_start(g["X"][:, bass.ds(c * 4, 4), :],
                             x_dram[bass.ds(c * 512, 512), :].rearrange("(t p) d -> p t d", p=P)
                             ).then_inc(x_in[s], 16)
            paired(sp, CH, step)

        @block.gpsimd
        def _(pool):
            pool.memset(vpad[:, :, :, :, DK:PAD], 0.0).then_inc(pad_done, 1)
            pool.wait_ge(pad_done, 1)
            pool.memset(vpad[:, :, :, :, DK:DK + 1], 1.0).then_inc(pad_done, 1)

            def step(c, s, first, last):
                for m in range(4):
                    slot = m % 2
                    pool.wait_ge(mid_done, 4 * c + m + 1)
                    pool.tensor_tensor(part[:, slot, 2], rest[:, slot], part[:, slot, 1],
                                       ALU.subtract).then_inc(lo_done, 1)
                    pool.wait_ge(lo_done, 4 * c + m + 1)
                    for r in range(3):
                        dst = qk_dram[r, m // 2, bass.ds(2 * (c - s) + 2 * (m % 2), 2), :, s * 512:(s + 1) * 512]
                        pool.dma_start(dst.rearrange("u r t -> (u r) t"), part[:, slot, r]).then_inc(part_out[slot], 16)
                pool.wait_ge(v0_copied, c + 1)
                pool.wait_ge(v1_copied, c + 1)
                for hg in range(HG):
                    pool.dma_start(v_dram[bass.ds(2 * (c - s) + hg, 1), s * 512:(s + 1) * 512, :]
                                   .rearrange("u (t p) d -> p (u t) d", p=P),
                                   vpad[:, s, :, hg * 4:hg * 4 + 4, :].rearrange("p t h d -> p t (h d)")
                                   ).then_inc(v_out[s], 16)
            paired(pool, CH, step)
            for s in range(2):
                pool.wait_ge(part_out[s], 48 * 2 * CH)
                pool.wait_ge(v_out[s], 64 * CH // 2)

        @block.scalar
        def _(act):
            def root(c, s):
                act.wait_ge(mv_done, c + 1)
                act.activation(std[:, s, :], mv[:, s, :, 1], ACT.Sqrt, bias=g["eps"][:, :]).then_inc(std_done, 1)

            root(0, 0)

            def step(c, s, first, last):
                act.wait_ge(t_done, c + 1)
                act.copy(nT[:, s, 1, :], p_t[:, 1, :]).then_inc(nT1_done, 1)
                for m in range(4):
                    slot = m % 2
                    act.wait_ge(qk_done, 4 * c + m + 1)
                    if not (first and s == 0 and m < 2):
                        act.wait_ge(part_out[slot], 96 * c + 48 * (m // 2))
                    act.copy(part[:, slot, 0], p_qk[:, slot, :]).then_inc(hi_done, 1)
                    act.wait_ge(rest_done, 4 * c + m + 1)
                    act.copy(part[:, slot, 1], rest[:, slot]).then_inc(mid_done, 1)
                    if m == 0 and not (last and s == 1):
                        root(c + 1, 1 - s)
                act.wait_ge(v0_done, c + 1)
                act.wait_ge(pad_done, 2)
                if not first:
                    act.wait_ge(v_out[s], 32 * (c - s))
                act.copy(vpad[:, s, 0:2, :, 0:DK], p_v[:, 0].rearrange("p t (h d) -> p t h d", h=H)
                         ).then_inc(v0_copied, 1)
            paired(act, CH, step)

        @block.vector
        def _(dve):
            def statistics(c, s):
                for t in range(4):
                    last = dve.bn_stats(stats[:, t, :], tile_of(g["X"], c * 4 + t))
                last.then_inc(stats_done, 1)

            def moments(c, s):
                for t in range(4):
                    last = dve.bn_aggr(mv[:, s, t, :], stats[:, t, :])
                last.then_inc(mv_done, 1)

            def inverse(c, s):
                dve.wait_ge(std_done, c + 1)
                dve.reciprocal(rstd[:, s, :], std[:, s, :]).then_inc(rstd_done, 1)

            def normalise(c, s):
                dve.wait_ge(rstd_done, c + 1)
                for t in range(4):
                    last = dve.tensor_scalar(n[:, s, t, :], tile_of(g["X"], c * 4 + t), mv[:, s, t, 0:1],
                                             rstd[:, s, t:t + 1], ALU.subtract, ALU.mult)
                last.then_inc(n_done, 1)

            dve.wait_ge(x_in[0], 16)
            statistics(0, 0)
            dve.wait_ge(stats_done, 1)
            moments(0, 0)
            inverse(0, 0)
            normalise(0, 0)

            def step(c, s, first, last):
                more = not (last and s == 1)
                if more:
                    dve.wait_ge(x_in[1 - s], 8 * (c + 1 - (1 - s)) + 16)
                dve.wait_ge(t_done, c + 1)
                dve.tensor_copy(nT[:, s, 0, :], p_t[:, 0, :]).then_inc(nT0_done, 1)
                if more:
                    statistics(c + 1, 1 - s)
                for m in range(4):
                    slot = m % 2
                    if more and m == 0:
                        dve.wait_ge(stats_done, c + 2)
                    if not (first and s == 0 and m < 2):
                        dve.wait_ge(lo_done, 4 * c + m - 1)
                    dve.wait_ge(hi_done, 4 * c + m + 1)
                    dve.tensor_tensor(rest[:, slot], p_qk[:, slot, :], part[:, slot, 0],
                                      ALU.subtract).then_inc(rest_done, 1)
                    if more:
                        if m == 0:
                            moments(c + 1, 1 - s)
                        if m == 1:
                            inverse(c + 1, 1 - s)
                        if m == 2:
                            normalise(c + 1, 1 - s)
                dve.wait_ge(v1_done, c + 1)
                dve.wait_ge(pad_done, 2)
                if not first:
                    dve.wait_ge(v_out[s], 32 * (c - s))
                dve.tensor_copy(vpad[:, s, 2:4, :, 0:DK], p_v[:, 1].rearrange("p t (h d) -> p t h d", h=H)
                                ).then_inc(v1_copied, 1)
            paired(dve, CH, step)

        @block.tensor
        def _(pe):
            pe.wait_ge(w_in, 48)

            def step(c, s, first, last):
                pe.wait_ge(n_done, c + 1)
                if not (first and s == 0):
                    pe.wait_ge(nT0_done, c)
                    pe.wait_ge(nT1_done, c)
                for k in range(KD):
                    for t in range(4):
                        mm = pe.transpose(p_t[:, k, t * P:(t + 1) * P], n[:, s, t, k * P:(k + 1) * P], g["ident"][:, :])
                mm.then_inc(t_done, 1)
                pe.wait_ge(nT0_done, c + 1)
                pe.wait_ge(nT1_done, c + 1)
                for m in range(4):
                    if not (first and s == 0 and m < 2):
                        pe.wait_ge(rest_done, 4 * c + m - 1)
                    for k in range(KD):
                        mm = pe.matmul(p_qk[:, m % 2, :], w3[:, m // 2, k, (m % 2) * P:(m % 2 + 1) * P],
                                       nT[:, s, k, :], start=(k == 0), stop=(k == KD - 1))
                    mm.then_inc(qk_done, 1)
                for half, (copied, done) in enumerate(((v0_copied, v0_done), (v1_copied, v1_done))):
                    if not (first and s == 0):
                        pe.wait_ge(copied, c)
                    for t in range(2):
                        for k in range(KD):
                            mm = pe.matmul(p_v[:, half, t, :], nT[:, s, k, (2 * half + t) * P:(2 * half + t + 1) * P],
                                           w3[:, 2, k, :], start=(k == 0), stop=(k == KD - 1))
                    mm.then_inc(done, 1)
            paired(pe, CH, step)


def sn_items():
    items = []
    for pair in range(HG // 2):
        hs = (2 * pair, 2 * pair + 1)
        for qb in range(2):
            w = (qb + 1) * P
            items.append(([(h, qb, 0, w, j * w) for j, h in enumerate(hs)], hs, w, qb))
        for qb in range(2, QB):
            for h in hs:
                w = min((qb + 1) * P, 512)
                items.append(([(h, qb, 0, w, 0)], (h,), w, qb))
        for qb in range(4, QB):
            w = (qb - 3) * P
            if w <= 2 * P:
                items.append(([(h, qb, 512, w, j * w) for j, h in enumerate(hs)], hs, w, qb + 4))
            else:
                for h in hs:
                    items.append(([(h, qb, 512, w, 0)], (h,), w, qb + 4))
    return items


def attend_a(nc, mem, g, qk_dram, v_dram, o_dram):
    items = sn_items()
    NI = len(items) + 1
    steps = [(kb, h) for kb in range(4) for h in range(HG)] + [(kb, h) for kb in range(4, QB) for h in (0, 2)]
    NS = len(steps)
    ends = [max(i for i, st in enumerate(steps) if st[0] == kb) + 1 for kb in range(QB)]

    Kst = mem.sb("Kst", [P, 2, HG, S], BF16)
    Qst = mem.sb("Qst", [P, 2, HG, S], BF16)
    Vst = mem.sb("Vst", [P, 2, QB, P])
    Pt = mem.sb("Pt", [P, 2, HG, S])
    OT = mem.sb("OT", [P, 2, 512])
    mx = mem.sb("mx", [P, HG, 12])
    mrest = mem.sb("mrest", [P, HG, QB])
    mpart = mem.sb("mpart", [P, MROWS, HG, QB], BF16)
    mT = mem.sb("mT", [MROWS * HG * QB, 2, P], BF16)
    p_st = mem.ps("p_st", [P, 2, 2, 512])
    p_sn = mem.ps("p_sn", [P, 2, 512])
    p_o = mem.ps("p_o", [P, 2, 512])

    kq_in = [mem.sem(f"kq_in{pair}") for pair in range(2)]
    v_in, m_in, ones_done = (mem.sem(s) for s in ("v_in", "m_in", "ones_d"))
    sn_done, sn_read, mx_step, mT_done = (mem.sem(s) for s in ("sn_d", "sn_r", "mx_step", "mT_d"))
    mp_done = mem.sem("mp_d")
    st_done, exp_done, mask_done, pv_done = (mem.sem(s) for s in ("st_d", "exp_d", "mask_d", "pv_d"))
    o_copied = [mem.sem(f"o_c{c}") for c in range(2)]
    o_out = [mem.sem(f"o_out{c}") for c in range(2)]

    with nc.Block() as block:
        @block.sync
        def _(sp):
            def load(u, s):
                for pair in range(2):
                    for c in range(len(Q_PART)):
                        for dst, which, r in ((Kst, 1, K_PART[c]), (Qst, 0, Q_PART[c])):
                            src = qk_dram[r, which, bass.ds(u, 1), pair * 32:(pair + 1) * 32, :]
                            sp.dma_start(dst[c * DK:(c + 1) * DK, s, 2 * pair:2 * pair + 2, :],
                                         src.rearrange("u (h d) t -> d (u h) t", d=DK)).then_inc(kq_in[pair], 16)

            def load_v(u, s):
                sp.dma_start(Vst[:, s], v_dram[bass.ds(u, 1), :, :].rearrange("u (k p) d -> p (u k) d", p=P)
                             ).then_inc(v_in, 16)

            def max_rows(u, s):
                sp.wait_ge(mT_done, u + 1)
                for r in range(MROWS):
                    sp.dma_start(Qst[ROWS + r:ROWS + r + 1, s, :, :].rearrange("p h (q t) -> p (h q) t", t=P),
                                 mT[r * HG * QB:(r + 1) * HG * QB, s, :]).then_inc(m_in, 16)

            load(0, 0)
            load_v(0, 0)
            max_rows(0, 0)

            def step(u, s, first, last):
                if not (last and s == 1):
                    if not (first and s == 0):
                        sp.wait_ge(st_done, NS * u)
                    load(u + 1, 1 - s)
                    if not (first and s == 0):
                        sp.wait_ge(pv_done, QB * u)
                    load_v(u + 1, 1 - s)
                    max_rows(u + 1, 1 - s)
            paired(sp, U, step)

        @block.gpsimd
        def _(pool):
            pool.memset(Kst[ROWS:P, :, :, :], 1.0).then_inc(ones_done, 1)

            def step(u, s, first, last):
                for kb in range(QB):
                    pool.wait_ge(exp_done, NS * u + ends[kb])
                    diag = Pt[:, kb % 2, :, kb * P:(kb + 1) * P]
                    pool.nop(nofuse=True)
                    pool.affine_select(out=diag, in_=diag, compare_op=ALU.is_ge, fill=0.0, base=0,
                                       pattern=[[0, HG], [1, P]], channel_multiplier=-1).then_inc(mask_done, 1)
            paired(pool, U, step)

        @block.scalar
        def _(act):
            def copy_out(u, c):
                act.wait_ge(pv_done, QB * u + (4 if c == 0 else QB))
                if not (isinstance(u, int) and u == 0):
                    act.wait_ge(o_out[c], 16 * u)
                act.copy(OT[:, c, :], p_o[:, c, :]).then_inc(o_copied[c], 1)

            def store(u, c):
                act.wait_ge(o_copied[c], u + 1)
                act.dma_start(o_dram[bass.ds(u, 1), :, c * 512:(c + 1) * 512].rearrange("u p t -> (u p) t"),
                              OT[:, c, :]).then_inc(o_out[c], 16)

            def step(u, s, first, last):
                for i, (kb, h) in enumerate(steps):
                    act.wait_ge(st_done, NS * u + i + 1)
                    if not (first and s == 0 and kb < 2):
                        act.wait_ge(pv_done, QB * u + kb - 1)
                    ring = p_st[:, i % 2]
                    if kb < 4:
                        out = Pt[:, kb % 2, h, kb * P:S]
                        inp = ring.rearrange("p a b -> p (a b)")[:, kb * P:S]
                    else:
                        out = Pt[:, kb % 2, h:h + 2, kb * P:S]
                        inp = ring[:, :, kb * P - 512:512]
                    act.activation(out, inp, ACT.Exp, scale=DK ** -0.5).then_inc(exp_done, 1)
                    if i == 6 and not (first and s == 0):
                        copy_out(u - 1, 1)
                    if i == 7 and not (first and s == 0):
                        store(u - 1, 1)
                    if i == ends[4]:
                        copy_out(u, 0)
                    if i == ends[4] + 1:
                        store(u, 0)
            paired(act, U, step)
            copy_out(U - 1, 1)
            store(U - 1, 1)
            for c in range(2):
                act.wait_ge(o_out[c], 16 * U)

        @block.vector
        def _(dve):
            def maxima(u, s, first):
                for k, (_, hs, w, place) in enumerate(items):
                    dve.wait_ge(sn_done, NI * u + k + 1)
                    dve.tensor_reduce(mx[:, hs[0]:hs[-1] + 1, place],
                                      p_sn[:, k % 2, 0:w * len(hs)].rearrange("p (h w) -> p h w", w=w),
                                      AX.X, ALU.max).then_inc(sn_read, 1)
                dve.wait_ge(sn_read, len(items) * (u + 1))
                dve.tensor_tensor(mx[:, :, 4:8], mx[:, :, 4:8], mx[:, :, 8:12], ALU.max).then_inc(mx_step, 1)
                dve.wait_ge(mx_step, 4 * u + 1)
                dve.tensor_scalar(mpart[:, 0], mx[:, :, 0:8], -1.0, None, ALU.mult).then_inc(mx_step, 1)
                dve.wait_ge(mx_step, 4 * u + 2)
                dve.scalar_tensor_tensor(out=mrest[:, :, :], in0=mx[:, :, 0:8], scalar=-1.0, in1=mpart[:, 0],
                                         op0=ALU.mult, op1=ALU.subtract).then_inc(mx_step, 1)
                dve.wait_ge(mx_step, 4 * u + 3)
                dve.tensor_copy(mpart[:, 1], mrest[:, :, :]).then_inc(mx_step, 1)
                dve.wait_ge(mx_step, 4 * u + 4)
                dve.tensor_tensor(mpart[:, 2], mrest[:, :, :], mpart[:, 1], ALU.subtract).then_inc(mp_done, 1)
                dve.wait_ge(sn_done, NI * u + NI)
                if not first:
                    dve.wait_ge(m_in, 48 * (u - 1))
                dve.tensor_copy(mT[:, s, :], p_sn[0:MROWS * HG * QB, 0, :].bitcast(BF16)[:, 0:P]
                                ).then_inc(mT_done, 1)

            maxima(0, 0, True)

            def step(u, s, first, last):
                if not (last and s == 1):
                    maxima(u + 1, 1 - s, first and s == 0)
            paired(dve, U, step)

        @block.tensor
        def _(pe):
            def scores_by_query(u, s, k, first):
                segments, hs, w, place = items[k]
                if k == 0 or k == len(items) // 2:
                    pe.wait_ge(kq_in[k * 2 // len(items)], 192 * (u + 1))
                if k >= 2:
                    pe.wait_ge(sn_read, len(items) * u + k - 1)
                elif not first:
                    pe.wait_ge(mT_done, u)
                for h, qb, k0, kw, col in segments:
                    out = p_sn[:, k % 2, col:col + kw]
                    diagonal = k0 + kw == (qb + 1) * P
                    mm = pe.matmul(out, Qst[0:ROWS, s, h, qb * P:(qb + 1) * P], Kst[0:ROWS, s, h, k0:k0 + kw],
                                   start=True, stop=True, skip_group_check=True)
                    if diagonal:
                        mm = pe.matmul(p_sn[:, k % 2, col + kw - P:col + kw], g["identb"][:, :], g["maskb"][:, :],
                                       start=False, stop=True, skip_group_check=True)
                mm.then_inc(sn_done, 1)

            def maxima_by_row(u, s):
                pe.wait_ge(mp_done, u + 1)
                pe.transpose(p_sn[0:MROWS * HG * QB, 0, :].bitcast(BF16)[:, 0:P],
                             mpart[:, :, :, :].rearrange("p r h q -> p (r h q)"), g["identb"][:, :]).then_inc(sn_done, 1)

            def scores_by_key(u, s, i, first):
                kb, h = steps[i]
                if not (first and s == 0 and i < 2):
                    pe.wait_ge(exp_done, NS * u + i - 1)
                if kb < 4:
                    spans = [(h, 0, kb * P, 512), (h, 1, 0, 512)]
                else:
                    spans = [(h + j, j, kb * P - 512, 512) for j in range(2)]
                for hh, bank, a, b in spans:
                    q0 = a + (512 * bank if kb < 4 else 512)
                    mm = pe.matmul(p_st[:, i % 2, bank, a:b], Kst[0:ROWS + MROWS, s, hh, kb * P:(kb + 1) * P],
                                   Qst[0:ROWS + MROWS, s, hh, q0:q0 + b - a], start=True, stop=True)
                mm.then_inc(st_done, 1)

            def values(u, s, kb, first):
                pe.wait_ge(mask_done, QB * u + kb + 1)
                if kb == 0:
                    pe.wait_ge(v_in, 16 * (u + 1))
                    if not first:
                        pe.wait_ge(o_copied[0], u)
                        pe.wait_ge(o_copied[1], u)
                for c in range(2):
                    if kb >= 4 * (c + 1):
                        continue
                    a = max(kb * P - 512 * c, 0)
                    for h in range(HG):
                        mm = pe.matmul(p_o[PAD * h:PAD * (h + 1), c, a:512], Vst[:, s, kb, PAD * h:PAD * (h + 1)],
                                       Pt[:, kb % 2, h, 512 * c + a:512 * (c + 1)],
                                       start=(kb == 0), stop=(kb == 4 * c + 3))
                mm.then_inc(pv_done, 1)

            pe.wait_ge(ones_done, 1)
            for k in range(len(items)):
                scores_by_query(0, 0, k, True)
            maxima_by_row(0, 0)
            start, end = ends[0], ends[4]

            def step(u, s, first, last):
                pe.wait_ge(m_in, 48 * (u + 1))
                done = 0
                more = not (last and s == 1)
                for i, (kb, h) in enumerate(steps):
                    scores_by_key(u, s, i, first)
                    if more and i >= start:
                        want = min(len(items), len(items) * (i + 1 - start) // (end - start))
                        while done < want:
                            scores_by_query(u + 1, 1 - s, done, False)
                            done += 1
                    if i + 1 == ends[0] and not (first and s == 0):
                        values(u - 1, 1 - s, QB - 1, False)
                    if i + 1 in ends and kb >= 1:
                        values(u, s, kb - 1, first and s == 0)
                    if more and i + 1 == ends[5]:
                        maxima_by_row(u + 1, 1 - s)

            paired(pe, U, step)
            values(U - 1, 1, QB - 1, False)


def tile_of(t, j):
    return t[:, bass.ds(j, 1), :].rearrange("p a d -> p (a d)")


def project_out(nc, mem, g, o_dram):
    W = HG * P
    Ot = mem.sb("Ot", [P, 2, HG, P])
    rec = mem.sb("rec", [P, 2, H])
    On = mem.sb("On", [P, 2, D])
    OnT = mem.sb("OnT", [P, 2, D])
    wo = mem.sb("wo", [P, KD, D])
    p_r = mem.ps("p_r", [P, 2, W])
    p_t = mem.ps("p_t", [P, 2, 512])
    p_x = mem.ps("p_x", [P, 2, 512])
    w_in = mem.sem("w_in")
    o_in = [mem.sem(f"o_in{s}") for s in range(2)]
    rows_done, rec_done, on_done, onT_done, t_done, px_done, x_done, st_done = (
        mem.sem(s) for s in ("rows_d", "rec_d", "on_d", "onT_d", "t_d", "px_d", "x_d", "st_d"))

    with nc.Block() as block:
        @block.sync
        def _(sp):
            sp.dma_start(wo[:, :, :], g["WoT"].rearrange("(k p) n -> p k n", p=P)).then_inc(w_in, 16)

            def step(j, s, first, last):
                if not first:
                    sp.wait_ge(rows_done, j - 1)
                src = o_dram[bass.ds((j // QB) * HG, HG), :, bass.ds((j % QB) * P, P)]
                sp.dma_start(Ot[:, s], src.rearrange("u p t -> p u t")).then_inc(o_in[s], 16)
            paired(sp, NT, step)

        @block.tensor
        def _(pe):
            pe.wait_ge(w_in, 16)

            def finish(j, s, first):
                pe.wait_ge(on_done, j + 1)
                for k in range(KD):
                    mm = pe.transpose(p_t[:, s, k * P:(k + 1) * P], On[:, s, k * P:(k + 1) * P], g["ident"][:, :])
                mm.then_inc(t_done, 1)
                pe.wait_ge(onT_done, j + 1)
                for k in range(KD):
                    mm = pe.matmul(p_x[:, s, 0:D], OnT[:, s, k * P:(k + 1) * P], wo[:, k, :],
                                   start=(k == 0), stop=(k == KD - 1))
                mm.then_inc(px_done, 1)

            def step(j, s, first, last):
                pe.wait_ge(o_in[s], 8 * (j - s) + 16)
                if not first:
                    pe.wait_ge(on_done, j - 1)
                for u in range(HG):
                    mm = pe.transpose(p_r[:, s, u * P:(u + 1) * P], Ot[:, s, u, :], g["ident"][:, :])
                mm.then_inc(rows_done, 1)
                if not (first and s == 0):
                    finish(j - 1, 1 - s, first)
            paired(pe, NT, step)
            finish(NT - 1, 1, False)

        @block.scalar
        def _(act):
            def step(j, s, first, last):
                act.wait_ge(t_done, j + 1)
                act.copy(OnT[:, s, :], p_t[:, s, 0:D]).then_inc(onT_done, 1)
            paired(act, NT, step)

        @block.vector
        def _(dve):
            def add(j, s):
                dve.wait_ge(px_done, j + 1)
                x = tile_of(g["X"], j)
                dve.tensor_tensor(x, p_x[:, s, 0:D], x, ALU.add).then_inc(x_done, 1)

            def step(j, s, first, last):
                if not first:
                    dve.wait_ge(x_done, j - 1)
                dve.wait_ge(rows_done, j + 1)
                rows = p_r[:, s, :].rearrange("p (h c) -> p h c", c=PAD)
                dve.reciprocal(rec[:, s, :], rows[:, :, DK]).then_inc(rec_done, 1)
                if not first:
                    dve.bn_stats(tile_of(g["st6"], j - 2), tile_of(g["X"], j - 2))
                dve.wait_ge(rec_done, j + 1)
                dve.tensor_tensor(On[:, s, :].rearrange("p (h d) -> p h d", d=DK), rows[:, :, 0:DK],
                                  rec[:, s, :].unsqueeze(2).to_broadcast([P, H, DK]), ALU.mult).then_inc(on_done, 1)
                if not (first and s == 0):
                    add(j - 1, 1 - s)
            paired(dve, NT, step)
            add(NT - 1, 1)
            dve.wait_ge(x_done, NT)
            for j in range(NT - 2, NT):
                last = dve.bn_stats(g["st6"][:, j, :], g["X"][:, j, :])
            last.then_inc(st_done, 1)
            dve.wait_ge(st_done, 1)
            for j in range(NT):
                dve.bn_aggr(g["mv"][:, j, :], g["st6"][:, j, :])


def route(nc, mem, g, xs_dram):
    n = mem.sb("n", [P, 2, D])
    t = mem.sb("t", [P, 2, D])
    tT = mem.sb("tT", [P, 2, D])
    var1 = mem.sb("var1", [P, NT])
    root = mem.sb("root", [P, 2, NT])
    inv = mem.sb("inv", [P, 2, NT])
    srep = mem.sb("srep", [P, D])
    gw = mem.sb("gw", [P, KD, E])
    gb = mem.sb("gb", [P, E])
    L = mem.sb("L", [P, NT, E])
    work = mem.sb("work", [P, NT, E])
    oh = [mem.sb(f"oh{r}", [P, NT, E]) for r in range(2)]
    best = mem.sb("best", [P, 4, NT])
    picks = mem.sb("picks", [P, E, NT], BF16)
    tot = mem.sb("tot", [P, E, NT])
    cum = mem.sb("cum", [P, E, NT])
    cnt = mem.sb("cnt", [P, 6, E])
    tiles = mem.sb("tiles", [P, MT, E])
    fslot = mem.sb("fslot", [P, MT])
    diff = mem.sb("diff", [P, 3, NT])
    p_t = mem.ps("p_t", [P, 2, 512])
    p_l = mem.ps("p_l", [P, 512])
    p_c = mem.ps("p_c", [P, 2, 512])
    c_in, chain, roots, n_done, t_done, added, tp_done, tT_done, l_done = (
        mem.sem(s) for s in ("c_in", "chain", "roots", "n_d", "t_d", "added", "tp_d", "tT_d", "l_d"))
    diff_done, exp_done, picks_done, counts_done, slots_done = (
        mem.sem(s) for s in ("diff_d", "exp_d", "picks_d", "cnt_d", "slots_d"))
    scattered = mem.pool_dma_sem("scattered")

    with nc.Block() as block:
        @block.sync
        def _(sp):
            sp.dma_start(srep[:, :], g["scale"].partition_broadcast(P)).then_inc(c_in, 16)
            sp.dma_start(gb[:, :], g["gate_b"].partition_broadcast(P)).then_inc(c_in, 16)
            sp.dma_start(gw[:, :, :], g["gate_w"].rearrange("(k p) e -> p k e", p=P)).then_inc(c_in, 16)

        @block.scalar
        def _(act):
            for r in range(2):
                act.wait_ge(chain, 1 if r == 0 else 4)
                act.activation(root[:, r, :], var1[:, :], ACT.Sqrt, bias=g["eps"][:, :]).then_inc(roots, 1)

            def step(j, s, first, last):
                act.wait_ge(tp_done, j + 1)
                act.copy(tT[:, s, :], p_t[:, s, 0:D]).then_inc(tT_done, 1)
            paired(act, NT, step)
            act.wait_ge(diff_done, 1)
            act.activation(diff[:, 1, :], diff[:, 0, :], ACT.Exp).then_inc(exp_done, 1)

        @block.vector
        def _(dve):
            count = [0]

            def link(ins):
                count[0] += 1
                ins.then_inc(chain, 1)
                dve.wait_ge(chain, count[0])

            link(dve.tensor_copy(var1[:, :], g["mv"][:, :, 1]))
            dve.wait_ge(roots, 1)
            link(dve.reciprocal(inv[:, 0, :], root[:, 0, :]))
            link(dve.tensor_tensor(var1[:, :], var1[:, :], inv[:, 0, :], ALU.mult))
            link(dve.tensor_tensor(var1[:, :], var1[:, :], inv[:, 0, :], ALU.mult))
            dve.wait_ge(roots, 2)
            link(dve.reciprocal(inv[:, 1, :], root[:, 1, :]))
            dve.wait_ge(c_in, 48)

            def step(j, s, first, last):
                if not first:
                    dve.wait_ge(added, j - 1)
                    dve.wait_ge(tp_done, j - 1)
                dve.tensor_scalar(n[:, s, :], tile_of(g["X"], j), g["mv"][:, bass.ds(j, 1), 0],
                                  inv[:, 0, bass.ds(j, 1)], ALU.subtract, ALU.mult).then_inc(n_done, 1)
                dve.wait_ge(n_done, j + 1)
                dve.scalar_tensor_tensor(out=t[:, s, :], in0=n[:, s, :], scalar=inv[:, 1, bass.ds(j, 1)],
                                         in1=srep[:, :], op0=ALU.mult, op1=ALU.mult).then_inc(t_done, 1)
            paired(dve, NT, step)

            dve.wait_ge(l_done, NT)
            link(dve.tensor_tensor(L[:, :, :], p_l[:, 0:NT * E].rearrange("p (i e) -> p i e", e=E),
                                   gb[:, :].unsqueeze(1).to_broadcast([P, NT, E]), ALU.add))
            rev = g["rev"][:, :].unsqueeze(1).to_broadcast([P, NT, E])
            for r in range(2):
                top, place = best[:, r, :], best[:, 2 + r, :]
                link(dve.tensor_reduce(top, L[:, :, :], AX.X, ALU.max))
                link(dve.tensor_tensor(work[:, :, :], L[:, :, :], top.unsqueeze(2).to_broadcast([P, NT, E]), ALU.is_ge))
                link(dve.tensor_tensor(work[:, :, :], work[:, :, :], rev, ALU.mult))
                link(dve.tensor_reduce(place, work[:, :, :], AX.X, ALU.max))
                link(dve.tensor_tensor(oh[r][:, :, :], rev, place.unsqueeze(2).to_broadcast([P, NT, E]), ALU.is_equal))
                if r == 0:
                    link(dve.scalar_tensor_tensor(out=L[:, :, :], in0=oh[0][:, :, :], scalar=NEG, in1=L[:, :, :],
                                                  op0=ALU.mult, op1=ALU.add))
            dve.tensor_tensor(diff[:, 0, :], best[:, 1, :], best[:, 0, :], ALU.subtract).then_inc(diff_done, 1)
            dve.tensor_tensor(picks[:, :, :], oh[0][:, :, :].rearrange("p i e -> p e i"),
                              oh[1][:, :, :].rearrange("p i e -> p e i"), ALU.add).then_inc(picks_done, 1)
            dve.wait_ge(exp_done, 1)
            link(dve.tensor_scalar(diff[:, 2, :], diff[:, 1, :], 1.0, None, ALU.add))
            link(dve.reciprocal(g["w"][:, 0, :], diff[:, 2, :]))
            link(dve.tensor_tensor(g["w"][:, 1, :], g["w"][:, 0, :], diff[:, 1, :], ALU.mult))
            dve.wait_ge(counts_done, 1)
            link(dve.tensor_copy(tot[:, :, :], p_c[:, 1, 0:E * NT].rearrange("p (e i) -> p e i", e=E)))
            flat = tot[:, :, :].rearrange("p e i -> p (e i)")
            link(dve.tensor_tensor_scan(cum[:, :, :].rearrange("p e i -> p (e i)"), g["ones"][:, 0:E * NT], flat,
                                        0.0, ALU.mult, ALU.add))
            link(dve.tensor_tensor(cum[:, :, :], cum[:, :, :], tot[:, :, :], ALU.subtract))
            link(dve.tensor_reduce(cnt[:, 0, :], tot[:, :, :], AX.X, ALU.add))
            cmp = work[:, :, :].rearrange("p i e -> p (i e)").rearrange("p (e i) -> p e i", e=E)
            link(dve.tensor_tensor(cmp, cnt[:, 0, :].unsqueeze(2).to_broadcast([P, E, NT]),
                                   g["tile_starts"][:, 0:NT].unsqueeze(1).to_broadcast([P, E, NT]), ALU.is_gt))
            link(dve.tensor_reduce(cnt[:, 1, :], cmp, AX.X, ALU.add))
            link(dve.tensor_tensor_scan(cnt[:, 2, :], g["ones"][:, 0:E], cnt[:, 1, :], 0.0, ALU.mult, ALU.add))
            link(dve.tensor_tensor(cnt[:, 3, :], cnt[:, 2, :], cnt[:, 1, :], ALU.subtract))
            link(dve.scalar_tensor_tensor(out=cnt[:, 4, :], in0=cnt[:, 3, :], scalar=float(P), in1=cum[:, :, 0],
                                          op0=ALU.mult, op1=ALU.subtract))
            link(dve.tensor_tensor(cum[:, :, :], cum[:, :, :], cnt[:, 4, :].unsqueeze(2).to_broadcast([P, E, NT]), ALU.add))
            link(dve.tensor_tensor(cum[:, :, :], p_c[:, 0, 0:E * NT].rearrange("p (e i) -> p e i", e=E), cum[:, :, :], ALU.add))
            for r in range(2):
                link(dve.tensor_tensor(work[:, :, :], oh[r][:, :, :], cum[:, :, :].rearrange("p e i -> p i e"), ALU.mult))
                link(dve.tensor_reduce(fslot[:, 0:NT], work[:, :, :], AX.X, ALU.add))
                dve.tensor_copy(g["slot"][:, r, :], fslot[:, 0:NT]).then_inc(slots_done, 1)
            link(dve.tensor_tensor(tiles[:, :, :], g["tile_no"][:, :].unsqueeze(2).to_broadcast([P, MT, E]),
                                   cnt[:, 2, :].unsqueeze(1).to_broadcast([P, MT, E]), ALU.is_ge))
            link(dve.tensor_reduce(fslot[:, :], tiles[:, :, :], AX.X, ALU.add))
            link(dve.tensor_scalar(g["expert"][:, :], fslot[:, :], float(E - 1), None, ALU.min))

        @block.tensor
        def _(pe):
            pe.wait_ge(c_in, 48)

            def logits(j, s):
                pe.wait_ge(tT_done, j + 1)
                for k in range(KD):
                    mm = pe.matmul(p_l[:, bass.ds(E * j, E)], tT[:, s, k * P:(k + 1) * P], gw[:, k, :],
                                   start=(k == 0), stop=(k == KD - 1), skip_group_check=True)
                mm.then_inc(l_done, 1)

            def step(j, s, first, last):
                pe.wait_ge(t_done, j + 1)
                if not first:
                    pe.wait_ge(tT_done, j - 1)
                for k in range(KD):
                    mm = pe.transpose(p_t[:, s, k * P:(k + 1) * P],
                                      t[:, s, k * P:(k + 1) * P], g["ident"][:, :])
                mm.then_inc(tp_done, 1)
                if not (first and s == 0):
                    logits(j - 1, 1 - s)
            paired(pe, NT, step)
            logits(NT - 1, 1)
            pe.wait_ge(picks_done, 1)
            flat = picks[:, :, :].rearrange("p e i -> p (e i)")
            pe.matmul(p_c[:, 0, 0:E * NT], g["before"][:, :], flat, start=True, stop=True)
            pe.matmul(p_c[:, 1, 0:E * NT], g["onesb"][:, :], flat, start=True, stop=True).then_inc(counts_done, 1)

        @block.gpsimd
        def _(pool):
            def step(j, s, first, last):
                pool.wait_ge(t_done, j + 1)
                x = tile_of(g["X"], j)
                pool.tensor_tensor(x, x, n[:, s, :], ALU.add)
                pool.tensor_copy(tile_of(g["R"], j), t[:, s, :]).then_inc(added, 1)
            paired(pool, NT, step)
            pool.wait_ge(slots_done, 2)
            pool.wait_ge(added, NT)
            for i in range(NT):
                for r in range(2):
                    pool.indirect_dma_start(out=xs_dram, out_offset=bass.IndirectOffsetOnAxis(
                        ap=g["slot"][:, r, i:i + 1], axis=0), in_=g["R"][:, i, :], in_offset=None
                    ).then_inc(scattered, 16)
            pool.wait_ge(scattered, 32 * NT)


def experts(nc, mem, g, xs_dram, ys_dram):
    xs = mem.sb("xs", [P, 2, D])
    tT = mem.sb("tT", [P, 2, D])
    glu = mem.sb("glu", [P, 2, I])
    sig = mem.sb("sig", [P, 2, I])
    lin = mem.sb("lin", [P, 2, I])
    hid = mem.sb("hid", [P, 2, I])
    hT = mem.sb("hT", [P, 2, I])
    y = mem.sb("y", [P, 2, D])
    p_g = mem.ps("p_g", [P, 2, I])
    p_l = mem.ps("p_l", [P, 2, I])
    p_t = mem.ps("p_t", [P, 512])
    p_h = mem.ps("p_h", [P, 512])
    p_y = mem.ps("p_y", [P, 512])
    xs_in = [mem.sem(f"xs_in{s}") for s in range(2)]
    y_out = [mem.sem(f"y_out{s}") for s in range(2)]
    tp_done, tT_done, g_done, l_done, glu_done, sig_done, lin_done, prod_done, hid_done, hp_done, hT_done, py_done, y_done = (
        mem.sem(s) for s in ("tp_d", "tT_d", "g_d", "l_d", "glu_d", "sig_d", "lin_d", "prod_d", "hid_d", "hp_d",
                             "hT_d", "py_d", "y_d"))

    with nc.Block() as block:
        @block.sync
        def _(sp):
            def store(j, s):
                sp.wait_ge(y_done, j + 1)
                sp.dma_start(ys_dram[bass.ds(j * P, P), :], y[:, s, :]).then_inc(y_out[s], 16)

            def step(j, s, first, last):
                if not (isinstance(j, int) and j < 2):
                    sp.wait_ge(tp_done, j - 1)
                sp.dma_start(xs[:, s, :], xs_dram[bass.ds(j * P, P), :]).then_inc(xs_in[s], 16)
                if not (isinstance(j, int) and j < 4):
                    store(j - 4, s)
            paired(sp, MT, step, 2)
            for t in range(MT - 4, MT):
                store(t, t % 2)
            for s in range(2):
                sp.wait_ge(y_out[s], 16 * MT // 2)

        @block.tensor
        def _(pe):
            pe.wait_ge(g["w_in"], 2 * 16 * E)

            def rows(j, s, first):
                pe.wait_ge(xs_in[s], 8 * (j - s) + 16)
                if not first:
                    pe.wait_ge(tT_done, j)
                for k in range(KD):
                    mm = pe.transpose(p_t[:, k * P:(k + 1) * P], xs[:, s, k * P:(k + 1) * P], g["ident"][:, :])
                mm.then_inc(tp_done, 1)

            def up(j, s, e, half, bank, done, read, first):
                if not first:
                    pe.wait_ge(read, j - 1)
                cols = slice(half * I, (half + 1) * I)
                for k in range(KD):
                    pe.matmul(bank[:, s, :], tT[:, s, k * P:(k + 1) * P],
                              g["w1"][:, bass.ds(e, 1), k, cols].rearrange("p a n -> p (a n)"), start=(k == 0), stop=False)
                pe.matmul(bank[:, s, :], g["pick_e"][:, bass.ds(e, 1), :].rearrange("p a n -> p (a n)"),
                          g["b1"][:, cols], start=False, stop=True).then_inc(done, 1)

            def hidden_rows(j, s, first):
                pe.wait_ge(hid_done, j + 1)
                if not first:
                    pe.wait_ge(hT_done, j)
                for k in range(KI):
                    mm = pe.transpose(p_h[:, k * P:(k + 1) * P], hid[:, s, k * P:(k + 1) * P], g["ident"][:, :])
                mm.then_inc(hp_done, 1)

            def down(j, s, first):
                e = pe.value_load(g["expert"][0:1, bass.ds(j, 1)], min_val=0, max_val=E - 1)
                pe.wait_ge(hT_done, j + 1)
                if not first:
                    pe.wait_ge(y_done, j)
                for k in range(KI):
                    pe.matmul(p_y[:, 0:D], hT[:, s, k * P:(k + 1) * P],
                              g["w2"][:, bass.ds(e, 1), k, :].rearrange("p a n -> p (a n)"), start=(k == 0), stop=False)
                pe.matmul(p_y[:, 0:D], g["pick_e"][:, bass.ds(e, 1), :].rearrange("p a n -> p (a n)"),
                          g["b2"][:, :], start=False, stop=True).then_inc(py_done, 1)

            rows(0, 0, True)

            def step(j, s, first, last):
                e = pe.value_load(g["expert"][0:1, bass.ds(j, 1)], min_val=0, max_val=E - 1)
                pe.wait_ge(tT_done, j + 1)
                if not (last and s == 1):
                    rows(j + 1, 1 - s, False)
                up(j, s, e, 0, p_g, g_done, glu_done, first)
                if not (first and s == 0):
                    hidden_rows(j - 1, 1 - s, first)
                up(j, s, e, 1, p_l, l_done, lin_done, first)
                if not (first and s == 0):
                    down(j - 1, 1 - s, first)
            paired(pe, MT, step)
            hidden_rows(MT - 1, 1, False)
            down(MT - 1, 1, False)

        @block.scalar
        def _(act):
            def rows(j, s, first):
                act.wait_ge(tp_done, j + 1)
                if not first:
                    act.wait_ge(l_done, j - 1)
                act.copy(tT[:, s, :], p_t[:, 0:D]).then_inc(tT_done, 1)

            def hidden(j, s, first):
                act.wait_ge(hp_done, j + 1)
                act.copy(hT[:, s, :], p_h[:, :]).then_inc(hT_done, 1)

            def result(j, s, first):
                act.wait_ge(py_done, j + 1)
                if not (isinstance(j, int) and j < 2):
                    act.wait_ge(y_out[s], 8 * (j - s))
                act.copy(y[:, s, :], p_y[:, 0:D]).then_inc(y_done, 1)

            rows(0, 0, True)

            def step(j, s, first, last):
                if not (last and s == 1):
                    rows(j + 1, 1 - s, first and s == 0)
                act.wait_ge(glu_done, j + 1)
                if not first:
                    act.wait_ge(hid_done, j - 1)
                act.activation(sig[:, s, :], glu[:, s, :], ACT.Sigmoid, scale=ALPHA).then_inc(sig_done, 1)
                if not (first and s == 0):
                    hidden(j - 1, 1 - s, first)
                    result(j - 1, 1 - s, first)
            paired(act, MT, step, 2)
            hidden(MT - 1, 1, False)
            result(MT - 1, 1, False)

        @block.vector
        def _(dve):
            def step(j, s, first, last):
                dve.wait_ge(g_done, j + 1)
                dve.tensor_scalar(glu[:, s, :], p_g[:, s, :], LIMIT, None, ALU.min).then_inc(glu_done, 1)
                dve.wait_ge(l_done, j + 1)
                dve.tensor_scalar(lin[:, s, :], p_l[:, s, :], LIMIT, -LIMIT, ALU.min, ALU.max).then_inc(lin_done, 1)
                dve.wait_ge(lin_done, j + 1)
                dve.scalar_tensor_tensor(out=lin[:, s, :], in0=lin[:, s, :], scalar=1.0, in1=glu[:, s, :],
                                         op0=ALU.add, op1=ALU.mult).then_inc(prod_done, 1)
                dve.wait_ge(prod_done, j + 1)
                dve.wait_ge(sig_done, j + 1)
                if not first:
                    dve.wait_ge(hp_done, j - 1)
                dve.tensor_tensor(hid[:, s, :], lin[:, s, :], sig[:, s, :], ALU.mult).then_inc(hid_done, 1)
            paired(dve, MT, step)


def combine(nc, mem, g, ys_dram, out=None):
    RING = 4
    got = mem.sb("got", [P, RING, 2, D])
    st6 = mem.sb("st6", [P, 2, 6])
    y_in = [mem.pool_dma_sem(f"y_in{r}") for r in range(RING)]
    half_done, x_done, st_done, stored = (mem.sem(s) for s in ("half_d", "x_d", "st_d", "stored"))

    with nc.Block() as block:
        @block.gpsimd
        def _(pool):
            for i in range(NT):
                if i >= RING:
                    pool.wait_ge(x_done, i - RING + 1)
                for r in range(2):
                    pool.indirect_dma_start(out=got[:, i % RING, r, :], out_offset=None, in_=ys_dram,
                                            in_offset=bass.IndirectOffsetOnAxis(ap=g["slot"][:, r, i:i + 1], axis=0)
                                            ).then_inc(y_in[i % RING], 16)

        @block.vector
        def _(dve):
            for i in range(NT):
                x = g["X"][:, i, :]
                dve.wait_ge(y_in[i % RING], 32 * (i // RING + 1))
                dve.scalar_tensor_tensor(out=x, in0=got[:, i % RING, 0, :], scalar=g["w"][:, 0, i:i + 1], in1=x,
                                         op0=ALU.mult, op1=ALU.add).then_inc(half_done, 1)
                dve.wait_ge(half_done, i + 1)
                dve.scalar_tensor_tensor(out=x, in0=got[:, i % RING, 1, :], scalar=g["w"][:, 1, i:i + 1], in1=x,
                                         op0=ALU.mult, op1=ALU.add).then_inc(x_done, 1)
                if out is None:
                    dve.wait_ge(x_done, i + 1)
                    dve.bn_stats(st6[:, i % 2, :], x).then_inc(st_done, 1)
                    dve.wait_ge(st_done, i + 1)
                    dve.bn_aggr(g["mv"][:, i, :], st6[:, i % 2, :])

        if out is not None:
            @block.sync
            def _(sp):
                for c in range(NT // 4):
                    sp.wait_ge(x_done, 4 * c + 4)
                    sp.dma_start(out[c * 512:(c + 1) * 512, :].rearrange("(t p) d -> p t d", p=P),
                                 g["X"][:, 4 * c:4 * c + 4, :]).then_inc(stored, 16)
                sp.wait_ge(stored, 16 * (NT // 4))


def attend_b(nc, mem, g, spent):
    SCALE = D ** -0.5
    before = list(spent)
    del spent[:]
    Mw = mem.sb("Mw", [P, KD, D])
    Nw = mem.sb("Nw", [P, KD, D])
    bias = mem.sb("bias", [P, D])
    std = mem.sb("std", [P, NT])
    inv = mem.sb("inv", [P, NT])
    n = mem.sb("n", [P, QB, D])
    nT = mem.sb("nT", [P, KD, S])
    gT = mem.sb("gT", [P, KD, S])
    wn = gT[:, 0, 0:3 * D].rearrange("p (m d) -> p m d", m=3), gT[:, 1, 0:3 * D].rearrange("p (m d) -> p m d", m=3)
    wfT = nT
    nsum = mem.sb("nsum", [P, KD])
    nsum_rep = mem.sb("nsum_rep", [P, KD, P])
    vsum = mem.sb("vsum", [P, D])
    small = mem.sb("small", [P, 2, 5])
    p_s = mem.ps("p_s", [P, 2, 2, 512])
    p_w = mem.ps("p_w", [P, 2, 512])
    p_v = mem.ps("p_v", [P, 512])
    IT = 8
    c_in, ww_done, ww_read, std_done, inv_done, n_done, nb_done, all_done = (
        mem.sem(s) for s in ("c_in", "ww_d", "ww_r", "std_d", "inv_d", "n_d", "nb_d", "all_d"))
    w_done = mem.sem("w_d")
    w_read = [mem.sem(f"w_r{s}") for s in range(2)]
    ns_done, rep_done, pv_done, vs_done = (mem.sem(s) for s in ("ns_d", "rep_d", "pv_d", "vs_d"))
    s_done, m_done, nm_done, e_done, r_done, t_done, h_done, st_done = (
        mem.sem(s) for s in ("s_d", "m_d", "nm_d", "e_d", "r_d", "t_d", "h_d", "st_d"))

    def batches(eng, body):
        body(0, True)
        with eng.Fori(1, B, 1) as b:
            body(b, False)

    def target(i):
        return (nT if i < 4 else gT)[:, (i % 4) // 2, i % 2 * 512:(i % 2 + 1) * 512]

    with nc.Block() as block:
        @block.sync
        def _(sp):
            w = g["w_qkv"].rearrange("(m k p) d -> k p m d", m=3, p=P)
            for k in range(KD):
                sp.dma_start(wn[k], w[k]).then_inc(c_in, 16)
                sp.dma_start(wfT[:, k, 0:D], g["w_fcT"][k * P:(k + 1) * P, :]).then_inc(c_in, 16)
            sp.dma_start(bias[:, :], g["b_fc"].partition_broadcast(P)).then_inc(c_in, 16)
            for s in before:
                sp.sem_clear(s)

        @block.gpsimd
        def _(pool):
            pool.wait_ge(c_in, 80)

            def body(b, first):
                pool.wait_ge(n_done, b + 1)
                pool.wait_ge(w_done, IT * b + 4)
                for t in range(QB):
                    last = pool.tensor_tensor(n[:, t, :], n[:, t, :], bias[:, :], ALU.add)
                last.then_inc(nb_done, 1)
            batches(pool, body)

        @block.scalar
        def _(act):
            act.activation(std[:, :], g["mv"][:, :, 1], ACT.Sqrt, bias=g["eps"][:, :]).then_inc(std_done, 1)

            def body(b, first):
                for i in range(0, IT, 2):
                    act.wait_ge(w_done, IT * b + i + 1)
                    act.copy(target(i), p_w[:, 0, :]).then_inc(w_read[0], 1)
                for q in range(QB):
                    s = q % 2
                    if not (first and q < 2):
                        act.wait_ge(t_done, QB * b + q - 1)
                    act.wait_ge(nm_done, QB * b + q + 1)
                    scores = p_s[:, s].rearrange("p a b -> p (a b)")
                    act.activation(scores, scores, ACT.Exp, scale=SCALE, bias=small[:, s, 1:2],
                                   accum_out=small[:, s, 2:3]).then_inc(e_done, 1)
            batches(act, body)

        @block.vector
        def _(dve):
            dve.wait_ge(std_done, 1)
            dve.reciprocal(inv[:, :], std[:, :]).then_inc(inv_done, 1)
            for i, w in enumerate((Mw, Nw)):
                for k in range(KD):
                    dve.wait_ge(ww_done, 2 * i + k + 1)
                    dve.tensor_copy(w[:, k, :], p_w[:, k, 0:D]).then_inc(ww_read, 1)
            dve.wait_ge(inv_done, 1)

            def body(b, first):
                if not first:
                    dve.wait_ge(h_done, QB * b)
                for t in range(QB):
                    j = b * QB + t
                    last = dve.tensor_scalar(n[:, t, :], tile_of(g["X"], j), g["mv"][:, bass.ds(j, 1), 0],
                                             inv[:, bass.ds(j, 1)], ALU.subtract, ALU.mult)
                last.then_inc(n_done, 1)
                for i in range(1, IT, 2):
                    dve.wait_ge(w_done, IT * b + i + 1)
                    dve.tensor_copy(target(i), p_w[:, 1, :]).then_inc(w_read[1], 1)
                dve.wait_ge(w_read[0], IT // 2 * b + 2)
                dve.wait_ge(w_read[1], IT // 2 * b + 2)
                dve.tensor_reduce(nsum[:, :], nT[:, :, :], AX.X, ALU.add).then_inc(ns_done, 1)
                dve.wait_ge(ns_done, b + 1)
                dve.tensor_copy(nsum_rep[:, :, :], nsum[:, :].unsqueeze(2).to_broadcast([P, KD, P])).then_inc(rep_done, 1)

                def maximum(q):
                    s = q % 2
                    dve.wait_ge(s_done, QB * b + q + 1)
                    dve.tensor_reduce(small[:, s, 0:1], p_s[:, s], AX.XY, ALU.max).then_inc(m_done, 1)
                    dve.wait_ge(m_done, QB * b + q + 1)
                    dve.tensor_scalar(small[:, s, 1:2], small[:, s, 0:1], -SCALE, None, ALU.mult).then_inc(nm_done, 1)

                def result(q):
                    s = q % 2
                    j = b * QB + q
                    dve.wait_ge(e_done, j + 1)
                    dve.reciprocal(small[:, s, 3:4], small[:, s, 2:3]).then_inc(r_done, 1)
                    dve.wait_ge(r_done, j + 1)
                    dve.tensor_tensor(small[:, s, 4:5], small[:, s, 2:3], small[:, s, 3:4], ALU.mult).then_inc(t_done, 1)
                    dve.wait_ge(t_done, j + 1)
                    dve.scalar_tensor_tensor(out=tile_of(g["R"], j), in0=vsum[:, :], scalar=small[:, s, 4:5],
                                             in1=n[:, q, :], op0=ALU.mult, op1=ALU.add).then_inc(h_done, 1)

                def statistics(q):
                    dve.bn_stats(tile_of(g["st6"], b * QB + q), tile_of(g["R"], b * QB + q)).then_inc(st_done, 1)

                maximum(0)
                dve.wait_ge(pv_done, b + 1)
                dve.tensor_copy(vsum[:, :], p_v[:, 0:D]).then_inc(vs_done, 1)
                dve.wait_ge(nb_done, b + 1)
                dve.wait_ge(vs_done, b + 1)
                for q in range(1, QB):
                    if q > 1:
                        dve.wait_ge(h_done, QB * b + q - 1)
                    maximum(q)
                    if q > 1:
                        statistics(q - 2)
                    result(q - 1)
                dve.wait_ge(h_done, QB * b + QB - 1)
                result(QB - 1)
                statistics(QB - 2)
            batches(dve, body)
            dve.wait_ge(h_done, NT)
            for b in range(B):
                j = b * QB + QB - 1
                last = dve.bn_stats(g["st6"][:, j, :], g["R"][:, j, :])
            last.then_inc(all_done, 1)
            dve.wait_ge(all_done, 1)
            dve.wait_ge(st_done, (QB - 1) * B)
            for j in range(NT):
                dve.bn_aggr(g["mv2"][:, j, :], g["st6"][:, j, :])

        @block.tensor
        def _(pe):
            pe.wait_ge(c_in, 80)
            for i in range(2):
                if i:
                    pe.wait_ge(ww_read, 2)
                for k in range(KD):
                    for e in range(KD):
                        lhs = wn[e][:, 2 * i, k * P:(k + 1) * P]
                        rhs = wn[e][:, 1, :] if i == 0 else wfT[:, e, 0:D]
                        mm = pe.matmul(p_w[:, k, 0:D], lhs, rhs, start=(e == 0), stop=(e == KD - 1))
                    mm.then_inc(ww_done, 1)
            pe.wait_ge(ww_read, 4)

            def body(b, first):
                def free(i):
                    if not (first and i < 2):
                        pe.wait_ge(w_read[i % 2], IT // 2 * b + i // 2)

                pe.wait_ge(n_done, b + 1)
                for i in range(4):
                    free(i)
                    k, half = i // 2, i % 2
                    for t in range(4):
                        mm = pe.transpose(p_w[:, i % 2, t * P:(t + 1) * P], n[:, 4 * half + t, k * P:(k + 1) * P],
                                          g["ident"][:, :])
                    mm.then_inc(w_done, 1)
                for i in range(4, IT):
                    free(i)
                    ko, half = (i - 4) // 2, i % 2
                    for k in range(KD):
                        mm = pe.matmul(p_w[:, i % 2, :], Mw[:, k, ko * P:(ko + 1) * P], nT[:, k, half * 512:(half + 1) * 512],
                                       start=(k == 0), stop=(k == KD - 1))
                    mm.then_inc(w_done, 1)
                for s in range(2):
                    pe.wait_ge(w_read[s], IT // 2 * (b + 1))
                for q in range(QB):
                    if not (first and q < 2):
                        pe.wait_ge(e_done, QB * b + q - 1)
                    for half in range(2):
                        for k in range(KD):
                            mm = pe.matmul(p_s[:, q % 2, half, :], gT[:, k, q * P:(q + 1) * P],
                                           nT[:, k, half * 512:(half + 1) * 512], start=(k == 0), stop=(k == KD - 1))
                    mm.then_inc(s_done, 1)
                    if q == 0:
                        pe.wait_ge(rep_done, b + 1)
                        if not first:
                            pe.wait_ge(vs_done, b)
                        for k in range(KD):
                            mm = pe.matmul(p_v[:, 0:D], nsum_rep[:, k, :], Nw[:, k, :], start=(k == 0), stop=(k == KD - 1))
                        mm.then_inc(pv_done, 1)
            batches(pe, body)


def add_b(nc, mem, g):
    a = mem.sb("a", [P, 2, D])
    std = mem.sb("std", [P, NT])
    inv = mem.sb("inv", [P, NT])
    gam = mem.sb("gam", [P, D])
    bet = mem.sb("bet", [P, D])
    c_in, std_done, inv_done, a_done, scaled, shifted, x_done, st_done = (
        mem.sem(s) for s in ("c_in", "std_d", "inv_d", "a_d", "scaled", "shifted", "x_d", "st_d"))

    with nc.Block() as block:
        @block.sync
        def _(sp):
            sp.dma_start(gam[:, :], g["gamma"].partition_broadcast(P)).then_inc(c_in, 16)
            sp.dma_start(bet[:, :], g["beta"].partition_broadcast(P)).then_inc(c_in, 16)

        @block.scalar
        def _(act):
            act.activation(std[:, :], g["mv2"][:, :, 1], ACT.Sqrt, bias=g["eps"][:, :]).then_inc(std_done, 1)

        @block.gpsimd
        def _(pool):
            pool.wait_ge(c_in, 32)

            def step(j, s, first, last):
                x = tile_of(g["X"], j)
                pool.tensor_tensor(x, x, bet[:, :], ALU.add).then_inc(shifted, 1)
                pool.wait_ge(a_done, j + 1)
                pool.tensor_tensor(a[:, s, :], a[:, s, :], gam[:, :], ALU.mult).then_inc(scaled, 1)
            paired(pool, NT, step)

        @block.vector
        def _(dve):
            dve.wait_ge(std_done, 1)
            dve.reciprocal(inv[:, :], std[:, :]).then_inc(inv_done, 1)
            dve.wait_ge(inv_done, 1)

            def finish(j, s):
                x = tile_of(g["X"], j)
                dve.wait_ge(scaled, j + 1)
                dve.wait_ge(shifted, j + 1)
                dve.tensor_tensor(x, x, a[:, s, :], ALU.add).then_inc(x_done, 1)

            def step(j, s, first, last):
                if not first:
                    dve.wait_ge(x_done, j - 1)
                dve.tensor_scalar(a[:, s, :], tile_of(g["R"], j), g["mv2"][:, bass.ds(j, 1), 0], inv[:, bass.ds(j, 1)],
                                  ALU.subtract, ALU.mult).then_inc(a_done, 1)
                if not first:
                    dve.bn_stats(tile_of(g["st6"], j - 2), tile_of(g["X"], j - 2))
                if not (first and s == 0):
                    finish(j - 1, 1 - s)
            paired(dve, NT, step)
            finish(NT - 1, 1)
            dve.wait_ge(x_done, NT)
            for j in range(NT - 2, NT):
                last = dve.bn_stats(g["st6"][:, j, :], g["X"][:, j, :])
            last.then_inc(st_done, 1)
            dve.wait_ge(st_done, 1)
            for j in range(NT):
                dve.bn_aggr(g["mv"][:, j, :], g["st6"][:, j, :])


def constants(nc, mem, g, xs_dram):
    g["ident"] = mem.sb("ident", [P, P])
    g["identb"] = mem.sb("identb", [P, P], BF16)
    g["maskb"] = mem.sb("maskb", [P, P], BF16)
    g["before"] = mem.sb("before", [P, P], BF16)
    g["onesb"] = mem.sb("onesb", [P, P], BF16)
    g["ones"] = mem.sb("ones", [P, E * NT])
    g["eps"] = mem.sb("eps", [P, 1])
    g["rev"] = mem.sb("rev", [P, E])
    g["tile_starts"] = mem.sb("tile_starts", [P, NT])
    g["tile_no"] = mem.sb("tile_no", [P, MT])
    set_done, = (mem.sem(s) for s in ("set_d",))
    g["zeroed"] = mem.sem("zeroed")
    zeros = g["R"]
    with nc.Block() as block:
        @block.gpsimd
        def _(pool):
            pool.memset(zeros[:, 0:8, :], 0.0).then_inc(set_done, 1)
            for name, value in (("ident", 0.0), ("identb", 0.0), ("maskb", 0.0), ("before", 1.0), ("onesb", 1.0),
                                ("ones", 1.0), ("eps", EPS)):
                pool.memset(g[name][:, :], value).then_inc(set_done, 1)
            pool.wait_ge(set_done, 8)
            for name in ("ident", "identb"):
                pool.affine_select(out=g[name][:, :], in_=g[name][:, :], compare_op=ALU.not_equal, fill=1.0, base=0,
                                   pattern=[[-1, P]], channel_multiplier=1)
            pool.affine_select(out=g["maskb"][:, :], in_=g["maskb"][:, :], compare_op=ALU.is_ge, fill=NEG, base=0,
                               pattern=[[-1, P]], channel_multiplier=1)
            pool.affine_select(out=g["before"][:, :], in_=g["before"][:, :], compare_op=ALU.is_gt, fill=0.0, base=0,
                               pattern=[[1, P]], channel_multiplier=-1)
            for name, base, step, count in (("rev", E, -1, E), ("tile_starts", 0, P, NT), ("tile_no", 0, 1, MT)):
                pool.iota(g[name][:, :], pattern=[[step, count]], base=base, channel_multiplier=0,
                          allow_small_or_imprecise_dtypes=True)

        @block.sync
        def _(sp):
            sp.wait_ge(set_done, 1)
            for i in range(MT // 8):
                sp.dma_start(xs_dram[i * 8 * P:(i + 1) * 8 * P, :].rearrange("(p t) d -> p t d", p=P), zeros[:, 0:8, :]
                             ).then_inc(g["zeroed"], 16)
            sp.wait_ge(g["zeroed"], 16 * (MT // 8))


def expert_weights(nc, mem, g):
    g["w1"] = mem.sb("w1", [P, E, KD, 2 * I])
    g["w2"] = mem.sb("w2", [P, E, KI, D])
    g["b1"] = mem.sb("b1", [P, 2 * I], BF16)
    g["b2"] = mem.sb("b2", [P, D], BF16)
    g["pick_e"] = mem.sb("pick_e", [P, E, P], BF16)
    g["w_in"] = mem.sem("w_in")


def split_biases(nc, mem, g):
    W = 2 * I + D
    raw = mem.sb("raw", [P, W])
    hi = mem.sb("hi", [P, W], BF16)
    mid = mem.sb("mid", [P, W], BF16)
    r = mem.sb("r", [P, W])
    out = mem.sb("out", [P, W])
    part = mem.sb("part", [P, 3])
    zero, b_in, sel, chain = (mem.sem(s) for s in ("zero", "b_in", "sel", "chain"))
    with nc.Block() as block:
        @block.sync
        def _(sp):
            for e in range(E):
                sp.dma_start(g["w1"][:, e], g["mlp1"][e].rearrange("(k p) n -> p k n", p=P)).then_inc(g["w_in"], 16)
                sp.dma_start(g["w2"][:, e], g["mlp2"][e].rearrange("(k p) n -> p k n", p=P)).then_inc(g["w_in"], 16)


        @block.scalar
        def _(act):
            act.wait_ge(zero, 1)
            for m in range(3):
                act.dma_start(raw[m * E:(m + 1) * E, 0:2 * I], g["mlp1_b"]).then_inc(b_in, 16)
                act.dma_start(raw[m * E:(m + 1) * E, 2 * I:W], g["mlp2_b"]).then_inc(b_in, 16)

        @block.gpsimd
        def _(pool):
            pool.memset(raw[:, :], 0.0).then_inc(zero, 1)
            pool.memset(part[:, :], 1.0).then_inc(sel, 1)
            pool.memset(g["pick_e"][:, :, :], 0.0).then_inc(sel, 1)
            pool.wait_ge(sel, 2)
            pool.affine_select(out=part[:, :], in_=part[:, :], compare_op=ALU.is_ge, fill=0.0, base=0,
                               pattern=[[-E, 3]], channel_multiplier=1).then_inc(sel, 1)
            pool.wait_ge(sel, 3)
            pool.affine_select(out=part[:, :], in_=part[:, :], compare_op=ALU.is_ge, fill=0.0, base=E - 1,
                               pattern=[[E, 3]], channel_multiplier=-1).then_inc(sel, 1)
            for m in range(3):
                pool.affine_select(out=g["pick_e"][:, :, :], in_=g["pick_e"][:, :, :], compare_op=ALU.not_equal,
                                   fill=1.0, base=-m * E, pattern=[[-1, E], [0, P]], channel_multiplier=1
                                   ).then_inc(sel, 1)
                pool.wait_ge(sel, 5 + m)

        @block.vector
        def _(dve):
            count = [0]

            def link(ins):
                count[0] += 1
                ins.then_inc(chain, 1)
                dve.wait_ge(chain, count[0])

            dve.wait_ge(b_in, 96)
            dve.wait_ge(sel, 4)
            link(dve.tensor_copy(hi[:, :], raw[:, :]))
            link(dve.tensor_tensor(r[:, :], raw[:, :], hi[:, :], ALU.subtract))
            link(dve.tensor_copy(mid[:, :], r[:, :]))
            link(dve.tensor_tensor(r[:, :], r[:, :], mid[:, :], ALU.subtract))
            link(dve.tensor_scalar(out[:, :], hi[:, :], part[:, 0:1], None, ALU.mult))
            link(dve.scalar_tensor_tensor(out=out[:, :], in0=mid[:, :], scalar=part[:, 1:2], in1=out[:, :],
                                          op0=ALU.mult, op1=ALU.add))
            link(dve.scalar_tensor_tensor(out=out[:, :], in0=r[:, :], scalar=part[:, 2:3], in1=out[:, :],
                                          op0=ALU.mult, op1=ALU.add))
            link(dve.tensor_copy(g["b1"][:, :], out[:, 0:2 * I]))
            link(dve.tensor_copy(g["b2"][:, :], out[:, 2 * I:W]))


def program(nc, a, out, stop=99):
    g = dict(a)
    qk_dram = nc.dram_tensor("qk_parts", [3, 2, U, HG * DK, S], BF16).ap()
    v_dram = nc.dram_tensor("v_padded", [U, S, HG * PAD], F32).ap()
    o_dram = nc.dram_tensor("o_rows", [U, P, S], F32).ap()
    xs_dram = nc.dram_tensor("slot_rows", [SLOTS, D], F32).ap()
    ys_dram = nc.dram_tensor("slot_results", [SLOTS, D], F32).ap()
    with ExitStack() as whole:
        keep = Mem(nc, whole)
        g["X"] = keep.sb("X", [P, NT, D])
        g["R"] = keep.sb("R", [P, NT, D])
        g["st6"] = keep.sb("st6", [P, NT, 6])
        g["mv"] = keep.sb("mv_all", [P, NT, 2])
        g["mv2"] = keep.sb("mv2_all", [P, NT, 2])
        g["w"] = keep.sb("w", [P, 2, NT])
        g["slot"] = keep.sb("slot", [P, 2, NT], I32)
        g["expert"] = keep.sb("expert", [P, MT], I32)
        constants(nc, keep, g, xs_dram)

        spent = []

        def phase(f, tag, *args, **kw):
            with ExitStack() as own:
                f(nc, Mem(nc, own, tag, spent, whole), g, *args, **kw)

        phase(project_qkv, "a1_", a["x"], qk_dram, v_dram)
        phase(attend_a, "a2_", qk_dram, v_dram, o_dram)
        expert_weights(nc, keep, g)
        phase(split_biases, "sb_")
        phase(project_out, "a3_", o_dram)
        if stop == 1:
            return save(nc, keep, g, out)
        phase(route, "r1_", xs_dram)
        phase(experts, "e1_", xs_dram, ys_dram)
        if stop == 2:
            return phase(combine, "c1_", ys_dram, out=out)
        phase(combine, "c1_", ys_dram)
        phase(attend_b, "b_", spent)
        phase(add_b, "ab_")
        if stop == 3:
            return save(nc, keep, g, out)
        phase(route, "r2_", xs_dram)
        phase(experts, "e2_", xs_dram, ys_dram)
        phase(combine, "c2_", ys_dram, out=out)


def save(nc, mem, g, out):
    stored = mem.sem("dbg_stored")
    with nc.Block() as block:
        @block.sync
        def _(sp):
            sp.dma_start(out.rearrange("(t p) d -> p t d", p=P), g["X"][:, :, :]).then_inc(stored, 16)
            sp.wait_ge(stored, 16)


def laid_out(inputs):
    import numpy as np
    v = {k.split("_", 1)[1]: np.asarray(a) for k, a in inputs.items()}
    c = np.ascontiguousarray
    m1 = v["ffn_mlp1_w"]
    b1 = v["ffn_mlp1_b"]
    return {
        "x": v["attn_a_x"].reshape(T, D),
        "WqT": c(v["attn_a_Wq"].T), "WkT": c(v["attn_a_Wk"].T), "WvT": c(v["attn_a_Wv"].T), "WoT": c(v["attn_a_Wo"].T),
        "w_qkv": c(v["attn_b_w_qkv"]), "w_fcT": c(v["attn_b_w_fc"].T),
        "b_fc": v["attn_b_b_fc"], "gamma": v["attn_b_gamma"], "beta": v["attn_b_beta"],
        "scale": v["ffn_norm_scale"], "gate_w": v["ffn_gate_w"], "gate_b": v["ffn_gate_b"],
        "mlp1": c(m1.reshape(E, D, I, 2).transpose(0, 1, 3, 2).reshape(E, D, 2 * I)),
        "mlp1_b": c(b1.reshape(E, I, 2).transpose(0, 2, 1).reshape(E, 2 * I)),
        "mlp2": c(v["ffn_mlp2_w"]), "mlp2_b": v["ffn_mlp2_b"],
    }


def kernel(**inputs):
    import concourse.bacc as bacc
    from concourse.bass_utils import run_bass_kernel_spmd

    nc = bacc.Bacc("TRN2", target_bir_lowering=False, num_devices=1)
    arrays = laid_out(inputs)
    aps = {k: nc.dram_tensor(f"in_{k}", a.shape, mybir.dt.from_np(a.dtype), kind="ExternalInput").ap()
           for k, a in arrays.items()}
    out = nc.dram_tensor("out", (T, D), F32, kind="ExternalOutput").ap()
    program(nc, aps, out)
    r = run_bass_kernel_spmd(nc, [{f"in_{k}": a for k, a in arrays.items()}], core_ids=[0])
    return r.results[0]["out"].reshape(B, S, D)
```

```python
from contextlib import ExitStack

import concourse.bass as bass
from concourse import mybir

F32 = mybir.dt.float32
BF16 = mybir.dt.bfloat16
I32 = mybir.dt.int32
ALU = mybir.AluOpType
ACT = mybir.ActivationFunctionType
AX = mybir.AxisListType

P = 128
B, S, D = 4, 1024, 256
T = B * S
NT = T // P
KD = D // P
EPS = 1e-5

H, DK = 16, 16
HG = 4
U = B * H // HG
QB = S // P
PAD = 32
NEG = -1e30
Q_PART = (0, 0, 0, 1, 1, 2)
K_PART = (0, 1, 2, 0, 1, 0)
Q_RUNS = ((0, 0, 3), (3, 1, 2), (5, 2, 1))
ROWS = len(Q_PART) * DK
MROWS = 3

E, I = 8, 512
KI = I // P
LIMIT, ALPHA = 7.0, 1.702
MT = 2 * T // P + E
SLOTS = MT * P


def paired(eng, count, body, lead=1):
    pairs = count // 2
    for i in range(lead):
        for s in range(2):
            body(2 * i + s, s, i == 0, i == pairs - 1)
    if pairs > lead + 1:
        with eng.Fori(lead, pairs - 1, 1) as i:
            for s in range(2):
                body(2 * i + s, s, False, False)
    for s in range(2):
        body(count - 2 + s, s, False, True)


def rotating(eng, body):
    for u in range(2):
        body(u, u % 3)
    with eng.Fori(0, (U - 4) // 3, 1) as i:
        for s in range(3):
            body(3 * i + (2 + s), (2 + s) % 3)
    for u in range(U - 2, U):
        body(u, u % 3)


class Mem:

    def __init__(self, nc, ctx, tag="", spent=None, whole=None):
        self.nc, self.ctx, self.tag, self.spent, self.whole = nc, ctx, tag, spent, whole

    def sb(self, name, shape, dt=F32):
        return self.ctx.enter_context(self.nc.sbuf_tensor(self.tag + name, shape, dt))

    def ps(self, name, shape, dt=F32):
        return self.ctx.enter_context(self.nc.psum_tensor(self.tag + name, shape, dt))

    def sem(self, name):
        s = self.ctx.enter_context(self.nc.semaphore(self.tag + name))
        if self.spent is not None:
            assert s.num not in [t.num for t in self.spent], "a spent semaphore is used again"
            self.spent.append(s)
        return s

    def pool_dma_sem(self, name):
        return self.whole.enter_context(self.nc.semaphore(self.tag + name))


def project_qkv(nc, mem, g, x_dram, qk_dram, v_dram):
    CH = T // 512
    n = mem.sb("n", [P, 2, 4, D])
    nT = mem.sb("nT", [P, 2, KD, 512])
    stats = mem.sb("stats", [P, 4, 6])
    mv = mem.sb("mv", [P, 2, 4, 2])
    std = mem.sb("std", [P, 2, 4])
    rstd = mem.sb("rstd", [P, 2, 4])
    part = mem.sb("part", [P, 2, 3, 512], BF16)
    rest = mem.sb("rest", [P, 2, 512])
    vpad = mem.sb("vpad", [P, 2, 4, H, PAD])
    w3 = mem.sb("wqkv", [P, 3, KD, D])
    p_t = mem.ps("p_t", [P, KD, 512])
    p_qk = mem.ps("p_qk", [P, 2, 512])
    p_v = mem.ps("p_v", [P, 2, 2, D])

    w_in = mem.sem("w_in")
    x_in = [mem.sem(f"x_in{s}") for s in range(2)]
    stats_done, mv_done, std_done, rstd_done = (mem.sem(s) for s in ("stats_d", "mv_d", "std_d", "rstd_d"))
    n_done, t_done, nT0_done, nT1_done = (mem.sem(s) for s in ("n_d", "t_d", "nT0_d", "nT1_d"))
    qk_done, hi_done, rest_done, mid_done, lo_done = (mem.sem(s) for s in ("qk_d", "hi_d", "rest_d", "mid_d", "lo_d"))
    v0_done, v1_done, v0_copied, v1_copied = (mem.sem(s) for s in ("v0_d", "v1_d", "v0_c", "v1_c"))
    pad_done = mem.sem("pad_d")
    part_out = [mem.sem(f"part_out{s}") for s in range(2)]
    v_out = [mem.sem(f"v_out{s}") for s in range(2)]

    with nc.Block() as block:
        @block.sync
        def _(sp):
            def load(c, s):
                sp.dma_start(g["X"][:, bass.ds(c * 4, 4), :],
                             x_dram[bass.ds(c * 512, 512), :].rearrange("(t p) d -> p t d", p=P)
                             ).then_inc(x_in[s], 16)

            def step(c, s, first, last):
                if not last:
                    sp.wait_ge(x_in[s], 8 * (c - s) + 16)
                    load(c + 2, s)
                store(c, s)

            def store(c, s):
                for m in range(4):
                    slot = m % 2
                    sp.wait_ge(lo_done, 4 * c + m + 1)
                    sp.nop(nofuse=True)
                    for u in range(2):
                        rows = slice(u * HG * DK, (u + 1) * HG * DK)
                        dst = qk_dram[m // 2, bass.ds(2 * (c - s) + 2 * (m % 2) + u, 1), :, :, s * 512:(s + 1) * 512]
                        sp.dma_start(dst.rearrange("u (r d) h t -> (u d h) r t", d=DK), part[rows, slot]
                                     ).then_inc(part_out[slot], 16)
                sp.wait_ge(v0_copied, c + 1)
                sp.nop(nofuse=True)
                sp.wait_ge(v1_copied, c + 1)
                sp.nop(nofuse=True)
                for hg in range(HG):
                    sp.dma_start(v_dram[bass.ds(2 * (c - s) + hg, 1), s * 512:(s + 1) * 512, :]
                                 .rearrange("u (t p) d -> p (u t) d", p=P),
                                 vpad[:, s, :, hg * 4:hg * 4 + 4, :].rearrange("p t h d -> p t (h d)")
                                 ).then_inc(v_out[s], 16)
            load(0, 0)
            for m, w in enumerate((g["WqT"], g["WkT"], g["WvT"])):
                sp.dma_start(w3[:, m], w.rearrange("(k p) n -> p k n", p=P)).then_inc(w_in, 16)
            load(1, 1)
            paired(sp, CH, step)
            for s in range(2):
                sp.wait_ge(part_out[s], 32 * 2 * CH)
                sp.wait_ge(v_out[s], 64 * CH // 2)

        @block.gpsimd
        def _(pool):
            pool.memset(vpad[:, :, :, :, DK:PAD], 0.0).then_inc(pad_done, 1)
            pool.wait_ge(pad_done, 1)
            pool.memset(vpad[:, :, :, :, DK:DK + 1], 1.0).then_inc(pad_done, 1)

            def step(c, s, first, last):
                for m in range(4):
                    slot = m % 2
                    pool.wait_ge(mid_done, 4 * c + m + 1)
                    pool.tensor_tensor(part[:, slot, 2], rest[:, slot], part[:, slot, 1],
                                       ALU.subtract).then_inc(lo_done, 1)
            paired(pool, CH, step)

        @block.scalar
        def _(act):
            def root(c, s):
                act.wait_ge(mv_done, c + 1)
                act.activation(std[:, s, :], mv[:, s, :, 1], ACT.Sqrt, bias=g["eps"][:, :]).then_inc(std_done, 1)

            root(0, 0)

            def step(c, s, first, last):
                act.wait_ge(t_done, c + 1)
                act.copy(nT[:, s, 1, :], p_t[:, 1, :]).then_inc(nT1_done, 1)
                for m in range(4):
                    slot = m % 2
                    act.wait_ge(qk_done, 4 * c + m + 1)
                    if not (first and s == 0 and m < 2):
                        act.wait_ge(part_out[slot], 64 * c + 32 * (m // 2))
                    act.copy(part[:, slot, 0], p_qk[:, slot, :]).then_inc(hi_done, 1)
                    act.wait_ge(rest_done, 4 * c + m + 1)
                    act.copy(part[:, slot, 1], rest[:, slot]).then_inc(mid_done, 1)
                    if m == 0 and not (last and s == 1):
                        root(c + 1, 1 - s)
                act.wait_ge(v0_done, c + 1)
                act.wait_ge(pad_done, 2)
                if not first:
                    act.wait_ge(v_out[s], 32 * (c - s))
                act.copy(vpad[:, s, 0:2, :, 0:DK], p_v[:, 0].rearrange("p t (h d) -> p t h d", h=H)
                         ).then_inc(v0_copied, 1)
            paired(act, CH, step)

        @block.vector
        def _(dve):
            def statistics(c, s):
                for t in range(4):
                    last = dve.bn_stats(stats[:, t, :], tile_of(g["X"], c * 4 + t))
                last.then_inc(stats_done, 1)

            def moments(c, s):
                for t in range(4):
                    last = dve.bn_aggr(mv[:, s, t, :], stats[:, t, :])
                last.then_inc(mv_done, 1)

            def inverse(c, s):
                dve.wait_ge(std_done, c + 1)
                dve.reciprocal(rstd[:, s, :], std[:, s, :]).then_inc(rstd_done, 1)

            def normalise(c, s):
                dve.wait_ge(rstd_done, c + 1)
                for t in range(4):
                    last = dve.tensor_scalar(n[:, s, t, :], tile_of(g["X"], c * 4 + t), mv[:, s, t, 0:1],
                                             rstd[:, s, t:t + 1], ALU.subtract, ALU.mult)
                last.then_inc(n_done, 1)

            dve.wait_ge(x_in[0], 16)
            statistics(0, 0)
            dve.wait_ge(stats_done, 1)
            moments(0, 0)
            inverse(0, 0)
            normalise(0, 0)

            def step(c, s, first, last):
                more = not (last and s == 1)
                if more:
                    dve.wait_ge(x_in[1 - s], 8 * (c + 1 - (1 - s)) + 16)
                dve.wait_ge(t_done, c + 1)
                dve.tensor_copy(nT[:, s, 0, :], p_t[:, 0, :]).then_inc(nT0_done, 1)
                if more:
                    statistics(c + 1, 1 - s)
                for m in range(4):
                    slot = m % 2
                    if more and m == 0:
                        dve.wait_ge(stats_done, c + 2)
                    if not (first and s == 0 and m < 2):
                        dve.wait_ge(lo_done, 4 * c + m - 1)
                    dve.wait_ge(hi_done, 4 * c + m + 1)
                    dve.tensor_tensor(rest[:, slot], p_qk[:, slot, :], part[:, slot, 0],
                                      ALU.subtract).then_inc(rest_done, 1)
                    if more:
                        if m == 0:
                            moments(c + 1, 1 - s)
                        if m == 1:
                            inverse(c + 1, 1 - s)
                        if m == 2:
                            normalise(c + 1, 1 - s)
                dve.wait_ge(v1_done, c + 1)
                dve.wait_ge(pad_done, 2)
                if not first:
                    dve.wait_ge(v_out[s], 32 * (c - s))
                dve.tensor_copy(vpad[:, s, 2:4, :, 0:DK], p_v[:, 1].rearrange("p t (h d) -> p t h d", h=H)
                                ).then_inc(v1_copied, 1)
            paired(dve, CH, step)

        @block.tensor
        def _(pe):
            pe.wait_ge(w_in, 48)

            def step(c, s, first, last):
                pe.wait_ge(n_done, c + 1)
                if not (first and s == 0):
                    pe.wait_ge(nT0_done, c)
                    pe.wait_ge(nT1_done, c)
                for k in range(KD):
                    for t in range(4):
                        mm = pe.transpose(p_t[:, k, t * P:(t + 1) * P], n[:, s, t, k * P:(k + 1) * P], g["ident"][:, :])
                mm.then_inc(t_done, 1)
                pe.wait_ge(nT0_done, c + 1)
                pe.wait_ge(nT1_done, c + 1)
                for m in range(4):
                    if not (first and s == 0 and m < 2):
                        pe.wait_ge(rest_done, 4 * c + m - 1)
                    for k in range(KD):
                        mm = pe.matmul(p_qk[:, m % 2, :], w3[:, m // 2, k, (m % 2) * P:(m % 2 + 1) * P],
                                       nT[:, s, k, :], start=(k == 0), stop=(k == KD - 1))
                    mm.then_inc(qk_done, 1)
                for half, (copied, done) in enumerate(((v0_copied, v0_done), (v1_copied, v1_done))):
                    if not (first and s == 0):
                        pe.wait_ge(copied, c)
                    for t in range(2):
                        for k in range(KD):
                            mm = pe.matmul(p_v[:, half, t, :], nT[:, s, k, (2 * half + t) * P:(2 * half + t + 1) * P],
                                           w3[:, 2, k, :], start=(k == 0), stop=(k == KD - 1))
                    mm.then_inc(done, 1)
            paired(pe, CH, step)


MT_ITEM = 2


def sn_items():
    items = []
    for pair in range(HG // 2):
        hs = (2 * pair, 2 * pair + 1)
        for qb in range(2):
            w = (qb + 1) * P
            items.append(([(h, qb, 0, w, j * w) for j, h in enumerate(hs)], hs, w, qb))
        for qb in range(2, QB):
            for h in hs:
                w = min((qb + 1) * P, 512)
                items.append(([(h, qb, 0, w, 0)], (h,), w, qb))
        for qb in range(4, QB):
            w = (qb - 3) * P
            if w <= 2 * P:
                items.append(([(h, qb, 512, w, j * w) for j, h in enumerate(hs)], hs, w, qb + 4))
            else:
                for h in hs:
                    items.append(([(h, qb, 512, w, 0)], (h,), w, qb + 4))
    narrow = next(i for i, it in enumerate(items) if i > 2 and len(it[0]) * it[2] <= 2 * P)
    items.insert(MT_ITEM, items.pop(narrow))
    return items


def expert_biases(mem, g):
    W = 2 * I + D
    raw = mem.sb("raw", [P, W])
    hi = mem.sb("hi", [P, W], BF16)
    mid = mem.sb("mid", [P, W], BF16)
    part = mem.sb("part", [P, 3])
    zero, b_in, sel, chain = (mem.sem(s) for s in ("zero", "b_in", "sel", "chain"))

    def clear(dve):
        dve.memset(raw[:, :], 0.0).then_inc(zero, 1)

    def load_biases(act):
        act.wait_ge(zero, 1)
        for m in range(3):
            act.dma_start(raw[m * E:(m + 1) * E, 0:2 * I], g["mlp1_b"]).then_inc(b_in, 16)
            act.dma_start(raw[m * E:(m + 1) * E, 2 * I:W], g["mlp2_b"]).then_inc(b_in, 16)

    def select_experts(pool):
        pool.memset(part[:, :], 1.0).then_inc(sel, 1)
        pool.memset(g["pick_e"][:, :, :], 0.0).then_inc(sel, 1)
        pool.wait_ge(sel, 2)
        pool.affine_select(out=part[:, :], in_=part[:, :], compare_op=ALU.is_ge, fill=0.0, base=0,
                           pattern=[[-E, 3]], channel_multiplier=1).then_inc(sel, 1)
        pool.wait_ge(sel, 3)
        pool.affine_select(out=part[:, :], in_=part[:, :], compare_op=ALU.is_ge, fill=0.0, base=E - 1,
                           pattern=[[E, 3]], channel_multiplier=-1).then_inc(sel, 1)
        for m in range(3):
            pool.affine_select(out=g["pick_e"][:, :, :], in_=g["pick_e"][:, :, :], compare_op=ALU.not_equal,
                               fill=1.0, base=-m * E, pattern=[[-1, E], [0, P]], channel_multiplier=1
                               ).then_inc(sel, 1)
            pool.wait_ge(sel, 5 + m)

    def split(dve):
        count = [0]

        def link(ins):
            count[0] += 1
            ins.then_inc(chain, 1)
            dve.wait_ge(chain, count[0])

        dve.wait_ge(b_in, 96)
        dve.wait_ge(sel, 4)
        link(dve.tensor_copy(hi[:, :], raw[:, :]))
        link(dve.tensor_tensor(raw[:, :], raw[:, :], hi[:, :], ALU.subtract))
        link(dve.tensor_copy(mid[:, :], raw[:, :]))
        link(dve.tensor_tensor(raw[:, :], raw[:, :], mid[:, :], ALU.subtract))
        link(dve.tensor_scalar(raw[:, :], raw[:, :], part[:, 2:3], None, ALU.mult))
        link(dve.scalar_tensor_tensor(out=raw[:, :], in0=mid[:, :], scalar=part[:, 1:2], in1=raw[:, :],
                                      op0=ALU.mult, op1=ALU.add))
        link(dve.scalar_tensor_tensor(out=raw[:, :], in0=hi[:, :], scalar=part[:, 0:1], in1=raw[:, :],
                                      op0=ALU.mult, op1=ALU.add))
        link(dve.tensor_copy(g["b1"][:, :], raw[:, 0:2 * I]))
        link(dve.tensor_copy(g["b2"][:, :], raw[:, 2 * I:W]))

    return clear, load_biases, select_experts, split


def attend_a(nc, mem, g, qk_dram, v_dram, o_dram, xs_dram):
    items = sn_items()
    NI = len(items)
    AHEAD = 14
    steps = [(kb, h) for kb in range(4) for h in range(HG)] + [(kb, h) for kb in range(4, QB) for h in (0, 2)]
    NS = len(steps)
    ends = [max(i for i, st in enumerate(steps) if st[0] == kb) + 1 for kb in range(QB)]
    LOADS = 16 * 2 * len(Q_RUNS)

    Kst = mem.sb("Kst", [P, 3, HG, S], BF16)
    Qst = mem.sb("Qst", [P, 3, HG, S], BF16)
    Vst = mem.sb("Vst", [P, 3, QB, P])
    Pt = mem.sb("Pt", [P, 2, HG, S])
    OT = mem.sb("OT", [P, 2, 512])
    mx = mem.sb("mx", [P, HG, 12])
    mrest = mem.sb("mrest", [P, HG, QB])
    mpart = mem.sb("mpart", [P, MROWS, HG, QB], BF16)
    mT = mem.sb("mT", [MROWS * HG * QB, P], BF16)
    p_st = mem.ps("p_st", [P, 2, 2, 512])
    p_sn = mem.ps("p_sn", [P, 2, 512])
    p_o = mem.ps("p_o", [P, 2, 512])
    p_mT = p_sn[0:MROWS * HG * QB, MT_ITEM % 2, :].bitcast(BF16)[:, 4 * P:5 * P]

    kq_in, v_in, m_in, ones_done = (mem.sem(s) for s in ("kq_in", "v_in", "m_in", "ones_d"))
    sn_done, sn_read, mx_step, mp_done = (mem.sem(s) for s in ("sn_d", "sn_r", "mx_step", "mp_d"))
    mr_done, mT_done = (mem.sem(s) for s in ("mr_d", "mT_d"))
    st_done, exp_done, mask_done, pv_done = (mem.sem(s) for s in ("st_d", "exp_d", "mask_d", "pv_d"))
    o_copied = [mem.sem(f"o_c{c}") for c in range(2)]
    o_out = [mem.sem(f"o_out{c}") for c in range(2)]

    clear, load_biases, select_experts, split = expert_biases(mem, g)

    def is_first(u):
        return isinstance(u, int) and u == 0

    with nc.Block() as block:
        @block.sync
        def _(sp):
            def load(u, s):
                for c, r, n in Q_RUNS:
                    k_part = qk_dram[1, bass.ds(u, 1), 0:n * DK, :, :].rearrange("u p h t -> p (u h t)")
                    q_part = qk_dram[0, bass.ds(u, 1), r * DK:(r + 1) * DK, :, :].rearrange("u d h t -> u d (h t)")
                    sp.dma_start(Kst[c * DK:(c + n) * DK, s, :, :].rearrange("p h t -> p (h t)"), k_part
                                 ).then_inc(kq_in, 16)
                    sp.dma_start(Qst[c * DK:(c + n) * DK, s, :, :].rearrange("p h t -> p (h t)"),
                                 q_part.broadcast_to([n, DK, HG * S])).then_inc(kq_in, 16)

            def load_v(u, s):
                sp.dma_start(Vst[:, s], v_dram[bass.ds(u, 1), :, :].rearrange("u (k p) d -> p (u k) d", p=P)
                             ).then_inc(v_in, 16)

            def max_rows(u, s):
                sp.wait_ge(mT_done, u + 1)
                for r in range(MROWS):
                    sp.dma_start(Qst[ROWS + r:ROWS + r + 1, s, :, :].rearrange("p h (q t) -> p (h q) t", t=P),
                                 mT[r * HG * QB:(r + 1) * HG * QB, :]).then_inc(m_in, 16)

            load(0, 0)
            sp.wait_ge(kq_in, LOADS)
            load(1, 1)
            load_v(0, 0)
            max_rows(0, 0)
            sp.wait_ge(v_in, 16)
            load_v(1, 1)

            def step(u, s):
                if not (isinstance(u, int) and u >= U - 2):
                    if is_first(u):
                        sp.wait_ge(kq_in, LOADS * 2)
                    else:
                        sp.wait_ge(st_done, NS * u)
                    sp.nop(nofuse=True)
                    load(u + 2, (s + 2) % 3)
                    if not is_first(u):
                        sp.wait_ge(pv_done, QB * u)
                    sp.nop(nofuse=True)
                    sp.wait_ge(v_in, 16 * (u + 2))
                    sp.nop(nofuse=True)
                    load_v(u + 2, (s + 2) % 3)
                if not (isinstance(u, int) and u == U - 1):
                    max_rows(u + 1, (s + 1) % 3)
                if isinstance(u, int) and u < 2:
                    for i in range(u, MT // 8, 2):
                        sp.dma_start(xs_dram[i * 8 * P:(i + 1) * 8 * P, :].rearrange("(p t) d -> p t d", p=P),
                                     g["R"][:, 0:8, :]).then_inc(g["zeroed"], 16)
            rotating(sp, step)
            sp.wait_ge(g["zeroed"], 16 * (MT // 8))

        @block.gpsimd
        def _(pool):
            select_experts(pool)

            def step(u, s, first, last):
                for kb in range(QB):
                    pool.wait_ge(exp_done, NS * u + ends[kb])
                    diag = Pt[:, kb % 2, :, kb * P:(kb + 1) * P]
                    pool.nop(nofuse=True)
                    pool.affine_select(out=diag, in_=diag, compare_op=ALU.is_ge, fill=0.0, base=0,
                                       pattern=[[0, HG], [1, P]], channel_multiplier=-1).then_inc(mask_done, 1)
            paired(pool, U, step)

        @block.scalar
        def _(act):
            load_biases(act)

            def copy_out(u, c):
                act.wait_ge(pv_done, QB * u + (4 if c == 0 else QB))
                if not (isinstance(u, int) and u == 0):
                    act.wait_ge(o_out[c], 16 * u)
                act.copy(OT[:, c, :], p_o[:, c, :]).then_inc(o_copied[c], 1)

            def store(u, c):
                act.wait_ge(o_copied[c], u + 1)
                act.dma_start(o_dram[bass.ds(u, 1), :, c * 512:(c + 1) * 512].rearrange("u p t -> (u p) t"),
                              OT[:, c, :]).then_inc(o_out[c], 16)

            def step(u, s, first, last):
                for i, (kb, h) in enumerate(steps):
                    act.wait_ge(st_done, NS * u + i + 1)
                    if not (first and s == 0 and kb < 2):
                        act.wait_ge(pv_done, QB * u + kb - 1)
                    ring = p_st[:, i % 2]
                    if kb < 4:
                        out = Pt[:, kb % 2, h, kb * P:S]
                        inp = ring.rearrange("p a b -> p (a b)")[:, kb * P:S]
                    else:
                        out = Pt[:, kb % 2, h:h + 2, kb * P:S]
                        inp = ring[:, :, kb * P - 512:512]
                    act.activation(out, inp, ACT.Exp, scale=DK ** -0.5).then_inc(exp_done, 1)
                    if i == 6 and not (first and s == 0):
                        copy_out(u - 1, 1)
                    if i == 7 and not (first and s == 0):
                        store(u - 1, 1)
                    if i == ends[4]:
                        copy_out(u, 0)
                    if i == ends[4] + 1:
                        store(u, 0)
            paired(act, U, step)
            copy_out(U - 1, 1)
            store(U - 1, 1)
            for c in range(2):
                act.wait_ge(o_out[c], 16 * U)

        @block.vector
        def _(dve):
            def maxima_row(u):
                dve.wait_ge(mr_done, u + 1)
                dve.tensor_copy(mT[:, :], p_mT).then_inc(mT_done, 1)

            def maxima(u, s):
                for k, (_, hs, w, place) in enumerate(items):
                    dve.wait_ge(sn_done, NI * u + k + 1)
                    dve.tensor_reduce(mx[:, hs[0]:hs[-1] + 1, place],
                                      p_sn[:, k % 2, 0:w * len(hs)].rearrange("p (h w) -> p h w", w=w),
                                      AX.X, ALU.max).then_inc(sn_read, 1)
                    if k == MT_ITEM and not is_first(u):
                        maxima_row(u - 1)
                dve.wait_ge(sn_read, NI * (u + 1))
                dve.tensor_tensor(mx[:, :, 4:8], mx[:, :, 4:8], mx[:, :, 8:12], ALU.max).then_inc(mx_step, 1)
                dve.wait_ge(mx_step, 4 * u + 1)
                dve.tensor_scalar(mpart[:, 0], mx[:, :, 0:8], -1.0, None, ALU.mult).then_inc(mx_step, 1)
                dve.wait_ge(mx_step, 4 * u + 2)
                dve.scalar_tensor_tensor(out=mrest[:, :, :], in0=mx[:, :, 0:8], scalar=-1.0, in1=mpart[:, 0],
                                         op0=ALU.mult, op1=ALU.subtract).then_inc(mx_step, 1)
                dve.wait_ge(mx_step, 4 * u + 3)
                dve.tensor_copy(mpart[:, 1], mrest[:, :, :]).then_inc(mx_step, 1)
                dve.wait_ge(mx_step, 4 * u + 4)
                dve.tensor_tensor(mpart[:, 2], mrest[:, :, :], mpart[:, 1], ALU.subtract).then_inc(mp_done, 1)

            clear(dve)
            dve.memset(Kst[ROWS:P, :, :, :], 1.0).then_inc(ones_done, 1)
            split(dve)
            rotating(dve, maxima)
            maxima_row(U - 1)

        @block.tensor
        def _(pe):
            def scores_by_query(u, s, k):
                segments, hs, w, place = items[k]
                if k == 0:
                    pe.wait_ge(kq_in, LOADS * (u + 1))
                if k >= 2 or not is_first(u):
                    pe.wait_ge(sn_read, NI * u + k - 1)
                if k == MT_ITEM + 2 and not is_first(u):
                    pe.wait_ge(mT_done, u)
                if k == MT_ITEM and not is_first(u):
                    maxima_by_row(u - 1)
                for h, qb, k0, kw, col in segments:
                    out = p_sn[:, k % 2, col:col + kw]
                    diagonal = k0 + kw == (qb + 1) * P
                    mm = pe.matmul(out, Qst[0:ROWS, s, h, qb * P:(qb + 1) * P], Kst[0:ROWS, s, h, k0:k0 + kw],
                                   start=True, stop=True, skip_group_check=True)
                    if diagonal:
                        mm = pe.matmul(p_sn[:, k % 2, col + kw - P:col + kw], g["identb"][:, :], g["maskb"][:, :],
                                       start=False, stop=True, skip_group_check=True)
                mm.then_inc(sn_done, 1)

            def maxima_by_row(u):
                pe.wait_ge(mp_done, u + 1)
                pe.transpose(p_mT, mpart[:, :, :, :].rearrange("p r h q -> p (r h q)"),
                             g["identb"][:, :]).then_inc(mr_done, 1)

            def scores_by_key(u, s, i):
                kb, h = steps[i]
                if not (is_first(u) and i < 2):
                    pe.wait_ge(exp_done, NS * u + i - 1)
                if kb < 4:
                    spans = [(h, 0, kb * P, 512), (h, 1, 0, 512)]
                else:
                    spans = [(h + j, j, kb * P - 512, 512) for j in range(2)]
                for hh, bank, a, b in spans:
                    q0 = a + (512 * bank if kb < 4 else 512)
                    mm = pe.matmul(p_st[:, i % 2, bank, a:b], Kst[0:ROWS + MROWS, s, hh, kb * P:(kb + 1) * P],
                                   Qst[0:ROWS + MROWS, s, hh, q0:q0 + b - a], start=True, stop=True)
                mm.then_inc(st_done, 1)

            def values(u, s, kb, c):
                if c == kb // 4:
                    pe.wait_ge(mask_done, QB * u + kb + 1)
                if kb == 0 and c == 0:
                    pe.wait_ge(v_in, 16 * (u + 1))
                    if not is_first(u):
                        pe.wait_ge(o_copied[0], u)
                        pe.wait_ge(o_copied[1], u)
                a = max(kb * P - 512 * c, 0)
                for h in range(HG):
                    mm = pe.matmul(p_o[PAD * h:PAD * (h + 1), c, a:512], Vst[:, s, kb, PAD * h:PAD * (h + 1)],
                                   Pt[:, kb % 2, h, 512 * c + a:512 * (c + 1)],
                                   start=(kb == 0), stop=(kb == 4 * c + 3))
                if c == 1:
                    mm.then_inc(pv_done, 1)

            work = []
            for i, (kb, h) in enumerate(steps):
                work.append(("scores", i, None, (QB - kb) * (1 if kb < 4 else 2)))
                if i + 1 == ends[0]:
                    work += [("values", QB - 1, c, HG * 1) for c in range(1, 2)]
                elif i + 1 in ends:
                    work += [("values", kb - 1, c, HG * (4 - max(kb - 1 - 4 * c, 0))) for c in range((kb - 1) // 4, 2)]
            total = sum(w[-1] for w in work)

            for k in range(NI):
                scores_by_query(0, 0, k)
            for k in range(AHEAD):
                scores_by_query(1, 1, k)
            pe.wait_ge(ones_done, 1)

            def step(u, s):
                pe.wait_ge(m_in, 48 * (u + 1))
                done = spent = 0
                left = U - 1 - u if isinstance(u, int) else U
                count = NI if left >= 2 else NI - AHEAD if left == 1 else 0
                for kind, i, c, cost in work:
                    if kind == "scores":
                        scores_by_key(u, s, i)
                    elif i < QB - 1:
                        values(u, s, i, c)
                    elif not is_first(u):
                        values(u - 1, (s + 2) % 3, i, c)
                    spent += cost
                    while done < min(count, NI * spent // total):
                        k = AHEAD + done
                        if k < NI:
                            scores_by_query(u + 1, (s + 1) % 3, k)
                        else:
                            scores_by_query(u + 2, (s + 2) % 3, k - NI)
                        done += 1
                    if left == 1 and done == count:
                        maxima_by_row(u + 1)
                        left = 0

            rotating(pe, step)
            values(U - 1, (U - 1) % 3, QB - 1, 1)


def tile_of(t, j):
    return t[:, bass.ds(j, 1), :].rearrange("p a d -> p (a d)")


def project_out(nc, mem, g, o_dram):
    W = HG * P
    Ot = mem.sb("Ot", [P, 2, HG, P])
    rec = mem.sb("rec", [P, 2, H])
    On = mem.sb("On", [P, 2, D])
    OnT = mem.sb("OnT", [P, 2, D])
    wo = mem.sb("wo", [P, KD, D])
    p_r = mem.ps("p_r", [P, 2, W])
    p_t = mem.ps("p_t", [P, 2, 512])
    p_x = mem.ps("p_x", [P, 2, 512])
    w_in = mem.sem("w_in")
    o_in = [mem.sem(f"o_in{s}") for s in range(2)]
    rows_done, rec_done, on_done, onT_done, t_done, px_done, x_done, st_done = (
        mem.sem(s) for s in ("rows_d", "rec_d", "on_d", "onT_d", "t_d", "px_d", "x_d", "st_d"))

    with nc.Block() as block:
        @block.sync
        def _(sp):
            sp.dma_start(wo[:, :, :], g["WoT"].rearrange("(k p) n -> p k n", p=P)).then_inc(w_in, 16)

            def step(j, s, first, last):
                if not first:
                    sp.wait_ge(rows_done, j - 1)
                src = o_dram[bass.ds((j // QB) * HG, HG), :, bass.ds((j % QB) * P, P)]
                sp.dma_start(Ot[:, s], src.rearrange("u p t -> p u t")).then_inc(o_in[s], 16)
                if s == 1:
                    e, k = j // (NT // E), (j // 2) % 2
                    sp.dma_start(g["w1"][:, bass.ds(e, 1), bass.ds(k, 1), :].rearrange("p e k n -> p (e k n)"),
                                 g["mlp1"][bass.ds(e, 1), bass.ds(k * P, P), :].rearrange("e p n -> p (e n)")
                                 ).then_inc(g["w_in"], 16)
                    sp.dma_start(g["w2"][:, bass.ds(e, 1), bass.ds(2 * k, 2), :].rearrange("p e k n -> p (e k) n"),
                                 g["mlp2"][bass.ds(e, 1), bass.ds(2 * k * P, 2 * P), :]
                                 .rearrange("e (k p) n -> p (e k) n", p=P)).then_inc(g["w_in"], 16)
            paired(sp, NT, step)

        @block.tensor
        def _(pe):
            pe.wait_ge(w_in, 16)

            def turn(j, s):
                pe.wait_ge(on_done, j + 1)
                for k in range(KD):
                    mm = pe.transpose(p_t[:, s, k * P:(k + 1) * P], On[:, s, k * P:(k + 1) * P], g["ident"][:, :])
                mm.then_inc(t_done, 1)

            def multiply(j, s):
                pe.wait_ge(onT_done, j + 1)
                for k in range(KD):
                    mm = pe.matmul(p_x[:, s, 0:D], OnT[:, s, k * P:(k + 1) * P], wo[:, k, :],
                                   start=(k == 0), stop=(k == KD - 1))
                mm.then_inc(px_done, 1)

            def step(j, s, first, last):
                pe.wait_ge(o_in[s], 8 * (j - s) + 16)
                if not first:
                    pe.wait_ge(on_done, j - 1)
                for u in range(HG):
                    mm = pe.transpose(p_r[:, s, u * P:(u + 1) * P], Ot[:, s, u, :], g["ident"][:, :])
                mm.then_inc(rows_done, 1)
                if not (first and s == 0):
                    turn(j - 1, 1 - s)
                if not first:
                    multiply(j - 2, s)
            paired(pe, NT, step)
            turn(NT - 1, 1)
            for t in range(NT - 2, NT):
                pe.wait_ge(x_done, t - 1)
                multiply(t, t % 2)

        @block.scalar
        def _(act):
            def step(j, s, first, last):
                act.wait_ge(t_done, j + 1)
                act.copy(OnT[:, s, :], p_t[:, s, 0:D]).then_inc(onT_done, 1)
            paired(act, NT, step)

        @block.vector
        def _(dve):
            def add(j, s):
                dve.wait_ge(px_done, j + 1)
                x = tile_of(g["X"], j)
                dve.tensor_tensor(x, p_x[:, s, 0:D], x, ALU.add).then_inc(x_done, 1)

            def step(j, s, first, last):
                dve.wait_ge(rows_done, j + 1)
                rows = p_r[:, s, :].rearrange("p (h c) -> p h c", c=PAD)
                dve.reciprocal(rec[:, s, :], rows[:, :, DK]).then_inc(rec_done, 1)
                dve.wait_ge(rec_done, j + 1)
                dve.tensor_tensor(On[:, s, :].rearrange("p (h d) -> p h d", d=DK), rows[:, :, 0:DK],
                                  rec[:, s, :].unsqueeze(2).to_broadcast([P, H, DK]), ALU.mult).then_inc(on_done, 1)
                if not (isinstance(j, int) and j < 3):
                    dve.wait_ge(x_done, j - 2)
                    dve.nop(nofuse=True)
                    dve.bn_stats(tile_of(g["st6"], j - 3), tile_of(g["X"], j - 3))
                if not first:
                    add(j - 2, s)
            paired(dve, NT, step, 2)
            add(NT - 2, 0)
            add(NT - 1, 1)
            dve.wait_ge(x_done, NT)
            for j in range(NT - 3, NT):
                last = dve.bn_stats(g["st6"][:, j, :], g["X"][:, j, :])
            last.then_inc(st_done, 1)
            dve.wait_ge(st_done, 1)
            for j in range(NT):
                dve.bn_aggr(g["mv"][:, j, :], g["st6"][:, j, :])


def route(nc, mem, g, xs_dram):
    n = mem.sb("n", [P, 2, D])
    t = mem.sb("t", [P, 2, D])
    tT = mem.sb("tT", [P, 2, D])
    var1 = mem.sb("var1", [P, NT])
    root = mem.sb("root", [P, 2, NT])
    inv = mem.sb("inv", [P, 2, NT])
    srep = mem.sb("srep", [P, D])
    gw = mem.sb("gw", [P, KD, E])
    gb = mem.sb("gb", [P, E])
    L = mem.sb("L", [P, NT, E])
    work = mem.sb("work", [P, NT, E])
    oh = [mem.sb(f"oh{r}", [P, NT, E]) for r in range(2)]
    best = mem.sb("best", [P, 4, NT])
    picks = mem.sb("picks", [P, E, NT], BF16)
    tot = mem.sb("tot", [P, E, NT])
    cum = mem.sb("cum", [P, E, NT])
    cnt = mem.sb("cnt", [P, 6, E])
    tiles = mem.sb("tiles", [P, MT, E])
    fslot = mem.sb("fslot", [P, MT])
    diff = mem.sb("diff", [P, 3, NT])
    p_t = mem.ps("p_t", [P, 2, 512])
    p_l = mem.ps("p_l", [P, 512])
    p_c = mem.ps("p_c", [P, 2, 512])
    c_in, chain, roots, n_done, t_done, added, tp_done, tT_done, l_done = (
        mem.sem(s) for s in ("c_in", "chain", "roots", "n_d", "t_d", "added", "tp_d", "tT_d", "l_d"))
    diff_done, exp_done, picks_done, counts_done, slots_done = (
        mem.sem(s) for s in ("diff_d", "exp_d", "picks_d", "cnt_d", "slots_d"))
    kept = mem.sem("kept")
    scattered = mem.pool_dma_sem("scattered")

    with nc.Block() as block:
        @block.sync
        def _(sp):
            sp.dma_start(srep[:, :], g["scale"].partition_broadcast(P)).then_inc(c_in, 16)
            sp.dma_start(gb[:, :], g["gate_b"].partition_broadcast(P)).then_inc(c_in, 16)
            sp.dma_start(gw[:, :, :], g["gate_w"].rearrange("(k p) e -> p k e", p=P)).then_inc(c_in, 16)

        @block.scalar
        def _(act):
            for r in range(2):
                act.wait_ge(chain, 1 if r == 0 else 4)
                act.activation(root[:, r, :], var1[:, :], ACT.Sqrt, bias=g["eps"][:, :]).then_inc(roots, 1)

            def step(j, s, first, last):
                act.wait_ge(tp_done, j + 1)
                act.copy(tT[:, s, :], p_t[:, s, 0:D]).then_inc(tT_done, 1)
                act.wait_ge(t_done, j + 1)
                act.copy(tile_of(g["R"], j), t[:, s, :]).then_inc(kept, 1)
            paired(act, NT, step)
            act.wait_ge(diff_done, 1)
            act.activation(diff[:, 1, :], diff[:, 0, :], ACT.Exp).then_inc(exp_done, 1)

        @block.vector
        def _(dve):
            count = [0]

            def link(ins):
                count[0] += 1
                ins.then_inc(chain, 1)
                dve.wait_ge(chain, count[0])

            link(dve.tensor_copy(var1[:, :], g["mv"][:, :, 1]))
            dve.wait_ge(roots, 1)
            link(dve.reciprocal(inv[:, 0, :], root[:, 0, :]))
            link(dve.tensor_tensor(var1[:, :], var1[:, :], inv[:, 0, :], ALU.mult))
            link(dve.tensor_tensor(var1[:, :], var1[:, :], inv[:, 0, :], ALU.mult))
            dve.wait_ge(roots, 2)
            link(dve.reciprocal(inv[:, 1, :], root[:, 1, :]))
            dve.wait_ge(c_in, 48)

            def step(j, s, first, last):
                if not first:
                    dve.wait_ge(added, j - 1)
                    dve.wait_ge(kept, j - 1)
                    dve.wait_ge(tp_done, j - 1)
                dve.tensor_scalar(n[:, s, :], tile_of(g["X"], j), g["mv"][:, bass.ds(j, 1), 0],
                                  inv[:, 0, bass.ds(j, 1)], ALU.subtract, ALU.mult).then_inc(n_done, 1)
                dve.wait_ge(n_done, j + 1)
                dve.scalar_tensor_tensor(out=t[:, s, :], in0=n[:, s, :], scalar=inv[:, 1, bass.ds(j, 1)],
                                         in1=srep[:, :], op0=ALU.mult, op1=ALU.mult).then_inc(t_done, 1)
            paired(dve, NT, step)

            dve.wait_ge(l_done, NT)
            link(dve.tensor_tensor(L[:, :, :], p_l[:, 0:NT * E].rearrange("p (i e) -> p i e", e=E),
                                   gb[:, :].unsqueeze(1).to_broadcast([P, NT, E]), ALU.add))
            rev = g["rev"][:, :].unsqueeze(1).to_broadcast([P, NT, E])
            for r in range(2):
                top, place = best[:, r, :], best[:, 2 + r, :]
                link(dve.tensor_reduce(top, L[:, :, :], AX.X, ALU.max))
                link(dve.tensor_tensor(work[:, :, :], L[:, :, :], top.unsqueeze(2).to_broadcast([P, NT, E]), ALU.is_ge))
                link(dve.tensor_tensor(work[:, :, :], work[:, :, :], rev, ALU.mult))
                link(dve.tensor_reduce(place, work[:, :, :], AX.X, ALU.max))
                link(dve.tensor_tensor(oh[r][:, :, :], rev, place.unsqueeze(2).to_broadcast([P, NT, E]), ALU.is_equal))
                if r == 0:
                    link(dve.scalar_tensor_tensor(out=L[:, :, :], in0=oh[0][:, :, :], scalar=NEG, in1=L[:, :, :],
                                                  op0=ALU.mult, op1=ALU.add))
            dve.tensor_tensor(diff[:, 0, :], best[:, 1, :], best[:, 0, :], ALU.subtract).then_inc(diff_done, 1)
            dve.tensor_tensor(picks[:, :, :], oh[0][:, :, :].rearrange("p i e -> p e i"),
                              oh[1][:, :, :].rearrange("p i e -> p e i"), ALU.add).then_inc(picks_done, 1)
            dve.wait_ge(exp_done, 1)
            link(dve.tensor_scalar(diff[:, 2, :], diff[:, 1, :], 1.0, None, ALU.add))
            link(dve.reciprocal(g["w"][:, 0, :], diff[:, 2, :]))
            link(dve.tensor_tensor(g["w"][:, 1, :], g["w"][:, 0, :], diff[:, 1, :], ALU.mult))
            dve.wait_ge(counts_done, 1)
            link(dve.tensor_copy(tot[:, :, :], p_c[:, 1, 0:E * NT].rearrange("p (e i) -> p e i", e=E)))
            flat = tot[:, :, :].rearrange("p e i -> p (e i)")
            link(dve.tensor_tensor_scan(cum[:, :, :].rearrange("p e i -> p (e i)"), g["ones"][:, 0:E * NT], flat,
                                        0.0, ALU.mult, ALU.add))
            link(dve.tensor_tensor(cum[:, :, :], cum[:, :, :], tot[:, :, :], ALU.subtract))
            link(dve.tensor_reduce(cnt[:, 0, :], tot[:, :, :], AX.X, ALU.add))
            cmp = work[:, :, :].rearrange("p i e -> p (i e)").rearrange("p (e i) -> p e i", e=E)
            link(dve.tensor_tensor(cmp, cnt[:, 0, :].unsqueeze(2).to_broadcast([P, E, NT]),
                                   g["tile_starts"][:, 0:NT].unsqueeze(1).to_broadcast([P, E, NT]), ALU.is_gt))
            link(dve.tensor_reduce(cnt[:, 1, :], cmp, AX.X, ALU.add))
            link(dve.tensor_tensor_scan(cnt[:, 2, :], g["ones"][:, 0:E], cnt[:, 1, :], 0.0, ALU.mult, ALU.add))
            link(dve.tensor_tensor(cnt[:, 3, :], cnt[:, 2, :], cnt[:, 1, :], ALU.subtract))
            link(dve.scalar_tensor_tensor(out=cnt[:, 4, :], in0=cnt[:, 3, :], scalar=float(P), in1=cum[:, :, 0],
                                          op0=ALU.mult, op1=ALU.subtract))
            link(dve.tensor_tensor(cum[:, :, :], cum[:, :, :], cnt[:, 4, :].unsqueeze(2).to_broadcast([P, E, NT]), ALU.add))
            link(dve.tensor_tensor(cum[:, :, :], p_c[:, 0, 0:E * NT].rearrange("p (e i) -> p e i", e=E), cum[:, :, :], ALU.add))
            for r in range(2):
                link(dve.tensor_tensor(work[:, :, :], oh[r][:, :, :], cum[:, :, :].rearrange("p e i -> p i e"), ALU.mult))
                link(dve.tensor_reduce(fslot[:, 0:NT], work[:, :, :], AX.X, ALU.add))
                dve.tensor_copy(g["slot"][:, r, :], fslot[:, 0:NT]).then_inc(slots_done, 1)
            link(dve.tensor_tensor(tiles[:, :, :], g["tile_no"][:, :].unsqueeze(2).to_broadcast([P, MT, E]),
                                   cnt[:, 2, :].unsqueeze(1).to_broadcast([P, MT, E]), ALU.is_ge))
            link(dve.tensor_reduce(fslot[:, :], tiles[:, :, :], AX.X, ALU.add))
            link(dve.tensor_scalar(g["expert"][:, :], fslot[:, :], float(E - 1), None, ALU.min))

        @block.tensor
        def _(pe):
            pe.wait_ge(c_in, 48)

            def logits(j, s):
                pe.wait_ge(tT_done, j + 1)
                for k in range(KD):
                    mm = pe.matmul(p_l[:, bass.ds(E * j, E)], tT[:, s, k * P:(k + 1) * P], gw[:, k, :],
                                   start=(k == 0), stop=(k == KD - 1), skip_group_check=True)
                mm.then_inc(l_done, 1)

            def step(j, s, first, last):
                pe.wait_ge(t_done, j + 1)
                if not first:
                    pe.wait_ge(tT_done, j - 1)
                for k in range(KD):
                    mm = pe.transpose(p_t[:, s, k * P:(k + 1) * P],
                                      t[:, s, k * P:(k + 1) * P], g["ident"][:, :])
                mm.then_inc(tp_done, 1)
                if not (first and s == 0):
                    logits(j - 1, 1 - s)
            paired(pe, NT, step)
            logits(NT - 1, 1)
            pe.wait_ge(picks_done, 1)
            flat = picks[:, :, :].rearrange("p e i -> p (e i)")
            pe.matmul(p_c[:, 0, 0:E * NT], g["before"][:, :], flat, start=True, stop=True)
            pe.matmul(p_c[:, 1, 0:E * NT], g["onesb"][:, :], flat, start=True, stop=True).then_inc(counts_done, 1)

        @block.gpsimd
        def _(pool):
            def step(j, s, first, last):
                pool.wait_ge(t_done, j + 1)
                x = tile_of(g["X"], j)
                pool.tensor_tensor(x, x, n[:, s, :], ALU.add).then_inc(added, 1)
            paired(pool, NT, step)
            pool.wait_ge(slots_done, 2)
            pool.wait_ge(kept, NT)
            for i in range(NT):
                for r in range(2):
                    pool.indirect_dma_start(out=xs_dram, out_offset=bass.IndirectOffsetOnAxis(
                        ap=g["slot"][:, r, i:i + 1], axis=0), in_=g["R"][:, i, :], in_offset=None
                    ).then_inc(scattered, 16)
            pool.wait_ge(scattered, 32 * NT)


def experts(nc, mem, g, xs_dram, ys_dram):
    xs = mem.sb("xs", [P, 2, D])
    tT = mem.sb("tT", [P, 2, D])
    glu = mem.sb("glu", [P, 2, I])
    sig = mem.sb("sig", [P, 2, I])
    lin = mem.sb("lin", [P, 2, I])
    hid = mem.sb("hid", [P, 2, I])
    hT = mem.sb("hT", [P, 2, I])
    y = mem.sb("y", [P, 2, D])
    p_g = mem.ps("p_g", [P, 2, I])
    p_l = mem.ps("p_l", [P, 2, I])
    p_t = mem.ps("p_t", [P, 512])
    p_h = mem.ps("p_h", [P, 512])
    p_y = mem.ps("p_y", [P, 512])
    xs_in = [mem.sem(f"xs_in{s}") for s in range(2)]
    y_out = [mem.sem(f"y_out{s}") for s in range(2)]
    tp_done, tT_done, g_done, l_done, glu_done, sig_done, lin_done, prod_done, hid_done, hp_done, hT_done, py_done, y_done = (
        mem.sem(s) for s in ("tp_d", "tT_d", "g_d", "l_d", "glu_d", "sig_d", "lin_d", "prod_d", "hid_d", "hp_d",
                             "hT_d", "py_d", "y_d"))

    with nc.Block() as block:
        @block.sync
        def _(sp):
            def store(j, s):
                sp.wait_ge(y_done, j + 1)
                sp.dma_start(ys_dram[bass.ds(j * P, P), :], y[:, s, :]).then_inc(y_out[s], 16)

            def step(j, s, first, last):
                if not (isinstance(j, int) and j < 2):
                    sp.wait_ge(tp_done, j - 1)
                sp.dma_start(xs[:, s, :], xs_dram[bass.ds(j * P, P), :]).then_inc(xs_in[s], 16)
                if not (isinstance(j, int) and j < 4):
                    store(j - 4, s)
            paired(sp, MT, step, 2)
            for t in range(MT - 4, MT):
                store(t, t % 2)
            for s in range(2):
                sp.wait_ge(y_out[s], 16 * MT // 2)

        @block.tensor
        def _(pe):
            pe.wait_ge(g["w_in"], 2 * 16 * NT // 2)

            def rows(j, s, first):
                pe.wait_ge(xs_in[s], 8 * (j - s) + 16)
                if not first:
                    pe.wait_ge(tT_done, j)
                for k in range(KD):
                    mm = pe.transpose(p_t[:, k * P:(k + 1) * P], xs[:, s, k * P:(k + 1) * P], g["ident"][:, :])
                mm.then_inc(tp_done, 1)

            def up(j, s, e, half, bank, done, read, first):
                if not first:
                    pe.wait_ge(read, j - 1)
                cols = slice(half * I, (half + 1) * I)
                for k in range(KD):
                    pe.matmul(bank[:, s, :], tT[:, s, k * P:(k + 1) * P],
                              g["w1"][:, bass.ds(e, 1), k, cols].rearrange("p a n -> p (a n)"), start=(k == 0), stop=False)
                pe.matmul(bank[:, s, :], g["pick_e"][:, bass.ds(e, 1), :].rearrange("p a n -> p (a n)"),
                          g["b1"][:, cols], start=False, stop=True).then_inc(done, 1)

            def hidden_rows(j, s, first):
                pe.wait_ge(hid_done, j + 1)
                if not first:
                    pe.wait_ge(hT_done, j)
                for k in range(KI):
                    mm = pe.transpose(p_h[:, k * P:(k + 1) * P], hid[:, s, k * P:(k + 1) * P], g["ident"][:, :])
                mm.then_inc(hp_done, 1)

            def down(j, s, first):
                e = pe.value_load(g["expert"][0:1, bass.ds(j, 1)], min_val=0, max_val=E - 1)
                pe.wait_ge(hT_done, j + 1)
                if not first:
                    pe.wait_ge(y_done, j)
                for k in range(KI):
                    pe.matmul(p_y[:, 0:D], hT[:, s, k * P:(k + 1) * P],
                              g["w2"][:, bass.ds(e, 1), k, :].rearrange("p a n -> p (a n)"), start=(k == 0), stop=False)
                pe.matmul(p_y[:, 0:D], g["pick_e"][:, bass.ds(e, 1), :].rearrange("p a n -> p (a n)"),
                          g["b2"][:, :], start=False, stop=True).then_inc(py_done, 1)

            rows(0, 0, True)

            def step(j, s, first, last):
                e = pe.value_load(g["expert"][0:1, bass.ds(j, 1)], min_val=0, max_val=E - 1)
                pe.wait_ge(tT_done, j + 1)
                if not (last and s == 1):
                    rows(j + 1, 1 - s, False)
                up(j, s, e, 0, p_g, g_done, glu_done, first)
                if not (first and s == 0):
                    hidden_rows(j - 1, 1 - s, first)
                up(j, s, e, 1, p_l, l_done, lin_done, first)
                if not (first and s == 0):
                    down(j - 1, 1 - s, first)
            paired(pe, MT, step)
            hidden_rows(MT - 1, 1, False)
            down(MT - 1, 1, False)

        @block.scalar
        def _(act):
            def rows(j, s, first):
                act.wait_ge(tp_done, j + 1)
                if not first:
                    act.wait_ge(l_done, j - 1)
                act.copy(tT[:, s, :], p_t[:, 0:D]).then_inc(tT_done, 1)

            def hidden(j, s, first):
                act.wait_ge(hp_done, j + 1)
                act.copy(hT[:, s, :], p_h[:, :]).then_inc(hT_done, 1)

            def result(j, s, first):
                act.wait_ge(py_done, j + 1)
                if not (isinstance(j, int) and j < 2):
                    act.wait_ge(y_out[s], 8 * (j - s))
                act.copy(y[:, s, :], p_y[:, 0:D]).then_inc(y_done, 1)

            rows(0, 0, True)

            def step(j, s, first, last):
                if not (last and s == 1):
                    rows(j + 1, 1 - s, first and s == 0)
                act.wait_ge(glu_done, j + 1)
                if not first:
                    act.wait_ge(hid_done, j - 1)
                act.activation(sig[:, s, :], glu[:, s, :], ACT.Sigmoid, scale=ALPHA).then_inc(sig_done, 1)
                if not (first and s == 0):
                    hidden(j - 1, 1 - s, first)
                    result(j - 1, 1 - s, first)
            paired(act, MT, step, 2)
            hidden(MT - 1, 1, False)
            result(MT - 1, 1, False)

        @block.vector
        def _(dve):
            def step(j, s, first, last):
                dve.wait_ge(g_done, j + 1)
                dve.tensor_scalar(glu[:, s, :], p_g[:, s, :], LIMIT, None, ALU.min).then_inc(glu_done, 1)
                dve.wait_ge(l_done, j + 1)
                dve.tensor_scalar(lin[:, s, :], p_l[:, s, :], LIMIT, -LIMIT, ALU.min, ALU.max).then_inc(lin_done, 1)
                dve.wait_ge(lin_done, j + 1)
                dve.scalar_tensor_tensor(out=lin[:, s, :], in0=lin[:, s, :], scalar=1.0, in1=glu[:, s, :],
                                         op0=ALU.add, op1=ALU.mult).then_inc(prod_done, 1)
                dve.wait_ge(prod_done, j + 1)
                dve.wait_ge(sig_done, j + 1)
                if not first:
                    dve.wait_ge(hp_done, j - 1)
                dve.tensor_tensor(hid[:, s, :], lin[:, s, :], sig[:, s, :], ALU.mult).then_inc(hid_done, 1)
            paired(dve, MT, step)


def combine(nc, mem, g, ys_dram, out=None):
    RING = 4
    got = mem.sb("got", [P, RING, 2, D])
    st6 = mem.sb("st6", [P, 2, 6])
    y_in = [mem.pool_dma_sem(f"y_in{r}") for r in range(RING)]
    half_done, x_done, st_done, stored = (mem.sem(s) for s in ("half_d", "x_d", "st_d", "stored"))

    with nc.Block() as block:
        @block.gpsimd
        def _(pool):
            for i in range(NT):
                if i >= RING:
                    pool.wait_ge(x_done, i - RING + 1)
                for r in range(2):
                    pool.indirect_dma_start(out=got[:, i % RING, r, :], out_offset=None, in_=ys_dram,
                                            in_offset=bass.IndirectOffsetOnAxis(ap=g["slot"][:, r, i:i + 1], axis=0)
                                            ).then_inc(y_in[i % RING], 16)

        @block.vector
        def _(dve):
            for i in range(NT):
                x = g["X"][:, i, :]
                dve.wait_ge(y_in[i % RING], 32 * (i // RING + 1))
                dve.scalar_tensor_tensor(out=x, in0=got[:, i % RING, 0, :], scalar=g["w"][:, 0, i:i + 1], in1=x,
                                         op0=ALU.mult, op1=ALU.add).then_inc(half_done, 1)
                dve.wait_ge(half_done, i + 1)
                dve.scalar_tensor_tensor(out=x, in0=got[:, i % RING, 1, :], scalar=g["w"][:, 1, i:i + 1], in1=x,
                                         op0=ALU.mult, op1=ALU.add).then_inc(x_done, 1)
                if out is None:
                    dve.wait_ge(x_done, i + 1)
                    dve.bn_stats(st6[:, i % 2, :], x).then_inc(st_done, 1)
                    dve.wait_ge(st_done, i + 1)
                    dve.bn_aggr(g["mv"][:, i, :], st6[:, i % 2, :])

        if out is not None:
            @block.sync
            def _(sp):
                for c in range(NT // 4):
                    sp.wait_ge(x_done, 4 * c + 4)
                    sp.dma_start(out[c * 512:(c + 1) * 512, :].rearrange("(t p) d -> p t d", p=P),
                                 g["X"][:, 4 * c:4 * c + 4, :]).then_inc(stored, 16)
                sp.wait_ge(stored, 16 * (NT // 4))


def attend_b(nc, mem, g, spent):
    SCALE = D ** -0.5
    before = list(spent)
    del spent[:]
    Mw = mem.sb("Mw", [P, KD, D])
    Nw = mem.sb("Nw", [P, KD, D])
    bias = mem.sb("bias", [P, D])
    std = mem.sb("std", [P, NT])
    inv = mem.sb("inv", [P, NT])
    n = mem.sb("n", [P, QB, D])
    nT = mem.sb("nT", [P, KD, S])
    gT = mem.sb("gT", [P, KD, S])
    wn = gT[:, 0, 0:3 * D].rearrange("p (m d) -> p m d", m=3), gT[:, 1, 0:3 * D].rearrange("p (m d) -> p m d", m=3)
    wfT = nT
    nsum = mem.sb("nsum", [P, KD])
    nsum_rep = mem.sb("nsum_rep", [P, KD, P])
    vsum = mem.sb("vsum", [P, D])
    small = mem.sb("small", [P, 2, 5])
    p_s = mem.ps("p_s", [P, 2, 2, 512])
    p_w = mem.ps("p_w", [P, 2, 512])
    p_v = mem.ps("p_v", [P, 512])
    IT = 8
    c_in, ww_done, ww_read, std_done, inv_done, n_done, nb_done, all_done = (
        mem.sem(s) for s in ("c_in", "ww_d", "ww_r", "std_d", "inv_d", "n_d", "nb_d", "all_d"))
    w_done = mem.sem("w_d")
    w_read = [mem.sem(f"w_r{s}") for s in range(2)]
    ns_done, rep_done, pv_done, vs_done = (mem.sem(s) for s in ("ns_d", "rep_d", "pv_d", "vs_d"))
    s_done, m_done, nm_done, e_done, r_done, t_done, h_done, st_done = (
        mem.sem(s) for s in ("s_d", "m_d", "nm_d", "e_d", "r_d", "t_d", "h_d", "st_d"))

    def batches(eng, body):
        body(0, True)
        with eng.Fori(1, B, 1) as b:
            body(b, False)

    def target(i):
        return (nT if i < 4 else gT)[:, (i % 4) // 2, i % 2 * 512:(i % 2 + 1) * 512]

    with nc.Block() as block:
        @block.sync
        def _(sp):
            w = g["w_qkv"].rearrange("(m k p) d -> k p m d", m=3, p=P)
            for k in range(KD):
                sp.dma_start(wn[k], w[k]).then_inc(c_in, 16)
                sp.dma_start(wfT[:, k, 0:D], g["w_fcT"][k * P:(k + 1) * P, :]).then_inc(c_in, 16)
            sp.dma_start(bias[:, :], g["b_fc"].partition_broadcast(P)).then_inc(c_in, 16)
            for s in before:
                sp.sem_clear(s)

        @block.gpsimd
        def _(pool):
            pool.wait_ge(c_in, 80)

            def body(b, first):
                pool.wait_ge(n_done, b + 1)
                pool.wait_ge(w_done, IT * b + 4)
                for t in range(QB):
                    last = pool.tensor_tensor(n[:, t, :], n[:, t, :], bias[:, :], ALU.add)
                last.then_inc(nb_done, 1)
            batches(pool, body)

        @block.scalar
        def _(act):
            act.activation(std[:, :], g["mv"][:, :, 1], ACT.Sqrt, bias=g["eps"][:, :]).then_inc(std_done, 1)

            def body(b, first):
                for i in range(0, IT, 2):
                    act.wait_ge(w_done, IT * b + i + 1)
                    act.copy(target(i), p_w[:, 0, :]).then_inc(w_read[0], 1)
                for q in range(QB):
                    s = q % 2
                    if not (first and q < 2):
                        act.wait_ge(t_done, QB * b + q - 1)
                    act.wait_ge(nm_done, QB * b + q + 1)
                    scores = p_s[:, s].rearrange("p a b -> p (a b)")
                    act.activation(scores, scores, ACT.Exp, scale=SCALE, bias=small[:, s, 1:2],
                                   accum_out=small[:, s, 2:3]).then_inc(e_done, 1)
            batches(act, body)

        @block.vector
        def _(dve):
            dve.wait_ge(std_done, 1)
            dve.reciprocal(inv[:, :], std[:, :]).then_inc(inv_done, 1)
            for i, w in enumerate((Mw, Nw)):
                for k in range(KD):
                    dve.wait_ge(ww_done, 2 * i + k + 1)
                    dve.tensor_copy(w[:, k, :], p_w[:, k, 0:D]).then_inc(ww_read, 1)
            dve.wait_ge(inv_done, 1)

            def body(b, first):
                if not first:
                    dve.wait_ge(h_done, QB * b)
                for t in range(QB):
                    j = b * QB + t
                    last = dve.tensor_scalar(n[:, t, :], tile_of(g["X"], j), g["mv"][:, bass.ds(j, 1), 0],
                                             inv[:, bass.ds(j, 1)], ALU.subtract, ALU.mult)
                last.then_inc(n_done, 1)
                for i in range(1, IT, 2):
                    dve.wait_ge(w_done, IT * b + i + 1)
                    dve.tensor_copy(target(i), p_w[:, 1, :]).then_inc(w_read[1], 1)
                dve.wait_ge(w_read[0], IT // 2 * b + 2)
                dve.wait_ge(w_read[1], IT // 2 * b + 2)
                dve.tensor_reduce(nsum[:, :], nT[:, :, :], AX.X, ALU.add).then_inc(ns_done, 1)
                dve.wait_ge(ns_done, b + 1)
                dve.tensor_copy(nsum_rep[:, :, :], nsum[:, :].unsqueeze(2).to_broadcast([P, KD, P])).then_inc(rep_done, 1)

                def maximum(q):
                    s = q % 2
                    dve.wait_ge(s_done, QB * b + q + 1)
                    dve.tensor_reduce(small[:, s, 0:1], p_s[:, s], AX.XY, ALU.max).then_inc(m_done, 1)
                    dve.wait_ge(m_done, QB * b + q + 1)
                    dve.tensor_scalar(small[:, s, 1:2], small[:, s, 0:1], -SCALE, None, ALU.mult).then_inc(nm_done, 1)

                def result(q):
                    s = q % 2
                    j = b * QB + q
                    dve.wait_ge(e_done, j + 1)
                    dve.reciprocal(small[:, s, 3:4], small[:, s, 2:3]).then_inc(r_done, 1)
                    dve.wait_ge(r_done, j + 1)
                    dve.tensor_tensor(small[:, s, 4:5], small[:, s, 2:3], small[:, s, 3:4], ALU.mult).then_inc(t_done, 1)
                    dve.wait_ge(t_done, j + 1)
                    dve.scalar_tensor_tensor(out=tile_of(g["R"], j), in0=vsum[:, :], scalar=small[:, s, 4:5],
                                             in1=n[:, q, :], op0=ALU.mult, op1=ALU.add).then_inc(h_done, 1)

                def statistics(q):
                    dve.bn_stats(tile_of(g["st6"], b * QB + q), tile_of(g["R"], b * QB + q)).then_inc(st_done, 1)

                maximum(0)
                dve.wait_ge(pv_done, b + 1)
                dve.tensor_copy(vsum[:, :], p_v[:, 0:D]).then_inc(vs_done, 1)
                dve.wait_ge(nb_done, b + 1)
                dve.wait_ge(vs_done, b + 1)
                for q in range(1, QB):
                    if q > 1:
                        dve.wait_ge(h_done, QB * b + q - 1)
                    maximum(q)
                    if q > 1:
                        statistics(q - 2)
                    result(q - 1)
                dve.wait_ge(h_done, QB * b + QB - 1)
                result(QB - 1)
                statistics(QB - 2)
            batches(dve, body)
            dve.wait_ge(h_done, NT)
            for b in range(B):
                j = b * QB + QB - 1
                last = dve.bn_stats(g["st6"][:, j, :], g["R"][:, j, :])
            last.then_inc(all_done, 1)
            dve.wait_ge(all_done, 1)
            dve.wait_ge(st_done, (QB - 1) * B)
            for j in range(NT):
                dve.bn_aggr(g["mv2"][:, j, :], g["st6"][:, j, :])

        @block.tensor
        def _(pe):
            pe.wait_ge(c_in, 80)
            for i in range(2):
                if i:
                    pe.wait_ge(ww_read, 2)
                for k in range(KD):
                    for e in range(KD):
                        lhs = wn[e][:, 2 * i, k * P:(k + 1) * P]
                        rhs = wn[e][:, 1, :] if i == 0 else wfT[:, e, 0:D]
                        mm = pe.matmul(p_w[:, k, 0:D], lhs, rhs, start=(e == 0), stop=(e == KD - 1))
                    mm.then_inc(ww_done, 1)
            pe.wait_ge(ww_read, 4)

            def body(b, first):
                def free(i):
                    if not (first and i < 2):
                        pe.wait_ge(w_read[i % 2], IT // 2 * b + i // 2)

                pe.wait_ge(n_done, b + 1)
                for i in range(4):
                    free(i)
                    k, half = i // 2, i % 2
                    for t in range(4):
                        mm = pe.transpose(p_w[:, i % 2, t * P:(t + 1) * P], n[:, 4 * half + t, k * P:(k + 1) * P],
                                          g["ident"][:, :])
                    mm.then_inc(w_done, 1)
                for i in range(4, IT):
                    free(i)
                    ko, half = (i - 4) // 2, i % 2
                    for k in range(KD):
                        mm = pe.matmul(p_w[:, i % 2, :], Mw[:, k, ko * P:(ko + 1) * P], nT[:, k, half * 512:(half + 1) * 512],
                                       start=(k == 0), stop=(k == KD - 1))
                    mm.then_inc(w_done, 1)
                for s in range(2):
                    pe.wait_ge(w_read[s], IT // 2 * (b + 1))
                for q in range(QB):
                    if not (first and q < 2):
                        pe.wait_ge(e_done, QB * b + q - 1)
                    for half in range(2):
                        for k in range(KD):
                            mm = pe.matmul(p_s[:, q % 2, half, :], gT[:, k, q * P:(q + 1) * P],
                                           nT[:, k, half * 512:(half + 1) * 512], start=(k == 0), stop=(k == KD - 1))
                    mm.then_inc(s_done, 1)
                    if q == 0:
                        pe.wait_ge(rep_done, b + 1)
                        if not first:
                            pe.wait_ge(vs_done, b)
                        for k in range(KD):
                            mm = pe.matmul(p_v[:, 0:D], nsum_rep[:, k, :], Nw[:, k, :], start=(k == 0), stop=(k == KD - 1))
                        mm.then_inc(pv_done, 1)
            batches(pe, body)


def add_b(nc, mem, g):
    a = mem.sb("a", [P, 2, D])
    std = mem.sb("std", [P, NT])
    inv = mem.sb("inv", [P, NT])
    gam = mem.sb("gam", [P, D])
    bet = mem.sb("bet", [P, D])
    c_in, std_done, inv_done, a_done, shifted, x_done, st_done = (
        mem.sem(s) for s in ("c_in", "std_d", "inv_d", "a_d", "shifted", "x_d", "st_d"))

    with nc.Block() as block:
        @block.sync
        def _(sp):
            sp.dma_start(gam[:, :], g["gamma"].partition_broadcast(P)).then_inc(c_in, 16)
            sp.dma_start(bet[:, :], g["beta"].partition_broadcast(P)).then_inc(c_in, 16)

        @block.scalar
        def _(act):
            act.activation(std[:, :], g["mv2"][:, :, 1], ACT.Sqrt, bias=g["eps"][:, :]).then_inc(std_done, 1)

        @block.gpsimd
        def _(pool):
            pool.wait_ge(c_in, 32)

            def step(j, s, first, last):
                x = tile_of(g["X"], j)
                pool.tensor_tensor(x, x, bet[:, :], ALU.add).then_inc(shifted, 1)
            paired(pool, NT, step)

        @block.vector
        def _(dve):
            dve.wait_ge(std_done, 1)
            dve.reciprocal(inv[:, :], std[:, :]).then_inc(inv_done, 1)
            dve.wait_ge(inv_done, 1)
            dve.wait_ge(c_in, 32)

            def finish(j, s):
                x = tile_of(g["X"], j)
                dve.wait_ge(a_done, j + 1)
                dve.wait_ge(shifted, j + 1)
                dve.scalar_tensor_tensor(out=x, in0=a[:, s, :], scalar=inv[:, bass.ds(j, 1)], in1=x,
                                         op0=ALU.mult, op1=ALU.add).then_inc(x_done, 1)

            def step(j, s, first, last):
                if not first:
                    dve.wait_ge(x_done, j - 1)
                dve.scalar_tensor_tensor(out=a[:, s, :], in0=tile_of(g["R"], j), scalar=g["mv2"][:, bass.ds(j, 1), 0],
                                         in1=gam[:, :], op0=ALU.subtract, op1=ALU.mult).then_inc(a_done, 1)
                if not first:
                    dve.bn_stats(tile_of(g["st6"], j - 2), tile_of(g["X"], j - 2))
                if not (first and s == 0):
                    finish(j - 1, 1 - s)
            paired(dve, NT, step)
            finish(NT - 1, 1)
            dve.wait_ge(x_done, NT)
            for j in range(NT - 2, NT):
                last = dve.bn_stats(g["st6"][:, j, :], g["X"][:, j, :])
            last.then_inc(st_done, 1)
            dve.wait_ge(st_done, 1)
            for j in range(NT):
                dve.bn_aggr(g["mv"][:, j, :], g["st6"][:, j, :])


def constants(nc, mem, g):
    g["ident"] = mem.sb("ident", [P, P])
    g["identb"] = mem.sb("identb", [P, P], BF16)
    g["maskb"] = mem.sb("maskb", [P, P], BF16)
    g["before"] = mem.sb("before", [P, P], BF16)
    g["onesb"] = mem.sb("onesb", [P, P], BF16)
    g["ones"] = mem.sb("ones", [P, E * NT])
    g["eps"] = mem.sb("eps", [P, 1])
    g["rev"] = mem.sb("rev", [P, E])
    g["tile_starts"] = mem.sb("tile_starts", [P, NT])
    g["tile_no"] = mem.sb("tile_no", [P, MT])
    set_done, = (mem.sem(s) for s in ("set_d",))
    g["zeroed"] = mem.sem("zeroed")
    zeros = g["R"]
    with nc.Block() as block:
        @block.gpsimd
        def _(pool):
            pool.memset(zeros[:, 0:8, :], 0.0).then_inc(set_done, 1)
            for name, value in (("ident", 0.0), ("identb", 0.0), ("maskb", 0.0), ("before", 1.0), ("onesb", 1.0),
                                ("ones", 1.0), ("eps", EPS)):
                pool.memset(g[name][:, :], value).then_inc(set_done, 1)
            pool.wait_ge(set_done, 8)
            for name in ("ident", "identb"):
                pool.affine_select(out=g[name][:, :], in_=g[name][:, :], compare_op=ALU.not_equal, fill=1.0, base=0,
                                   pattern=[[-1, P]], channel_multiplier=1)
            pool.affine_select(out=g["maskb"][:, :], in_=g["maskb"][:, :], compare_op=ALU.is_ge, fill=NEG, base=0,
                               pattern=[[-1, P]], channel_multiplier=1)
            pool.affine_select(out=g["before"][:, :], in_=g["before"][:, :], compare_op=ALU.is_gt, fill=0.0, base=0,
                               pattern=[[1, P]], channel_multiplier=-1)
            for name, base, step, count in (("rev", E, -1, E), ("tile_starts", 0, P, NT), ("tile_no", 0, 1, MT)):
                pool.iota(g[name][:, :], pattern=[[step, count]], base=base, channel_multiplier=0,
                          allow_small_or_imprecise_dtypes=True)


def program(nc, a, out, stop=99):
    g = dict(a)
    qk_dram = nc.dram_tensor("qk_parts", [2, U, 3 * DK, HG, S], BF16).ap()
    v_dram = nc.dram_tensor("v_padded", [U, S, HG * PAD], F32).ap()
    o_dram = nc.dram_tensor("o_rows", [U, P, S], F32).ap()
    xs_dram = nc.dram_tensor("slot_rows", [SLOTS, D], F32).ap()
    ys_dram = nc.dram_tensor("slot_results", [SLOTS, D], F32).ap()
    with ExitStack() as whole:
        keep = Mem(nc, whole)
        g["X"] = keep.sb("X", [P, NT, D])
        g["R"] = keep.sb("R", [P, NT, D])
        g["st6"] = keep.sb("st6", [P, NT, 6])
        g["mv"] = keep.sb("mv_all", [P, NT, 2])
        g["mv2"] = keep.sb("mv2_all", [P, NT, 2])
        g["w"] = keep.sb("w", [P, 2, NT])
        g["slot"] = keep.sb("slot", [P, 2, NT], I32)
        g["expert"] = keep.sb("expert", [P, MT], I32)
        g["b1"] = keep.sb("b1", [P, 2 * I], BF16)
        g["b2"] = keep.sb("b2", [P, D], BF16)
        g["pick_e"] = keep.sb("pick_e", [P, E, P], BF16)
        g["w_in"] = keep.sem("w_in")
        constants(nc, keep, g)

        spent = []

        def phase(f, tag, *args, **kw):
            with ExitStack() as own:
                f(nc, Mem(nc, own, tag, spent, whole), g, *args, **kw)

        phase(project_qkv, "a1_", a["x"], qk_dram, v_dram)
        phase(attend_a, "a2_", qk_dram, v_dram, o_dram, xs_dram)
        g["w1"] = keep.sb("w1", [P, E, KD, 2 * I])
        g["w2"] = keep.sb("w2", [P, E, KI, D])
        phase(project_out, "a3_", o_dram)
        if stop == 1:
            return save(nc, keep, g, out)
        phase(route, "r1_", xs_dram)
        phase(experts, "e1_", xs_dram, ys_dram)
        if stop == 2:
            return phase(combine, "c1_", ys_dram, out=out)
        phase(combine, "c1_", ys_dram)
        phase(attend_b, "b_", spent)
        phase(add_b, "ab_")
        if stop == 3:
            return save(nc, keep, g, out)
        phase(route, "r2_", xs_dram)
        phase(experts, "e2_", xs_dram, ys_dram)
        phase(combine, "c2_", ys_dram, out=out)


def save(nc, mem, g, out):
    stored = mem.sem("dbg_stored")
    with nc.Block() as block:
        @block.sync
        def _(sp):
            sp.dma_start(out.rearrange("(t p) d -> p t d", p=P), g["X"][:, :, :]).then_inc(stored, 16)
            sp.wait_ge(stored, 16)


def laid_out(inputs):
    import numpy as np
    v = {k.split("_", 1)[1]: np.asarray(a) for k, a in inputs.items()}
    c = np.ascontiguousarray

    def by_dim(w):
        return c(w.reshape(D, D // (HG * DK), HG, DK).transpose(0, 1, 3, 2).reshape(D, D))
    m1 = v["ffn_mlp1_w"]
    b1 = v["ffn_mlp1_b"]
    return {
        "x": v["attn_a_x"].reshape(T, D),
        "WqT": by_dim(v["attn_a_Wq"].T), "WkT": by_dim(v["attn_a_Wk"].T), "WvT": c(v["attn_a_Wv"].T), "WoT": c(v["attn_a_Wo"].T),
        "w_qkv": c(v["attn_b_w_qkv"]), "w_fcT": c(v["attn_b_w_fc"].T),
        "b_fc": v["attn_b_b_fc"], "gamma": v["attn_b_gamma"], "beta": v["attn_b_beta"],
        "scale": v["ffn_norm_scale"], "gate_w": v["ffn_gate_w"], "gate_b": v["ffn_gate_b"],
        "mlp1": c(m1.reshape(E, D, I, 2).transpose(0, 1, 3, 2).reshape(E, D, 2 * I)),
        "mlp1_b": c(b1.reshape(E, I, 2).transpose(0, 2, 1).reshape(E, 2 * I)),
        "mlp2": c(v["ffn_mlp2_w"]), "mlp2_b": v["ffn_mlp2_b"],
    }


def kernel(**inputs):
    import concourse.bacc as bacc
    from concourse.bass_utils import run_bass_kernel_spmd

    nc = bacc.Bacc("TRN2", target_bir_lowering=False, num_devices=1)
    arrays = laid_out(inputs)
    aps = {k: nc.dram_tensor(f"in_{k}", a.shape, mybir.dt.from_np(a.dtype), kind="ExternalInput").ap()
           for k, a in arrays.items()}
    out = nc.dram_tensor("out", (T, D), F32, kind="ExternalOutput").ap()
    program(nc, aps, out)
    r = run_bass_kernel_spmd(nc, [{f"in_{k}": a for k, a in arrays.items()}], core_ids=[0])
    return r.results[0]["out"].reshape(B, S, D)
```

```python
from contextlib import ExitStack

import concourse.bass as bass
from concourse import mybir

F32 = mybir.dt.float32
BF16 = mybir.dt.bfloat16
I32 = mybir.dt.int32
ALU = mybir.AluOpType
ACT = mybir.ActivationFunctionType
AX = mybir.AxisListType

P = 128
B, S, D = 4, 1024, 256
T = B * S
NT = T // P
KD = D // P
EPS = 1e-5

H, DK = 16, 16
HG = 4
U = B * H // HG
QB = S // P
PAD = 32
ROUND = 1.5 * 2 ** 23
NEG = -1e30
Q_PART = (0, 0, 0, 1, 1, 2)
K_PART = (0, 1, 2, 0, 1, 0)
Q_RUNS = ((0, 0, 3), (3, 1, 2), (5, 2, 1))
ROWS = len(Q_PART) * DK
MROWS = 3

E, I = 8, 512
KI = I // P
LIMIT, ALPHA = 7.0, 1.702
MT = 2 * T // P + E
SLOTS = MT * P


def paired(eng, count, body, lead=1):
    pairs = count // 2
    for i in range(lead):
        for s in range(2):
            body(2 * i + s, s, i == 0, i == pairs - 1)
    if pairs > lead + 1:
        with eng.Fori(lead, pairs - 1, 1) as i:
            for s in range(2):
                body(2 * i + s, s, False, False)
    for s in range(2):
        body(count - 2 + s, s, False, True)


def rotating(eng, body):
    for u in range(2):
        body(u, u % 3)
    with eng.Fori(0, (U - 4) // 3, 1) as i:
        for s in range(3):
            body(3 * i + (2 + s), (2 + s) % 3)
    for u in range(U - 2, U):
        body(u, u % 3)


class Mem:

    def __init__(self, nc, ctx, tag="", spent=None, whole=None):
        self.nc, self.ctx, self.tag, self.spent, self.whole = nc, ctx, tag, spent, whole

    def sb(self, name, shape, dt=F32):
        return self.ctx.enter_context(self.nc.sbuf_tensor(self.tag + name, shape, dt))

    def ps(self, name, shape, dt=F32):
        return self.ctx.enter_context(self.nc.psum_tensor(self.tag + name, shape, dt))

    def sem(self, name):
        s = self.ctx.enter_context(self.nc.semaphore(self.tag + name))
        if self.spent is not None:
            assert s.num not in [t.num for t in self.spent], "a spent semaphore is used again"
            self.spent.append(s)
        return s

    def pool_dma_sem(self, name):
        return self.whole.enter_context(self.nc.semaphore(self.tag + name))


def project_qkv(nc, mem, g, x_dram, qk_dram, v_dram):
    CH = T // 512
    n = mem.sb("n", [P, 2, 4, D])
    nT = mem.sb("nT", [P, 2, KD, 512])
    stats = mem.sb("stats", [P, 4, 6])
    mv = mem.sb("mv", [P, 2, 4, 2])
    std = mem.sb("std", [P, 2, 4])
    rstd = mem.sb("rstd", [P, 2, 4])
    part = mem.sb("part", [P, 2, 3, 512], BF16)
    rest = mem.sb("rest", [P, 2, 512])
    vpad = mem.sb("vpad", [P, 2, 4, H, PAD])
    w3 = mem.sb("wqkv", [P, 3, KD, D])
    p_t = mem.ps("p_t", [P, KD, 512])
    p_qk = mem.ps("p_qk", [P, 2, 512])
    p_v = mem.ps("p_v", [P, 2, 2, D])

    w_in = mem.sem("w_in")
    x_in = [mem.sem(f"x_in{s}") for s in range(2)]
    stats_done, mv_done, std_done, rstd_done = (mem.sem(s) for s in ("stats_d", "mv_d", "std_d", "rstd_d"))
    n_done, t_done, nT0_done, nT1_done = (mem.sem(s) for s in ("n_d", "t_d", "nT0_d", "nT1_d"))
    qk_done, hi_done, rest_done, mid_done, lo_done = (mem.sem(s) for s in ("qk_d", "hi_d", "rest_d", "mid_d", "lo_d"))
    v0_done, v1_done, v0_copied, v1_copied = (mem.sem(s) for s in ("v0_d", "v1_d", "v0_c", "v1_c"))
    pad_done = mem.sem("pad_d")
    part_out = [mem.sem(f"part_out{s}") for s in range(2)]
    v_out = [mem.sem(f"v_out{s}") for s in range(2)]

    with nc.Block() as block:
        @block.sync
        def _(sp):
            def load(c, s):
                sp.dma_start(g["X"][:, bass.ds(c * 4, 4), :],
                             x_dram[bass.ds(c * 512, 512), :].rearrange("(t p) d -> p t d", p=P)
                             ).then_inc(x_in[s], 16)

            def step(c, s, first, last):
                if not last:
                    sp.wait_ge(x_in[s], 8 * (c - s) + 16)
                    load(c + 2, s)
                store(c, s)

            def store(c, s):
                for m in range(4):
                    slot = m % 2
                    sp.wait_ge(lo_done, 4 * c + m + 1)
                    sp.nop(nofuse=True)
                    for u in range(2):
                        rows = slice(u * HG * DK, (u + 1) * HG * DK)
                        dst = qk_dram[m // 2, bass.ds(2 * (c - s) + 2 * (m % 2) + u, 1), :, :, s * 512:(s + 1) * 512]
                        sp.dma_start(dst.rearrange("u (r d) h t -> (u d h) r t", d=DK), part[rows, slot]
                                     ).then_inc(part_out[slot], 16)
                sp.wait_ge(v0_copied, c + 1)
                sp.nop(nofuse=True)
                sp.wait_ge(v1_copied, c + 1)
                sp.nop(nofuse=True)
                for hg in range(HG):
                    sp.dma_start(v_dram[bass.ds(2 * (c - s) + hg, 1), s * 512:(s + 1) * 512, :]
                                 .rearrange("u (t p) d -> p (u t) d", p=P),
                                 vpad[:, s, :, hg * 4:hg * 4 + 4, :].rearrange("p t h d -> p t (h d)")
                                 ).then_inc(v_out[s], 16)
            load(0, 0)
            for m, w in enumerate((g["WqT"], g["WkT"], g["WvT"])):
                sp.dma_start(w3[:, m], w.rearrange("(k p) n -> p k n", p=P)).then_inc(w_in, 16)
            load(1, 1)
            paired(sp, CH, step)
            for s in range(2):
                sp.wait_ge(part_out[s], 32 * 2 * CH)
                sp.wait_ge(v_out[s], 64 * CH // 2)

        @block.gpsimd
        def _(pool):
            pool.memset(vpad[:, :, :, :, DK:PAD], 0.0).then_inc(pad_done, 1)
            pool.wait_ge(pad_done, 1)
            pool.memset(vpad[:, :, :, :, DK:DK + 1], 1.0).then_inc(pad_done, 1)

            def step(c, s, first, last):
                for m in range(4):
                    slot = m % 2
                    pool.wait_ge(mid_done, 4 * c + m + 1)
                    pool.tensor_tensor(part[:, slot, 2], rest[:, slot], part[:, slot, 1],
                                       ALU.subtract).then_inc(lo_done, 1)
            paired(pool, CH, step)

        @block.scalar
        def _(act):
            def root(c, s):
                act.wait_ge(mv_done, c + 1)
                act.activation(std[:, s, :], mv[:, s, :, 1], ACT.Sqrt, bias=g["eps"][:, :]).then_inc(std_done, 1)

            root(0, 0)

            def step(c, s, first, last):
                act.wait_ge(t_done, c + 1)
                act.copy(nT[:, s, 1, :], p_t[:, 1, :]).then_inc(nT1_done, 1)
                for m in range(4):
                    slot = m % 2
                    act.wait_ge(qk_done, 4 * c + m + 1)
                    if not (first and s == 0 and m < 2):
                        act.wait_ge(part_out[slot], 64 * c + 32 * (m // 2))
                    act.copy(part[:, slot, 0], p_qk[:, slot, :]).then_inc(hi_done, 1)
                    act.wait_ge(rest_done, 4 * c + m + 1)
                    act.copy(part[:, slot, 1], rest[:, slot]).then_inc(mid_done, 1)
                    if m == 0 and not (last and s == 1):
                        root(c + 1, 1 - s)
                act.wait_ge(v0_done, c + 1)
                act.wait_ge(pad_done, 2)
                if not first:
                    act.wait_ge(v_out[s], 32 * (c - s))
                act.copy(vpad[:, s, 0:2, :, 0:DK], p_v[:, 0].rearrange("p t (h d) -> p t h d", h=H)
                         ).then_inc(v0_copied, 1)
            paired(act, CH, step)

        @block.vector
        def _(dve):
            def statistics(c, s):
                for t in range(4):
                    last = dve.bn_stats(stats[:, t, :], tile_of(g["X"], c * 4 + t))
                last.then_inc(stats_done, 1)

            def moments(c, s):
                for t in range(4):
                    last = dve.bn_aggr(mv[:, s, t, :], stats[:, t, :])
                last.then_inc(mv_done, 1)

            def inverse(c, s):
                dve.wait_ge(std_done, c + 1)
                dve.reciprocal(rstd[:, s, :], std[:, s, :]).then_inc(rstd_done, 1)

            def normalise(c, s):
                dve.wait_ge(rstd_done, c + 1)
                for t in range(4):
                    last = dve.tensor_scalar(n[:, s, t, :], tile_of(g["X"], c * 4 + t), mv[:, s, t, 0:1],
                                             rstd[:, s, t:t + 1], ALU.subtract, ALU.mult)
                last.then_inc(n_done, 1)

            dve.wait_ge(x_in[0], 16)
            statistics(0, 0)
            dve.wait_ge(stats_done, 1)
            moments(0, 0)
            inverse(0, 0)
            normalise(0, 0)

            def step(c, s, first, last):
                more = not (last and s == 1)
                if more:
                    dve.wait_ge(x_in[1 - s], 8 * (c + 1 - (1 - s)) + 16)
                dve.wait_ge(t_done, c + 1)
                dve.tensor_copy(nT[:, s, 0, :], p_t[:, 0, :]).then_inc(nT0_done, 1)
                if more:
                    statistics(c + 1, 1 - s)
                for m in range(4):
                    slot = m % 2
                    if more and m == 0:
                        dve.wait_ge(stats_done, c + 2)
                    if not (first and s == 0 and m < 2):
                        dve.wait_ge(lo_done, 4 * c + m - 1)
                    dve.wait_ge(hi_done, 4 * c + m + 1)
                    dve.tensor_tensor(rest[:, slot], p_qk[:, slot, :], part[:, slot, 0],
                                      ALU.subtract).then_inc(rest_done, 1)
                    if more:
                        if m == 0:
                            moments(c + 1, 1 - s)
                        if m == 1:
                            inverse(c + 1, 1 - s)
                        if m == 2:
                            normalise(c + 1, 1 - s)
                dve.wait_ge(v1_done, c + 1)
                dve.wait_ge(pad_done, 2)
                if not first:
                    dve.wait_ge(v_out[s], 32 * (c - s))
                dve.tensor_copy(vpad[:, s, 2:4, :, 0:DK], p_v[:, 1].rearrange("p t (h d) -> p t h d", h=H)
                                ).then_inc(v1_copied, 1)
            paired(dve, CH, step)

        @block.tensor
        def _(pe):
            pe.wait_ge(w_in, 48)

            def step(c, s, first, last):
                pe.wait_ge(n_done, c + 1)
                if not (first and s == 0):
                    pe.wait_ge(nT0_done, c)
                    pe.wait_ge(nT1_done, c)
                for k in range(KD):
                    for t in range(4):
                        mm = pe.transpose(p_t[:, k, t * P:(t + 1) * P], n[:, s, t, k * P:(k + 1) * P], g["ident"][:, :])
                mm.then_inc(t_done, 1)
                pe.wait_ge(nT0_done, c + 1)
                pe.wait_ge(nT1_done, c + 1)
                for m in range(4):
                    if not (first and s == 0 and m < 2):
                        pe.wait_ge(rest_done, 4 * c + m - 1)
                    for k in range(KD):
                        mm = pe.matmul(p_qk[:, m % 2, :], w3[:, m // 2, k, (m % 2) * P:(m % 2 + 1) * P],
                                       nT[:, s, k, :], start=(k == 0), stop=(k == KD - 1))
                    mm.then_inc(qk_done, 1)
                for half, (copied, done) in enumerate(((v0_copied, v0_done), (v1_copied, v1_done))):
                    if not (first and s == 0):
                        pe.wait_ge(copied, c)
                    for t in range(2):
                        for k in range(KD):
                            mm = pe.matmul(p_v[:, half, t, :], nT[:, s, k, (2 * half + t) * P:(2 * half + t + 1) * P],
                                           w3[:, 2, k, :], start=(k == 0), stop=(k == KD - 1))
                    mm.then_inc(done, 1)
            paired(pe, CH, step)


MT_ITEM = 2


def sn_items():
    items = []
    for pair in range(HG // 2):
        hs = (2 * pair, 2 * pair + 1)
        for qb in range(2):
            w = (qb + 1) * P
            items.append(([(h, qb, 0, w, j * w) for j, h in enumerate(hs)], hs, w, qb))
        for qb in range(2, QB):
            for h in hs:
                w = min((qb + 1) * P, 512)
                items.append(([(h, qb, 0, w, 0)], (h,), w, qb))
        for qb in range(4, QB):
            w = (qb - 3) * P
            if w <= 2 * P:
                items.append(([(h, qb, 512, w, j * w) for j, h in enumerate(hs)], hs, w, qb + 4))
            else:
                for h in hs:
                    items.append(([(h, qb, 512, w, 0)], (h,), w, qb + 4))
    narrow = next(i for i, it in enumerate(items) if i > 2 and len(it[0]) * it[2] <= 2 * P)
    items.insert(MT_ITEM, items.pop(narrow))
    return items


def expert_biases(mem, g):
    raw = mem.sb("raw", [P, D])
    hi = mem.sb("hi", [P, D], BF16)
    mid = mem.sb("mid", [P, D], BF16)
    part = mem.sb("part", [P, 3])
    zero, b_in, sel, chain = (mem.sem(s) for s in ("zero", "b_in", "sel", "chain"))

    def clear(dve):
        dve.memset(raw[:, :], 0.0).then_inc(zero, 1)

    def load_biases(act):
        act.wait_ge(zero, 1)
        for m in range(3):
            act.dma_start(raw[m * E:(m + 1) * E, :], g["mlp2_b"]).then_inc(b_in, 16)

    def select_experts(pool):
        pool.memset(part[:, :], 1.0).then_inc(sel, 1)
        pool.memset(g["pick_e"][:, :, :], 0.0).then_inc(sel, 1)
        pool.wait_ge(sel, 2)
        pool.affine_select(out=part[:, :], in_=part[:, :], compare_op=ALU.is_ge, fill=0.0, base=0,
                           pattern=[[-E, 3]], channel_multiplier=1).then_inc(sel, 1)
        pool.wait_ge(sel, 3)
        pool.affine_select(out=part[:, :], in_=part[:, :], compare_op=ALU.is_ge, fill=0.0, base=E - 1,
                           pattern=[[E, 3]], channel_multiplier=-1).then_inc(sel, 1)
        for m in range(3):
            pool.affine_select(out=g["pick_e"][:, :, :], in_=g["pick_e"][:, :, :], compare_op=ALU.not_equal,
                               fill=1.0, base=-m * E, pattern=[[-1, E], [0, P]], channel_multiplier=1
                               ).then_inc(sel, 1)
            pool.wait_ge(sel, 5 + m)

    def split(dve):
        count = [0]

        def link(ins):
            count[0] += 1
            ins.then_inc(chain, 1)
            dve.wait_ge(chain, count[0])

        dve.wait_ge(b_in, 48)
        dve.wait_ge(sel, 4)
        link(dve.tensor_copy(hi[:, :], raw[:, :]))
        link(dve.tensor_tensor(raw[:, :], raw[:, :], hi[:, :], ALU.subtract))
        link(dve.tensor_copy(mid[:, :], raw[:, :]))
        link(dve.tensor_tensor(raw[:, :], raw[:, :], mid[:, :], ALU.subtract))
        link(dve.tensor_scalar(raw[:, :], raw[:, :], part[:, 2:3], None, ALU.mult))
        link(dve.scalar_tensor_tensor(out=raw[:, :], in0=mid[:, :], scalar=part[:, 1:2], in1=raw[:, :],
                                      op0=ALU.mult, op1=ALU.add))
        link(dve.scalar_tensor_tensor(out=raw[:, :], in0=hi[:, :], scalar=part[:, 0:1], in1=raw[:, :],
                                      op0=ALU.mult, op1=ALU.add))
        link(dve.tensor_copy(g["b2"][:, :], raw[:, :]))

    return clear, load_biases, select_experts, split


def attend_a(nc, mem, g, qk_dram, v_dram, o_dram):
    items = sn_items()
    NI = len(items)
    AHEAD = 10
    steps = [(kb, h) for kb in range(4) for h in range(HG)] + [(kb, h) for kb in range(4, QB) for h in (0, 2)]
    NS = len(steps)
    ends = [max(i for i, st in enumerate(steps) if st[0] == kb) + 1 for kb in range(QB)]
    LOADS = 16 * 2 * len(Q_RUNS)

    Kst = mem.sb("Kst", [P, 3, HG, S], BF16)
    Qst = mem.sb("Qst", [P, 3, HG, S], BF16)
    Vst = mem.sb("Vst", [P, 3, QB, P])
    Pt = mem.sb("Pt", [P, 2, HG, S])
    OT = mem.sb("OT", [P, 2, 512])
    mx = mem.sb("mx", [P, HG, 12])
    mrest = mem.sb("mrest", [P, HG, QB])
    mpart = mem.sb("mpart", [P, MROWS, HG, QB], BF16)
    mT = mem.sb("mT", [MROWS * HG * QB, P], BF16)
    p_st = mem.ps("p_st", [P, 2, 2, 512])
    p_sn = mem.ps("p_sn", [P, 2, 512])
    p_o = mem.ps("p_o", [P, 2, 512])
    p_mT = p_sn[0:MROWS * HG * QB, MT_ITEM % 2, :].bitcast(BF16)[:, 4 * P:5 * P]

    kq_in, v_in, m_in, ones_done = (mem.sem(s) for s in ("kq_in", "v_in", "m_in", "ones_d"))
    sn_done, sn_read, mx_step, mp_done = (mem.sem(s) for s in ("sn_d", "sn_r", "mx_step", "mp_d"))
    mr_done, mT_done = (mem.sem(s) for s in ("mr_d", "mT_d"))
    st_done, exp_done, mask_done, pv_done = (mem.sem(s) for s in ("st_d", "exp_d", "mask_d", "pv_d"))
    o_copied = [mem.sem(f"o_c{c}") for c in range(2)]
    o_out = [mem.sem(f"o_out{c}") for c in range(2)]

    clear, load_biases, select_experts, split = expert_biases(mem, g)

    def is_first(u):
        return isinstance(u, int) and u == 0

    def weights(kb, h, q0, q1):
        shift = 512 if kb >= 6 else 0
        return Pt[:, kb % 2, h, q0 - shift:q1 - shift]

    with nc.Block() as block:
        @block.sync
        def _(sp):
            def load(u, s):
                for c, r, n in Q_RUNS:
                    k_part = qk_dram[1, bass.ds(u, 1), 0:n * DK, :, :].rearrange("u p h t -> p (u h t)")
                    q_part = qk_dram[0, bass.ds(u, 1), r * DK:(r + 1) * DK, :, :].rearrange("u d h t -> u d (h t)")
                    sp.dma_start(Kst[c * DK:(c + n) * DK, s, :, :].rearrange("p h t -> p (h t)"), k_part
                                 ).then_inc(kq_in, 16)
                    sp.dma_start(Qst[c * DK:(c + n) * DK, s, :, :].rearrange("p h t -> p (h t)"),
                                 q_part.broadcast_to([n, DK, HG * S])).then_inc(kq_in, 16)

            def load_v(u, s):
                sp.dma_start(Vst[:, s], v_dram[bass.ds(u, 1), :, :].rearrange("u (k p) d -> p (u k) d", p=P)
                             ).then_inc(v_in, 16)

            def max_rows(u, s):
                sp.wait_ge(mT_done, u + 1)
                for r in range(MROWS):
                    sp.dma_start(Qst[ROWS + r:ROWS + r + 1, s, :, :].rearrange("p h (q t) -> p (h q) t", t=P),
                                 mT[r * HG * QB:(r + 1) * HG * QB, :]).then_inc(m_in, 16)

            load(0, 0)
            sp.wait_ge(kq_in, LOADS)
            load(1, 1)
            load_v(0, 0)
            max_rows(0, 0)
            sp.wait_ge(v_in, 16)
            load_v(1, 1)

            def step(u, s):
                if not (isinstance(u, int) and u >= U - 2):
                    if is_first(u):
                        sp.wait_ge(kq_in, LOADS * 2)
                    else:
                        sp.wait_ge(st_done, NS * u)
                    sp.nop(nofuse=True)
                    load(u + 2, (s + 2) % 3)
                    if not is_first(u):
                        sp.wait_ge(pv_done, QB * u)
                    sp.nop(nofuse=True)
                    sp.wait_ge(v_in, 16 * (u + 2))
                    sp.nop(nofuse=True)
                    load_v(u + 2, (s + 2) % 3)
                if not (isinstance(u, int) and u == U - 1):
                    max_rows(u + 1, (s + 1) % 3)
            rotating(sp, step)

        @block.gpsimd
        def _(pool):
            select_experts(pool)
            pool.memset(Kst[ROWS:P, :, :, :], 1.0).then_inc(ones_done, 1)
            pool.wait_ge(ones_done, 1)

            def step(u, s, first, last):
                for kb in range(QB):
                    pool.wait_ge(exp_done, NS * u + ends[kb])
                    diag = weights(kb, slice(0, HG), kb * P, (kb + 1) * P)
                    pool.nop(nofuse=True)
                    pool.affine_select(out=diag, in_=diag, compare_op=ALU.is_ge, fill=0.0, base=0,
                                       pattern=[[0, HG], [1, P]], channel_multiplier=-1).then_inc(mask_done, 1)
            paired(pool, U, step)

        @block.scalar
        def _(act):
            load_biases(act)

            def copy_out(u, c):
                act.wait_ge(pv_done, QB * u + (4 if c == 0 else QB))
                if not (isinstance(u, int) and u == 0):
                    act.wait_ge(o_out[c], 16 * u)
                act.copy(OT[:, c, :], p_o[:, c, :]).then_inc(o_copied[c], 1)

            def store(u, c):
                act.wait_ge(o_copied[c], u + 1)
                act.dma_start(o_dram[bass.ds(u, 1), :, c * 512:(c + 1) * 512].rearrange("u p t -> (u p) t"),
                              OT[:, c, :]).then_inc(o_out[c], 16)

            def step(u, s, first, last):
                for i, (kb, h) in enumerate(steps):
                    act.wait_ge(st_done, NS * u + i + 1)
                    if not (first and s == 0 and kb < 2):
                        used = kb - 1 if kb < 6 else kb - 3
                        act.wait_ge(pv_done, QB * u + used)
                    ring = p_st[:, i % 2]
                    if kb < 4:
                        out = weights(kb, h, kb * P, S)
                        inp = ring.rearrange("p a b -> p (a b)")[:, kb * P:S]
                    else:
                        out = weights(kb, slice(h, h + 2), kb * P, S)
                        inp = ring[:, :, kb * P - 512:512]
                    act.activation(out, inp, ACT.Exp, scale=DK ** -0.5).then_inc(exp_done, 1)
                    if i == 6 and not (first and s == 0):
                        copy_out(u - 1, 1)
                    if i == 7 and not (first and s == 0):
                        store(u - 1, 1)
                    if i == ends[4]:
                        copy_out(u, 0)
                    if i == ends[4] + 1:
                        store(u, 0)
            paired(act, U, step)
            copy_out(U - 1, 1)
            store(U - 1, 1)
            for c in range(2):
                act.wait_ge(o_out[c], 16 * U)

        @block.vector
        def _(dve):
            def maxima_row(u):
                dve.wait_ge(mr_done, u + 1)
                dve.tensor_copy(mT[:, :], p_mT).then_inc(mT_done, 1)

            def maxima(u, s):
                for k, (_, hs, w, place) in enumerate(items):
                    dve.wait_ge(sn_done, NI * u + k + 1)
                    dve.tensor_reduce(mx[:, hs[0]:hs[-1] + 1, place],
                                      p_sn[:, k % 2, 0:w * len(hs)].rearrange("p (h w) -> p h w", w=w),
                                      AX.X, ALU.max).then_inc(sn_read, 1)
                    if k == MT_ITEM and not is_first(u):
                        maxima_row(u - 1)
                dve.wait_ge(sn_read, NI * (u + 1))
                dve.tensor_tensor(mx[:, :, 4:8], mx[:, :, 4:8], mx[:, :, 8:12], ALU.max).then_inc(mx_step, 1)
                dve.wait_ge(mx_step, 4 * u + 1)
                dve.tensor_scalar(mpart[:, 0], mx[:, :, 0:8], -1.0, None, ALU.mult).then_inc(mx_step, 1)
                dve.wait_ge(mx_step, 4 * u + 2)
                dve.scalar_tensor_tensor(out=mrest[:, :, :], in0=mx[:, :, 0:8], scalar=-1.0, in1=mpart[:, 0],
                                         op0=ALU.mult, op1=ALU.subtract).then_inc(mx_step, 1)
                dve.wait_ge(mx_step, 4 * u + 3)
                dve.tensor_copy(mpart[:, 1], mrest[:, :, :]).then_inc(mx_step, 1)
                dve.wait_ge(mx_step, 4 * u + 4)
                dve.tensor_tensor(mpart[:, 2], mrest[:, :, :], mpart[:, 1], ALU.subtract).then_inc(mp_done, 1)

            clear(dve)
            rotating(dve, maxima)
            maxima_row(U - 1)
            split(dve)

        @block.tensor
        def _(pe):
            def scores_by_query(u, s, k):
                segments, hs, w, place = items[k]
                if k == 0:
                    pe.wait_ge(kq_in, LOADS * (u + 1))
                if k >= 2 or not is_first(u):
                    pe.wait_ge(sn_read, NI * u + k - 1)
                if k == MT_ITEM + 2 and not is_first(u):
                    pe.wait_ge(mT_done, u)
                if k == MT_ITEM and not is_first(u):
                    maxima_by_row(u - 1)
                for h, qb, k0, kw, col in segments:
                    out = p_sn[:, k % 2, col:col + kw]
                    diagonal = k0 + kw == (qb + 1) * P
                    mm = pe.matmul(out, Qst[0:ROWS, s, h, qb * P:(qb + 1) * P], Kst[0:ROWS, s, h, k0:k0 + kw],
                                   start=True, stop=True, skip_group_check=True)
                    if diagonal:
                        mm = pe.matmul(p_sn[:, k % 2, col + kw - P:col + kw], g["identb"][:, :], g["maskb"][:, :],
                                       start=False, stop=True, skip_group_check=True)
                mm.then_inc(sn_done, 1)

            def maxima_by_row(u):
                pe.wait_ge(mp_done, u + 1)
                pe.transpose(p_mT, mpart[:, :, :, :].rearrange("p r h q -> p (r h q)"),
                             g["identb"][:, :]).then_inc(mr_done, 1)

            def scores_by_key(u, s, i):
                kb, h = steps[i]
                if not (is_first(u) and i < 2):
                    pe.wait_ge(exp_done, NS * u + i - 1)
                if kb < 4:
                    spans = [(h, 0, kb * P, 512), (h, 1, 0, 512)]
                else:
                    spans = [(h + j, j, kb * P - 512, 512) for j in range(2)]
                for hh, bank, a, b in spans:
                    q0 = a + (512 * bank if kb < 4 else 512)
                    mm = pe.matmul(p_st[:, i % 2, bank, a:b], Kst[0:ROWS + MROWS, s, hh, kb * P:(kb + 1) * P],
                                   Qst[0:ROWS + MROWS, s, hh, q0:q0 + b - a], start=True, stop=True)
                mm.then_inc(st_done, 1)

            def values(u, s, kb, c):
                if c == kb // 4:
                    pe.wait_ge(mask_done, QB * u + kb + 1)
                if kb == 0 and c == 0:
                    pe.wait_ge(v_in, 16 * (u + 1))
                    if not is_first(u):
                        pe.wait_ge(o_copied[0], u)
                        pe.wait_ge(o_copied[1], u)
                a = max(kb * P - 512 * c, 0)
                for h in range(HG):
                    mm = pe.matmul(p_o[PAD * h:PAD * (h + 1), c, a:512], Vst[:, s, kb, PAD * h:PAD * (h + 1)],
                                   weights(kb, h, 512 * c + a, 512 * (c + 1)),
                                   start=(kb == 0), stop=(kb == 4 * c + 3))
                if c == 1:
                    mm.then_inc(pv_done, 1)

            SHARE = 4
            after = {ends[kb + 1] - 1: kb for kb in range(4)}
            after.update({ends[0] - 1: 7, ends[5]: 4, ends[6]: 5, NS - 1: 6})
            work = []
            for i, (kb, h) in enumerate(steps):
                work.append(("scores", i, None, SHARE * (QB - kb) * (1 if kb < 4 else 2)))
                if i in after:
                    kb = after[i]
                    work += [("values", kb, c, HG * (4 - max(kb - 4 * c, 0))) for c in range(kb // 4, 2)]
            total = sum(w[-1] for w in work)

            for k in range(NI):
                scores_by_query(0, 0, k)
            for k in range(AHEAD):
                scores_by_query(1, 1, k)
            pe.wait_ge(ones_done, 1)

            def step(u, s):
                pe.wait_ge(m_in, 48 * (u + 1))
                done = spent = 0
                left = U - 1 - u if isinstance(u, int) else U
                count = NI if left >= 2 else NI - AHEAD if left == 1 else 0
                for kind, i, c, cost in work:
                    if kind == "scores":
                        scores_by_key(u, s, i)
                    elif i < QB - 1:
                        values(u, s, i, c)
                    elif not is_first(u):
                        values(u - 1, (s + 2) % 3, i, c)
                    spent += cost
                    while done < min(count, NI * spent // total):
                        k = AHEAD + done
                        if k < NI:
                            scores_by_query(u + 1, (s + 1) % 3, k)
                        else:
                            scores_by_query(u + 2, (s + 2) % 3, k - NI)
                        done += 1
                    if left == 1 and done == count:
                        maxima_by_row(u + 1)
                        left = 0

            rotating(pe, step)
            values(U - 1, (U - 1) % 3, QB - 1, 1)


def tile_of(t, j):
    return t[:, bass.ds(j, 1), :].rearrange("p a d -> p (a d)")


def project_out(nc, mem, g, o_dram):
    W = HG * P
    Ot = mem.sb("Ot", [P, 2, HG, P])
    rec = mem.sb("rec", [P, 2, H])
    On = mem.sb("On", [P, 2, D])
    OnT = mem.sb("OnT", [P, 2, D])
    wo = mem.sb("wo", [P, KD, D])
    p_r = mem.ps("p_r", [P, 2, W])
    p_t = mem.ps("p_t", [P, 2, 512])
    p_x = mem.ps("p_x", [P, 2, 512])
    w_in = mem.sem("w_in")
    o_in = [mem.sem(f"o_in{s}") for s in range(2)]
    rows_done, rec_done, on_done, onT_done, t_done, px_done, x_done, st_done = (
        mem.sem(s) for s in ("rows_d", "rec_d", "on_d", "onT_d", "t_d", "px_d", "x_d", "st_d"))

    with nc.Block() as block:
        @block.sync
        def _(sp):
            sp.dma_start(wo[:, :, :], g["WoT"].rearrange("(k p) n -> p k n", p=P)).then_inc(w_in, 16)

            def step(j, s, first, last):
                if not first:
                    sp.wait_ge(rows_done, j - 1)
                src = o_dram[bass.ds((j // QB) * HG, HG), :, bass.ds((j % QB) * P, P)]
                sp.dma_start(Ot[:, s], src.rearrange("u p t -> p u t")).then_inc(o_in[s], 16)
                if s == 1:
                    e, k = j // (NT // E), (j // 2) % 2
                    sp.dma_start(g["w1"][:, bass.ds(e, 1), bass.ds(k, 1), :].rearrange("p e k n -> p (e k n)"),
                                 g["mlp1"][bass.ds(e, 1), bass.ds(k * P, P), :].rearrange("e p n -> p (e n)")
                                 ).then_inc(g["w_in"], 16)
                    sp.dma_start(g["w2"][:, bass.ds(e, 1), bass.ds(2 * k, 2), :].rearrange("p e k n -> p (e k) n"),
                                 g["mlp2"][bass.ds(e, 1), bass.ds(2 * k * P, 2 * P), :]
                                 .rearrange("e (k p) n -> p (e k) n", p=P)).then_inc(g["w_in"], 16)
            paired(sp, NT, step)

        @block.tensor
        def _(pe):
            pe.wait_ge(w_in, 16)

            def turn(j, s):
                pe.wait_ge(on_done, j + 1)
                for k in range(KD):
                    mm = pe.transpose(p_t[:, s, k * P:(k + 1) * P], On[:, s, k * P:(k + 1) * P], g["ident"][:, :])
                mm.then_inc(t_done, 1)

            def multiply(j, s):
                pe.wait_ge(onT_done, j + 1)
                for k in range(KD):
                    mm = pe.matmul(p_x[:, s, 0:D], OnT[:, s, k * P:(k + 1) * P], wo[:, k, :],
                                   start=(k == 0), stop=(k == KD - 1))
                mm.then_inc(px_done, 1)

            def step(j, s, first, last):
                pe.wait_ge(o_in[s], 8 * (j - s) + 16)
                if not first:
                    pe.wait_ge(on_done, j - 1)
                for u in range(HG):
                    mm = pe.transpose(p_r[:, s, u * P:(u + 1) * P], Ot[:, s, u, :], g["ident"][:, :])
                mm.then_inc(rows_done, 1)
                if not (first and s == 0):
                    turn(j - 1, 1 - s)
                if not first:
                    multiply(j - 2, s)
            paired(pe, NT, step)
            turn(NT - 1, 1)
            for t in range(NT - 2, NT):
                pe.wait_ge(x_done, t - 1)
                multiply(t, t % 2)

        @block.scalar
        def _(act):
            def step(j, s, first, last):
                act.wait_ge(t_done, j + 1)
                act.copy(OnT[:, s, :], p_t[:, s, 0:D]).then_inc(onT_done, 1)
            paired(act, NT, step)

        @block.vector
        def _(dve):
            def add(j, s):
                dve.wait_ge(px_done, j + 1)
                x = tile_of(g["X"], j)
                dve.tensor_tensor(x, p_x[:, s, 0:D], x, ALU.add).then_inc(x_done, 1)

            def step(j, s, first, last):
                dve.wait_ge(rows_done, j + 1)
                rows = p_r[:, s, :].rearrange("p (h c) -> p h c", c=PAD)
                dve.reciprocal(rec[:, s, :], rows[:, :, DK]).then_inc(rec_done, 1)
                dve.wait_ge(rec_done, j + 1)
                dve.tensor_tensor(On[:, s, :].rearrange("p (h d) -> p h d", d=DK), rows[:, :, 0:DK],
                                  rec[:, s, :].unsqueeze(2).to_broadcast([P, H, DK]), ALU.mult).then_inc(on_done, 1)
                if not (isinstance(j, int) and j < 3):
                    dve.wait_ge(x_done, j - 2)
                    dve.nop(nofuse=True)
                    dve.bn_stats(tile_of(g["st6"], j - 3), tile_of(g["X"], j - 3))
                if not first:
                    add(j - 2, s)
            paired(dve, NT, step, 2)
            add(NT - 2, 0)
            add(NT - 1, 1)
            dve.wait_ge(x_done, NT)
            for j in range(NT - 3, NT):
                last = dve.bn_stats(g["st6"][:, j, :], g["X"][:, j, :])
            last.then_inc(st_done, 1)
            dve.wait_ge(st_done, 1)
            for j in range(NT):
                dve.bn_aggr(g["mv"][:, j, :], g["st6"][:, j, :])


def route(nc, mem, g, t_dram):
    Q = 2 * NT
    n = mem.sb("n", [P, 2, D])
    t = mem.sb("t", [P, 2, D])
    tT = mem.sb("tT", [P, 2, D])
    var1 = mem.sb("var1", [P, NT])
    root = mem.sb("root", [P, 2, NT])
    inv = mem.sb("inv", [P, 2, NT])
    srep = mem.sb("srep", [P, D])
    gw = mem.sb("gw", [P, KD, E])
    gb = mem.sb("gb", [P, E])
    L = mem.sb("L", [P, NT, E])
    work = mem.sb("work", [P, NT, E])
    oh = [mem.sb(f"oh{r}", [P, NT, E]) for r in range(2)]
    best = mem.sb("best", [P, 4, NT])
    picks = mem.sb("picks", [P, E, NT], BF16)
    tot = mem.sb("tot", [P, E, NT])
    cum = mem.sb("cum", [P, E, NT])
    cnt = mem.sb("cnt", [P, 6, E])
    tiles = mem.sb("tiles", [P, MT, E])
    fslot = mem.sb("fslot", [P, MT])
    slot = mem.sb("slot", [P, Q])
    slot_tile = mem.sb("slot_tile", [P, Q])
    slot_row = mem.sb("slot_row", [P, Q])
    in_row = mem.sb("in_row", [P, Q, P], BF16)
    free = g["R"][:, :, :].rearrange("p t d -> p (t d)").bitcast(BF16)
    marked = free[:, 0:Q * 2 * MT].rearrange("p (q c m) -> p q c m", c=2, m=MT)
    in_tile = free[:, Q * 2 * MT:Q * 3 * MT].rearrange("p (q m) -> p q m", m=MT)
    used = mem.sb("used", [P, MT])
    row = mem.sb("row", [P, 3, MT])
    diff = mem.sb("diff", [P, 3, NT])
    p_t = mem.ps("p_t", [P, 2, 512])
    p_l = mem.ps("p_l", [P, 512])
    p_c = mem.ps("p_c", [P, 2, 512])
    p_inv = mem.ps("p_inv", [P, 2, MT])
    c_in, chain, roots, n_done, t_done, added, tp_done, tT_done, l_done = (
        mem.sem(s) for s in ("c_in", "chain", "roots", "n_d", "t_d", "added", "tp_d", "tT_d", "l_d"))
    diff_done, exp_done, picks_done, counts_done = (mem.sem(s) for s in ("diff_d", "exp_d", "picks_d", "cnt_d"))
    kept, t_out, tile_done, low_done, inv_done = (mem.sem(s) for s in ("kept", "t_out", "tile_d", "low_d", "inv_d"))
    high_done = [mem.sem(f"high_d{r}") for r in range(2)]
    row_done = [mem.sem(f"row_d{r}") for r in range(2)]

    with nc.Block() as block:
        @block.sync
        def _(sp):
            sp.dma_start(srep[:, :], g["scale"].partition_broadcast(P)).then_inc(c_in, 16)
            sp.dma_start(gb[:, :], g["gate_b"].partition_broadcast(P)).then_inc(c_in, 16)
            sp.dma_start(gw[:, :, :], g["gate_w"].rearrange("(k p) e -> p k e", p=P)).then_inc(c_in, 16)
            with sp.Fori(0, NT // 4, 1) as c:
                sp.wait_ge(kept, 4 * c + 4)
                sp.nop(nofuse=True)
                sp.dma_start(t_dram[bass.ds(c * 4 * P, 4 * P), :].rearrange("(t p) d -> p t d", p=P),
                             g["R"][:, bass.ds(c * 4, 4), :]).then_inc(t_out, 16)
            sp.wait_ge(t_out, 16 * (NT // 4))

        @block.scalar
        def _(act):
            for r in range(2):
                act.wait_ge(chain, 1 if r == 0 else 4)
                act.activation(root[:, r, :], var1[:, :], ACT.Sqrt, bias=g["eps"][:, :]).then_inc(roots, 1)

            def step(j, s, first, last):
                act.wait_ge(t_done, j + 1)
                act.copy(tile_of(g["R"], j), t[:, s, :]).then_inc(kept, 1)
                act.wait_ge(tp_done, j + 1)
                act.copy(tT[:, s, :], p_t[:, s, 0:D]).then_inc(tT_done, 1)
            paired(act, NT, step)
            act.wait_ge(diff_done, 1)
            act.activation(diff[:, 1, :], diff[:, 0, :], ACT.Exp).then_inc(exp_done, 1)
            act.wait_ge(tile_done, 1)
            act.activation(marked[:, :, 1, :], in_tile, ACT.Copy, scale=g["row"][:, 0:1]).then_inc(low_done, 1)

        @block.vector
        def _(dve):
            count = [0]

            def link(ins):
                count[0] += 1
                ins.then_inc(chain, 1)
                dve.wait_ge(chain, count[0])

            link(dve.tensor_copy(var1[:, :], g["mv"][:, :, 1]))
            dve.wait_ge(roots, 1)
            link(dve.reciprocal(inv[:, 0, :], root[:, 0, :]))
            link(dve.tensor_tensor(var1[:, :], var1[:, :], inv[:, 0, :], ALU.mult))
            link(dve.tensor_tensor(var1[:, :], var1[:, :], inv[:, 0, :], ALU.mult))
            dve.wait_ge(roots, 2)
            link(dve.reciprocal(inv[:, 1, :], root[:, 1, :]))
            dve.wait_ge(c_in, 48)

            def normalise(j, s, first):
                if not first:
                    dve.wait_ge(added, j - 1)
                dve.tensor_scalar(n[:, s, :], tile_of(g["X"], j), g["mv"][:, bass.ds(j, 1), 0],
                                  inv[:, 0, bass.ds(j, 1)], ALU.subtract, ALU.mult).then_inc(n_done, 1)

            def scale(j, s, first):
                if not first:
                    dve.wait_ge(kept, j - 1)
                    dve.wait_ge(tp_done, j - 1)
                dve.wait_ge(n_done, j + 1)
                dve.scalar_tensor_tensor(out=t[:, s, :], in0=n[:, s, :], scalar=inv[:, 1, bass.ds(j, 1)],
                                         in1=srep[:, :], op0=ALU.mult, op1=ALU.mult).then_inc(t_done, 1)

            def step(j, s, first, last):
                if s == 1:
                    for part in (normalise, scale):
                        part(j - 1, 0, first)
                        part(j, 1, first)
            paired(dve, NT, step)

            dve.wait_ge(l_done, NT)
            link(dve.tensor_tensor(L[:, :, :], p_l[:, 0:NT * E].rearrange("p (i e) -> p i e", e=E),
                                   gb[:, :].unsqueeze(1).to_broadcast([P, NT, E]), ALU.add))
            rev = g["rev"][:, :].unsqueeze(1).to_broadcast([P, NT, E])
            for r in range(2):
                top, place = best[:, r, :], best[:, 2 + r, :]
                link(dve.tensor_reduce(top, L[:, :, :], AX.X, ALU.max))
                link(dve.tensor_tensor(work[:, :, :], L[:, :, :], top.unsqueeze(2).to_broadcast([P, NT, E]), ALU.is_ge))
                link(dve.tensor_tensor(work[:, :, :], work[:, :, :], rev, ALU.mult))
                link(dve.tensor_reduce(place, work[:, :, :], AX.X, ALU.max))
                link(dve.tensor_tensor(oh[r][:, :, :], rev, place.unsqueeze(2).to_broadcast([P, NT, E]), ALU.is_equal))
                if r == 0:
                    link(dve.scalar_tensor_tensor(out=L[:, :, :], in0=oh[0][:, :, :], scalar=NEG, in1=L[:, :, :],
                                                  op0=ALU.mult, op1=ALU.add))
            dve.tensor_tensor(diff[:, 0, :], best[:, 1, :], best[:, 0, :], ALU.subtract).then_inc(diff_done, 1)
            dve.tensor_tensor(picks[:, :, :], oh[0][:, :, :].rearrange("p i e -> p e i"),
                              oh[1][:, :, :].rearrange("p i e -> p e i"), ALU.add).then_inc(picks_done, 1)
            dve.wait_ge(exp_done, 1)
            link(dve.tensor_scalar(diff[:, 2, :], diff[:, 1, :], 1.0, None, ALU.add))
            link(dve.reciprocal(g["w"][:, 0, :], diff[:, 2, :]))
            link(dve.tensor_tensor(g["w"][:, 1, :], g["w"][:, 0, :], diff[:, 1, :], ALU.mult))
            dve.wait_ge(counts_done, 1)
            link(dve.tensor_copy(tot[:, :, :], p_c[:, 1, 0:E * NT].rearrange("p (e i) -> p e i", e=E)))
            flat = tot[:, :, :].rearrange("p e i -> p (e i)")
            link(dve.tensor_tensor_scan(cum[:, :, :].rearrange("p e i -> p (e i)"), g["ones"][:, 0:E * NT], flat,
                                        0.0, ALU.mult, ALU.add))
            link(dve.tensor_tensor(cum[:, :, :], cum[:, :, :], tot[:, :, :], ALU.subtract))
            link(dve.tensor_reduce(cnt[:, 0, :], tot[:, :, :], AX.X, ALU.add))
            cmp = work[:, :, :].rearrange("p i e -> p (i e)").rearrange("p (e i) -> p e i", e=E)
            link(dve.tensor_tensor(cmp, cnt[:, 0, :].unsqueeze(2).to_broadcast([P, E, NT]),
                                   g["tile_starts"][:, 0:NT].unsqueeze(1).to_broadcast([P, E, NT]), ALU.is_gt))
            link(dve.tensor_reduce(cnt[:, 1, :], cmp, AX.X, ALU.add))
            link(dve.tensor_tensor_scan(cnt[:, 2, :], g["ones"][:, 0:E], cnt[:, 1, :], 0.0, ALU.mult, ALU.add))
            link(dve.tensor_tensor(cnt[:, 3, :], cnt[:, 2, :], cnt[:, 1, :], ALU.subtract))
            link(dve.scalar_tensor_tensor(out=cnt[:, 4, :], in0=cnt[:, 3, :], scalar=float(P), in1=cum[:, :, 0],
                                          op0=ALU.mult, op1=ALU.subtract))
            link(dve.tensor_tensor(cum[:, :, :], cum[:, :, :], cnt[:, 4, :].unsqueeze(2).to_broadcast([P, E, NT]), ALU.add))
            link(dve.tensor_tensor(cum[:, :, :], p_c[:, 0, 0:E * NT].rearrange("p (e i) -> p e i", e=E), cum[:, :, :], ALU.add))
            for r in range(2):
                link(dve.tensor_tensor(work[:, :, :], oh[r][:, :, :], cum[:, :, :].rearrange("p e i -> p i e"), ALU.mult))
                link(dve.tensor_reduce(slot[:, r * NT:(r + 1) * NT], work[:, :, :], AX.X, ALU.add))
            link(dve.tensor_scalar(slot_tile[:, :], slot[:, :], 1.0 / P, 0.5 / P - 0.5, ALU.mult, ALU.add))
            link(dve.tensor_scalar(slot_tile[:, :], slot_tile[:, :], ROUND, None, ALU.add))
            link(dve.tensor_scalar(slot_tile[:, :], slot_tile[:, :], ROUND, None, ALU.subtract))
            link(dve.scalar_tensor_tensor(out=slot_row[:, :], in0=slot_tile[:, :], scalar=-float(P), in1=slot[:, :],
                                          op0=ALU.mult, op1=ALU.add))
            dve.wait_ge(t_out, 16 * (NT // 4))
            dve.tensor_tensor(in_tile, slot_tile[:, :].unsqueeze(2).to_broadcast([P, Q, MT]),
                              g["ramp"][:, 0:MT].unsqueeze(1).to_broadcast([P, Q, MT]), ALU.is_equal).then_inc(tile_done, 1)
            for r in range(2):
                half = slice(r * NT, (r + 1) * NT)
                dve.tensor_tensor(in_row[:, half, :], slot_row[:, half].unsqueeze(2).to_broadcast([P, NT, P]),
                                  g["ramp"][:, :].unsqueeze(1).to_broadcast([P, NT, P]), ALU.is_equal
                                  ).then_inc(row_done[r], 1)
                if r == 0:
                    dve.wait_ge(tile_done, 1)
                    dve.tensor_tensor(marked[:, NT:Q, 0, :], in_tile[:, NT:Q, :],
                                      g["place"][:, NT:Q].unsqueeze(2).to_broadcast([P, NT, MT]), ALU.mult
                                      ).then_inc(high_done[1], 1)
            link(dve.tensor_tensor(tiles[:, :, :], g["ramp"][:, 0:MT].unsqueeze(2).to_broadcast([P, MT, E]),
                                   cnt[:, 2, :].unsqueeze(1).to_broadcast([P, MT, E]), ALU.is_ge))
            link(dve.tensor_reduce(fslot[:, :], tiles[:, :, :], AX.X, ALU.add))
            link(dve.tensor_scalar(g["expert"][:, :], fslot[:, :], float(E - 1), None, ALU.min))
            dve.wait_ge(inv_done, 1)
            link(dve.tensor_scalar(used[:, :], p_inv[:, 0, :], 0.5, None, ALU.is_ge))
            link(dve.tensor_scalar(row[:, 0, :], p_inv[:, 0, :], float(P), -float(P), ALU.mult, ALU.add))
            link(dve.tensor_tensor(row[:, 0, :], p_inv[:, 1, :], row[:, 0, :], ALU.add))
            link(dve.tensor_tensor(row[:, 1, :], row[:, 0, :], g["spare"][:, :], ALU.subtract))
            link(dve.tensor_tensor(row[:, 1, :], row[:, 1, :], used[:, :], ALU.mult))
            link(dve.tensor_tensor(g["result"][:, :], row[:, 1, :], g["spare"][:, :], ALU.add))
            link(dve.tensor_scalar(row[:, 2, :], row[:, 0, :], float(T), -float(T), ALU.is_ge, ALU.mult))
            link(dve.tensor_tensor(row[:, 2, :], row[:, 2, :], row[:, 0, :], ALU.add))
            link(dve.tensor_scalar(g["token"][:, :], row[:, 2, :], 0.0, None, ALU.max))

        @block.tensor
        def _(pe):
            pe.wait_ge(c_in, 48)

            def logits(j, s):
                pe.wait_ge(tT_done, j + 1)
                for k in range(KD):
                    mm = pe.matmul(p_l[:, bass.ds(E * j, E)], tT[:, s, k * P:(k + 1) * P], gw[:, k, :],
                                   start=(k == 0), stop=(k == KD - 1), skip_group_check=True)
                mm.then_inc(l_done, 1)

            def step(j, s, first, last):
                pe.wait_ge(t_done, j + 1)
                if not first:
                    pe.wait_ge(tT_done, j - 1)
                for k in range(KD):
                    mm = pe.transpose(p_t[:, s, k * P:(k + 1) * P],
                                      t[:, s, k * P:(k + 1) * P], g["ident"][:, :])
                mm.then_inc(tp_done, 1)
                if not (first and s == 0):
                    logits(j - 1, 1 - s)
            paired(pe, NT, step)
            logits(NT - 1, 1)
            pe.wait_ge(picks_done, 1)
            flat = picks[:, :, :].rearrange("p e i -> p (e i)")
            pe.matmul(p_c[:, 0, 0:E * NT], g["before"][:, :], flat, start=True, stop=True)
            pe.matmul(p_c[:, 1, 0:E * NT], g["onesb"][:, :], flat, start=True, stop=True).then_inc(counts_done, 1)
            pe.wait_ge(low_done, 1)
            for q in range(Q):
                if q % NT == 0:
                    pe.wait_ge(high_done[q // NT], 1)
                    pe.wait_ge(row_done[q // NT], 1)
                mm = pe.matmul(p_inv[:, :, :].rearrange("p c m -> p (c m)"), in_row[:, q, :],
                               marked[:, q, :, :].rearrange("p c m -> p (c m)"), start=(q == 0), stop=(q == Q - 1))
            mm.then_inc(inv_done, 1)

        @block.gpsimd
        def _(pool):
            def step(j, s, first, last):
                pool.wait_ge(t_done, j + 1)
                x = tile_of(g["X"], j)
                pool.tensor_tensor(x, x, n[:, s, :], ALU.add).then_inc(added, 1)
            paired(pool, NT, step)
            pool.wait_ge(tile_done, 1)
            pool.tensor_tensor(marked[:, 0:NT, 0, :], in_tile[:, 0:NT, :],
                               g["place"][:, 0:NT].unsqueeze(2).to_broadcast([P, NT, MT]), ALU.mult
                               ).then_inc(high_done[0], 1)


def experts(nc, mem, g, t_dram, y_dram):
    xs = mem.sb("xs", [P, 2, D])
    tT = mem.sb("tT", [P, 2, D])
    glu = mem.sb("glu", [P, 2, I])
    sig = mem.sb("sig", [P, 2, I])
    lin = mem.sb("lin", [P, 2, I])
    hid = mem.sb("hid", [P, 2, I])
    hT = mem.sb("hT", [P, 2, I])
    y = mem.sb("y", [P, 2, D])
    b1 = g["R"][:, :, :].rearrange("p t d -> p (t d)").rearrange("p (e n) -> p e n", e=E)
    b_in, g_read, l_read = (mem.sem(s) for s in ("b_in", "g_read", "l_read"))
    p_g = mem.ps("p_g", [P, 2, I])
    p_l = mem.ps("p_l", [P, 2, I])
    p_t = mem.ps("p_t", [P, 512])
    p_h = mem.ps("p_h", [P, 512])
    p_y = mem.ps("p_y", [P, 512])
    xs_in = [mem.pool_dma_sem(f"xs_in{s}") for s in range(2)]
    y_out = [mem.pool_dma_sem(f"y_out{s}") for s in range(2)]
    tp_done, tT_done, g_done, l_done, glu_done, sig_done, lin_done, prod_done, hid_done, hp_done, hT_done, py_done, y_done = (
        mem.sem(s) for s in ("tp_d", "tT_d", "g_d", "l_d", "glu_d", "sig_d", "lin_d", "prod_d", "hid_d", "hp_d",
                             "hT_d", "py_d", "y_d"))

    with nc.Block() as block:
        @block.sync
        def _(sp):
            for e in range(E):
                sp.dma_start(b1[:, e, :], g["mlp1_b"][e, :].partition_broadcast(P)).then_inc(b_in, 16)

        @block.gpsimd
        def _(pool):
            def load(j):
                if j >= 2:
                    pool.wait_ge(tp_done, j - 1)
                pool.indirect_dma_start(out=xs[:, j % 2, :], out_offset=None, in_=t_dram,
                                        in_offset=bass.IndirectOffsetOnAxis(ap=g["token"][:, j:j + 1], axis=0)
                                        ).then_inc(xs_in[j % 2], 16)

            def store(j):
                pool.wait_ge(y_done, j + 1)
                pool.indirect_dma_start(out=y_dram, out_offset=bass.IndirectOffsetOnAxis(
                    ap=g["result"][:, j:j + 1], axis=0), in_=y[:, j % 2, :], in_offset=None
                ).then_inc(y_out[j % 2], 16)

            for j in range(MT + 4):
                if j < MT:
                    load(j)
                if j >= 4:
                    store(j - 4)
            for s in range(2):
                pool.wait_ge(y_out[s], 16 * MT // 2)

        @block.tensor
        def _(pe):
            pe.wait_ge(g["w_in"], 2 * 16 * NT // 2)

            def rows(j, s, first):
                pe.wait_ge(xs_in[s], 8 * (j - s) + 16)
                if not first:
                    pe.wait_ge(tT_done, j)
                for k in range(KD):
                    mm = pe.transpose(p_t[:, k * P:(k + 1) * P], xs[:, s, k * P:(k + 1) * P], g["ident"][:, :])
                mm.then_inc(tp_done, 1)

            def up(j, s, e, half, bank, done, read, first):
                if not first:
                    pe.wait_ge(read, j - 1)
                cols = slice(half * I, (half + 1) * I)
                for k in range(KD):
                    mm = pe.matmul(bank[:, s, :], tT[:, s, k * P:(k + 1) * P],
                                   g["w1"][:, bass.ds(e, 1), k, cols].rearrange("p a n -> p (a n)"),
                                   start=(k == 0), stop=(k == KD - 1))
                mm.then_inc(done, 1)

            def hidden_rows(j, s, first):
                pe.wait_ge(hid_done, j + 1)
                if not first:
                    pe.wait_ge(hT_done, j)
                for k in range(KI):
                    mm = pe.transpose(p_h[:, k * P:(k + 1) * P], hid[:, s, k * P:(k + 1) * P], g["ident"][:, :])
                mm.then_inc(hp_done, 1)

            def expert_of(j):
                return pe.value_load(g["expert"][0:1, bass.ds(j, 1)], min_val=0, max_val=E - 1)

            def down(j, s, e, first):
                pe.wait_ge(hT_done, j + 1)
                if not first:
                    pe.wait_ge(y_done, j)
                for k in range(KI):
                    pe.matmul(p_y[:, 0:D], hT[:, s, k * P:(k + 1) * P],
                              g["w2"][:, bass.ds(e, 1), k, :].rearrange("p a n -> p (a n)"), start=(k == 0), stop=False)
                pe.matmul(p_y[:, 0:D], g["pick_e"][:, bass.ds(e, 1), :].rearrange("p a n -> p (a n)"),
                          g["b2"][:, :], start=False, stop=True).then_inc(py_done, 1)

            rows(0, 0, True)
            even = [None]

            def step(j, s, first, last):
                e = expert_of(j)
                pe.wait_ge(tT_done, j + 1)
                if not (last and s == 1):
                    rows(j + 1, 1 - s, False)
                up(j, s, e, 0, p_g, g_done, g_read, first)
                if not (first and s == 0):
                    hidden_rows(j - 1, 1 - s, first)
                up(j, s, e, 1, p_l, l_done, l_read, first)
                if not (first and s == 0):
                    down(j - 1, 1 - s, even[0] if s == 1 else expert_of(j - 1), first)
                even[0] = e
            paired(pe, MT, step)
            hidden_rows(MT - 1, 1, False)
            e_last = expert_of(MT - 1)
            down(MT - 1, 1, e_last, False)

        @block.scalar
        def _(act):
            def rows(j, s, first):
                act.wait_ge(tp_done, j + 1)
                if not first:
                    act.wait_ge(l_done, j - 1)
                act.copy(tT[:, s, :], p_t[:, 0:D]).then_inc(tT_done, 1)

            def hidden(j, s, first):
                act.wait_ge(hp_done, j + 1)
                act.copy(hT[:, s, :], p_h[:, :]).then_inc(hT_done, 1)

            def result(j, s, first):
                act.wait_ge(py_done, j + 1)
                if not (isinstance(j, int) and j < 2):
                    act.wait_ge(y_out[s], 8 * (j - s))
                act.copy(y[:, s, :], p_y[:, 0:D]).then_inc(y_done, 1)

            rows(0, 0, True)

            def step(j, s, first, last):
                if not (last and s == 1):
                    rows(j + 1, 1 - s, first and s == 0)
                if not (first and s == 0):
                    hidden(j - 1, 1 - s, first)
                act.wait_ge(glu_done, j + 1)
                if not first:
                    act.wait_ge(hid_done, j - 1)
                act.activation(sig[:, s, :], glu[:, s, :], ACT.Sigmoid, scale=ALPHA).then_inc(sig_done, 1)
                if not (first and s == 0):
                    result(j - 1, 1 - s, first)
            paired(act, MT, step, 2)
            hidden(MT - 1, 1, False)
            result(MT - 1, 1, False)

        @block.vector
        def _(dve):
            dve.wait_ge(b_in, 16 * E)

            def step(j, s, first, last):
                e = dve.value_load(g["expert"][0:1, bass.ds(j, 1)], min_val=0, max_val=E - 1)

                def bias(half):
                    return b1[:, bass.ds(e, 1), half * I:(half + 1) * I].rearrange("p e n -> p (e n)")
                dve.wait_ge(g_done, j + 1)
                dve.tensor_tensor(glu[:, s, :], p_g[:, s, :], bias(0), ALU.add).then_inc(g_read, 1)
                dve.wait_ge(g_read, j + 1)
                dve.tensor_scalar(glu[:, s, :], glu[:, s, :], LIMIT, None, ALU.min).then_inc(glu_done, 1)
                dve.wait_ge(l_done, j + 1)
                dve.tensor_tensor(lin[:, s, :], p_l[:, s, :], bias(1), ALU.add).then_inc(l_read, 1)
                dve.wait_ge(l_read, j + 1)
                dve.tensor_scalar(lin[:, s, :], lin[:, s, :], LIMIT, -LIMIT, ALU.min, ALU.max).then_inc(lin_done, 1)
                dve.wait_ge(lin_done, j + 1)
                dve.scalar_tensor_tensor(out=lin[:, s, :], in0=lin[:, s, :], scalar=1.0, in1=glu[:, s, :],
                                         op0=ALU.add, op1=ALU.mult).then_inc(prod_done, 1)
                dve.wait_ge(prod_done, j + 1)
                dve.wait_ge(sig_done, j + 1)
                if not first:
                    dve.wait_ge(hp_done, j - 1)
                dve.tensor_tensor(hid[:, s, :], lin[:, s, :], sig[:, s, :], ALU.mult).then_inc(hid_done, 1)
            paired(dve, MT, step)


def combine(nc, mem, g, y_dram, out=None):
    CT = 4
    got = mem.sb("got", [P, 2, 2, CT, D])
    y_in = [mem.sem(f"y_in{s}") for s in range(2)]
    half_done, x_done, st_done, stored = (mem.sem(s) for s in ("half_d", "x_d", "st_d", "stored"))

    with nc.Block() as block:
        @block.sync
        def _(sp):
            def store(c):
                sp.wait_ge(x_done, CT * (c + 1))
                sp.dma_start(out[c * CT * P:(c + 1) * CT * P, :].rearrange("(t p) d -> p t d", p=P),
                             g["X"][:, CT * c:CT * (c + 1), :]).then_inc(stored, 16)

            for c in range(NT // CT):
                if c >= 2:
                    sp.wait_ge(x_done, CT * (c - 1))
                for r in range(2):
                    first = r * T + c * CT * P
                    sp.dma_start(got[:, c % 2, r], y_dram[first:first + CT * P, :].rearrange("(t p) d -> p t d", p=P)
                                 ).then_inc(y_in[c % 2], 16)
                if out is not None and c >= 1:
                    store(c - 1)
            if out is not None:
                store(NT // CT - 1)
                sp.wait_ge(stored, 16 * (NT // CT))

        @block.vector
        def _(dve):
            for c in range(NT // CT):
                tiles = range(c * CT, (c + 1) * CT)
                dve.wait_ge(y_in[c % 2], 32 * (c // 2 + 1))
                for r, done in enumerate((half_done, x_done)):
                    for i in tiles:
                        if r:
                            dve.wait_ge(half_done, i + 1)
                        x = g["X"][:, i, :]
                        dve.scalar_tensor_tensor(out=x, in0=got[:, c % 2, r, i % CT, :], scalar=g["w"][:, r, i:i + 1],
                                                 in1=x, op0=ALU.mult, op1=ALU.add).then_inc(done, 1)
                if out is None:
                    for i in tiles:
                        dve.wait_ge(x_done, i + 1)
                        last = dve.bn_stats(g["st6"][:, i, :], g["X"][:, i, :])
            if out is None:
                last.then_inc(st_done, 1)
                dve.wait_ge(st_done, 1)
                for i in range(NT):
                    dve.bn_aggr(g["mv"][:, i, :], g["st6"][:, i, :])


def attend_b(nc, mem, g, spent):
    SCALE = D ** -0.5
    before = list(spent)
    del spent[:]
    Mw = mem.sb("Mw", [P, KD, D])
    Nw = mem.sb("Nw", [P, KD, D])
    bias = mem.sb("bias", [P, D])
    std = mem.sb("std", [P, NT])
    inv = mem.sb("inv", [P, NT])
    n = mem.sb("n", [P, QB, D])
    nT = mem.sb("nT", [P, KD, S])
    gT = mem.sb("gT", [P, KD, S])
    wn = gT[:, 0, 0:3 * D].rearrange("p (m d) -> p m d", m=3), gT[:, 1, 0:3 * D].rearrange("p (m d) -> p m d", m=3)
    wfT = nT
    nsum = mem.sb("nsum", [P, KD])
    nsum_rep = mem.sb("nsum_rep", [P, KD, P])
    vsum = mem.sb("vsum", [P, D])
    small = mem.sb("small", [P, 2, 5])
    p_s = mem.ps("p_s", [P, 2, 2, 512])
    p_w = mem.ps("p_w", [P, 2, 512])
    p_v = mem.ps("p_v", [P, 512])
    IT = 8
    c_in, ww_done, ww_read, std_done, inv_done, n_done, nb_done, all_done = (
        mem.sem(s) for s in ("c_in", "ww_d", "ww_r", "std_d", "inv_d", "n_d", "nb_d", "all_d"))
    w_done = mem.sem("w_d")
    w_read = [mem.sem(f"w_r{s}") for s in range(2)]
    ns_done, rep_done, pv_done, vs_done = (mem.sem(s) for s in ("ns_d", "rep_d", "pv_d", "vs_d"))
    s_done, m_done, nm_done, e_done, r_done, t_done, h_done, st_done = (
        mem.sem(s) for s in ("s_d", "m_d", "nm_d", "e_d", "r_d", "t_d", "h_d", "st_d"))

    def batches(eng, body):
        body(0, True)
        with eng.Fori(1, B, 1) as b:
            body(b, False)

    def target(i):
        return (nT if i < 4 else gT)[:, (i % 4) // 2, i % 2 * 512:(i % 2 + 1) * 512]

    with nc.Block() as block:
        @block.sync
        def _(sp):
            w = g["w_qkv"].rearrange("(m k p) d -> k p m d", m=3, p=P)
            for k in range(KD):
                sp.dma_start(wn[k], w[k]).then_inc(c_in, 16)
                sp.dma_start(wfT[:, k, 0:D], g["w_fcT"][k * P:(k + 1) * P, :]).then_inc(c_in, 16)
            sp.dma_start(bias[:, :], g["b_fc"].partition_broadcast(P)).then_inc(c_in, 16)
            for s in before:
                sp.sem_clear(s)

        @block.gpsimd
        def _(pool):
            pool.wait_ge(c_in, 80)

            def body(b, first):
                pool.wait_ge(n_done, b + 1)
                pool.wait_ge(w_done, IT * b + 4)
                for t in range(QB):
                    last = pool.tensor_tensor(n[:, t, :], n[:, t, :], bias[:, :], ALU.add)
                last.then_inc(nb_done, 1)
            batches(pool, body)

        @block.scalar
        def _(act):
            act.activation(std[:, :], g["mv"][:, :, 1], ACT.Sqrt, bias=g["eps"][:, :]).then_inc(std_done, 1)

            def body(b, first):
                for i in range(0, IT, 2):
                    act.wait_ge(w_done, IT * b + i + 1)
                    act.copy(target(i), p_w[:, 0, :]).then_inc(w_read[0], 1)
                for q in range(QB):
                    s = q % 2
                    if not (first and q < 2):
                        act.wait_ge(t_done, QB * b + q - 1)
                    act.wait_ge(nm_done, QB * b + q + 1)
                    scores = p_s[:, s].rearrange("p a b -> p (a b)")
                    act.activation(scores, scores, ACT.Exp, scale=SCALE, bias=small[:, s, 1:2],
                                   accum_out=small[:, s, 2:3]).then_inc(e_done, 1)
            batches(act, body)

        @block.vector
        def _(dve):
            dve.wait_ge(std_done, 1)
            dve.reciprocal(inv[:, :], std[:, :]).then_inc(inv_done, 1)
            for i, w in enumerate((Mw, Nw)):
                for k in range(KD):
                    dve.wait_ge(ww_done, 2 * i + k + 1)
                    dve.tensor_copy(w[:, k, :], p_w[:, k, 0:D]).then_inc(ww_read, 1)
            dve.wait_ge(inv_done, 1)

            def body(b, first):
                if not first:
                    dve.wait_ge(h_done, QB * b)
                for t in range(QB):
                    j = b * QB + t
                    last = dve.tensor_scalar(n[:, t, :], tile_of(g["X"], j), g["mv"][:, bass.ds(j, 1), 0],
                                             inv[:, bass.ds(j, 1)], ALU.subtract, ALU.mult)
                last.then_inc(n_done, 1)
                for i in range(1, IT, 2):
                    dve.wait_ge(w_done, IT * b + i + 1)
                    dve.tensor_copy(target(i), p_w[:, 1, :]).then_inc(w_read[1], 1)
                dve.wait_ge(w_read[0], IT // 2 * b + 2)
                dve.wait_ge(w_read[1], IT // 2 * b + 2)
                dve.tensor_reduce(nsum[:, :], nT[:, :, :], AX.X, ALU.add).then_inc(ns_done, 1)
                dve.wait_ge(ns_done, b + 1)
                dve.tensor_copy(nsum_rep[:, :, :], nsum[:, :].unsqueeze(2).to_broadcast([P, KD, P])).then_inc(rep_done, 1)

                def maximum(q):
                    s = q % 2
                    dve.wait_ge(s_done, QB * b + q + 1)
                    dve.tensor_reduce(small[:, s, 0:1], p_s[:, s], AX.XY, ALU.max).then_inc(m_done, 1)
                    dve.wait_ge(m_done, QB * b + q + 1)
                    dve.tensor_scalar(small[:, s, 1:2], small[:, s, 0:1], -SCALE, None, ALU.mult).then_inc(nm_done, 1)

                def result(q):
                    s = q % 2
                    j = b * QB + q
                    dve.wait_ge(e_done, j + 1)
                    dve.reciprocal(small[:, s, 3:4], small[:, s, 2:3]).then_inc(r_done, 1)
                    dve.wait_ge(r_done, j + 1)
                    dve.tensor_tensor(small[:, s, 4:5], small[:, s, 2:3], small[:, s, 3:4], ALU.mult).then_inc(t_done, 1)
                    dve.wait_ge(t_done, j + 1)
                    dve.scalar_tensor_tensor(out=tile_of(g["R"], j), in0=vsum[:, :], scalar=small[:, s, 4:5],
                                             in1=n[:, q, :], op0=ALU.mult, op1=ALU.add).then_inc(h_done, 1)

                def statistics(q):
                    dve.bn_stats(tile_of(g["st6"], b * QB + q), tile_of(g["R"], b * QB + q)).then_inc(st_done, 1)

                maximum(0)
                dve.wait_ge(pv_done, b + 1)
                dve.tensor_copy(vsum[:, :], p_v[:, 0:D]).then_inc(vs_done, 1)
                dve.wait_ge(nb_done, b + 1)
                dve.wait_ge(vs_done, b + 1)
                for q in range(1, QB):
                    if q > 1:
                        dve.wait_ge(h_done, QB * b + q - 1)
                    maximum(q)
                    if q > 1:
                        statistics(q - 2)
                    result(q - 1)
                dve.wait_ge(h_done, QB * b + QB - 1)
                result(QB - 1)
                statistics(QB - 2)
            batches(dve, body)
            dve.wait_ge(h_done, NT)
            for b in range(B):
                j = b * QB + QB - 1
                last = dve.bn_stats(g["st6"][:, j, :], g["R"][:, j, :])
            last.then_inc(all_done, 1)
            dve.wait_ge(all_done, 1)
            dve.wait_ge(st_done, (QB - 1) * B)
            for j in range(NT):
                dve.bn_aggr(g["mv2"][:, j, :], g["st6"][:, j, :])

        @block.tensor
        def _(pe):
            pe.wait_ge(c_in, 80)
            for i in range(2):
                if i:
                    pe.wait_ge(ww_read, 2)
                for k in range(KD):
                    for e in range(KD):
                        lhs = wn[e][:, 2 * i, k * P:(k + 1) * P]
                        rhs = wn[e][:, 1, :] if i == 0 else wfT[:, e, 0:D]
                        mm = pe.matmul(p_w[:, k, 0:D], lhs, rhs, start=(e == 0), stop=(e == KD - 1))
                    mm.then_inc(ww_done, 1)
            pe.wait_ge(ww_read, 4)

            def body(b, first):
                def free(i):
                    if not (first and i < 2):
                        pe.wait_ge(w_read[i % 2], IT // 2 * b + i // 2)

                pe.wait_ge(n_done, b + 1)
                for i in range(4):
                    free(i)
                    k, half = i // 2, i % 2
                    for t in range(4):
                        mm = pe.transpose(p_w[:, i % 2, t * P:(t + 1) * P], n[:, 4 * half + t, k * P:(k + 1) * P],
                                          g["ident"][:, :])
                    mm.then_inc(w_done, 1)
                for i in range(4, IT):
                    free(i)
                    ko, half = (i - 4) // 2, i % 2
                    for k in range(KD):
                        mm = pe.matmul(p_w[:, i % 2, :], Mw[:, k, ko * P:(ko + 1) * P], nT[:, k, half * 512:(half + 1) * 512],
                                       start=(k == 0), stop=(k == KD - 1))
                    mm.then_inc(w_done, 1)
                for s in range(2):
                    pe.wait_ge(w_read[s], IT // 2 * (b + 1))
                for q in range(QB):
                    if not (first and q < 2):
                        pe.wait_ge(e_done, QB * b + q - 1)
                    for half in range(2):
                        for k in range(KD):
                            mm = pe.matmul(p_s[:, q % 2, half, :], gT[:, k, q * P:(q + 1) * P],
                                           nT[:, k, half * 512:(half + 1) * 512], start=(k == 0), stop=(k == KD - 1))
                    mm.then_inc(s_done, 1)
                    if q == 0:
                        pe.wait_ge(rep_done, b + 1)
                        if not first:
                            pe.wait_ge(vs_done, b)
                        for k in range(KD):
                            mm = pe.matmul(p_v[:, 0:D], nsum_rep[:, k, :], Nw[:, k, :], start=(k == 0), stop=(k == KD - 1))
                        mm.then_inc(pv_done, 1)
            batches(pe, body)


def add_b(nc, mem, g):
    a = mem.sb("a", [P, 2, D])
    std = mem.sb("std", [P, NT])
    inv = mem.sb("inv", [P, NT])
    gam = mem.sb("gam", [P, D])
    bet = mem.sb("bet", [P, D])
    c_in, std_done, inv_done, a_done, shifted, x_done, st_done = (
        mem.sem(s) for s in ("c_in", "std_d", "inv_d", "a_d", "shifted", "x_d", "st_d"))

    with nc.Block() as block:
        @block.sync
        def _(sp):
            sp.dma_start(gam[:, :], g["gamma"].partition_broadcast(P)).then_inc(c_in, 16)
            sp.dma_start(bet[:, :], g["beta"].partition_broadcast(P)).then_inc(c_in, 16)

        @block.scalar
        def _(act):
            act.activation(std[:, :], g["mv2"][:, :, 1], ACT.Sqrt, bias=g["eps"][:, :]).then_inc(std_done, 1)

        @block.gpsimd
        def _(pool):
            pool.wait_ge(c_in, 32)

            def step(j, s, first, last):
                x = tile_of(g["X"], j)
                pool.tensor_tensor(x, x, bet[:, :], ALU.add).then_inc(shifted, 1)
            paired(pool, NT, step)

        @block.vector
        def _(dve):
            dve.wait_ge(std_done, 1)
            dve.reciprocal(inv[:, :], std[:, :]).then_inc(inv_done, 1)
            dve.wait_ge(inv_done, 1)
            dve.wait_ge(c_in, 32)

            def finish(j, s):
                x = tile_of(g["X"], j)
                dve.wait_ge(a_done, j + 1)
                dve.wait_ge(shifted, j + 1)
                dve.scalar_tensor_tensor(out=x, in0=a[:, s, :], scalar=inv[:, bass.ds(j, 1)], in1=x,
                                         op0=ALU.mult, op1=ALU.add).then_inc(x_done, 1)

            def step(j, s, first, last):
                if not first:
                    dve.wait_ge(x_done, j - 1)
                dve.scalar_tensor_tensor(out=a[:, s, :], in0=tile_of(g["R"], j), scalar=g["mv2"][:, bass.ds(j, 1), 0],
                                         in1=gam[:, :], op0=ALU.subtract, op1=ALU.mult).then_inc(a_done, 1)
                if not first:
                    dve.bn_stats(tile_of(g["st6"], j - 2), tile_of(g["X"], j - 2))
                if not (first and s == 0):
                    finish(j - 1, 1 - s)
            paired(dve, NT, step)
            finish(NT - 1, 1)
            dve.wait_ge(x_done, NT)
            for j in range(NT - 2, NT):
                last = dve.bn_stats(g["st6"][:, j, :], g["X"][:, j, :])
            last.then_inc(st_done, 1)
            dve.wait_ge(st_done, 1)
            for j in range(NT):
                dve.bn_aggr(g["mv"][:, j, :], g["st6"][:, j, :])


def constants(nc, mem, g):
    g["ident"] = mem.sb("ident", [P, P])
    g["identb"] = mem.sb("identb", [P, P], BF16)
    g["maskb"] = mem.sb("maskb", [P, P], BF16)
    g["before"] = mem.sb("before", [P, P], BF16)
    g["onesb"] = mem.sb("onesb", [P, P], BF16)
    g["ones"] = mem.sb("ones", [P, E * NT])
    g["eps"] = mem.sb("eps", [P, 1])
    g["rev"] = mem.sb("rev", [P, E])
    g["tile_starts"] = mem.sb("tile_starts", [P, NT])
    g["ramp"] = mem.sb("ramp", [P, P])
    g["place"] = mem.sb("place", [P, 2 * NT])
    g["row"] = mem.sb("row", [P, 1])
    g["spare"] = mem.sb("spare", [P, MT])
    set_done, = (mem.sem(s) for s in ("set_d",))
    with nc.Block() as block:
        @block.gpsimd
        def _(pool):
            for name, value in (("ident", 0.0), ("identb", 0.0), ("maskb", 0.0), ("before", 1.0), ("onesb", 1.0),
                                ("ones", 1.0), ("eps", EPS)):
                pool.memset(g[name][:, :], value).then_inc(set_done, 1)
            pool.wait_ge(set_done, 7)
            for name in ("ident", "identb"):
                pool.affine_select(out=g[name][:, :], in_=g[name][:, :], compare_op=ALU.not_equal, fill=1.0, base=0,
                                   pattern=[[-1, P]], channel_multiplier=1)
            pool.affine_select(out=g["maskb"][:, :], in_=g["maskb"][:, :], compare_op=ALU.is_ge, fill=NEG, base=0,
                               pattern=[[-1, P]], channel_multiplier=1)
            pool.affine_select(out=g["before"][:, :], in_=g["before"][:, :], compare_op=ALU.is_gt, fill=0.0, base=0,
                               pattern=[[1, P]], channel_multiplier=-1)
            for name, base, by_row, step, count in (("rev", E, 0, -1, E), ("tile_starts", 0, 0, P, NT),
                                                    ("ramp", 0, 0, 1, P), ("place", 1, 0, 1, 2 * NT),
                                                    ("row", 0, 1, 1, 1), ("spare", 2 * T, 1, P, MT)):
                pool.iota(g[name][:, :], pattern=[[step, count]], base=base, channel_multiplier=by_row,
                          allow_small_or_imprecise_dtypes=True)


def program(nc, a, out):
    g = dict(a)
    qk_dram = nc.dram_tensor("qk_parts", [2, U, 3 * DK, HG, S], BF16).ap()
    v_dram = nc.dram_tensor("v_padded", [U, S, HG * PAD], F32).ap()
    o_dram = nc.dram_tensor("o_rows", [U, P, S], F32).ap()
    t_dram = nc.dram_tensor("t_rows", [T, D], F32).ap()
    y_dram = nc.dram_tensor("results", [2 * T + SLOTS, D], F32).ap()
    with ExitStack() as whole:
        keep = Mem(nc, whole)
        g["X"] = keep.sb("X", [P, NT, D])
        g["R"] = keep.sb("R", [P, NT, D])
        g["st6"] = keep.sb("st6", [P, NT, 6])
        g["mv"] = keep.sb("mv_all", [P, NT, 2])
        g["mv2"] = keep.sb("mv2_all", [P, NT, 2])
        g["w"] = keep.sb("w", [P, 2, NT])
        g["token"] = keep.sb("token", [P, MT], I32)
        g["result"] = keep.sb("result", [P, MT], I32)
        g["expert"] = keep.sb("expert", [P, MT], I32)
        g["b2"] = keep.sb("b2", [P, D], BF16)
        g["pick_e"] = keep.sb("pick_e", [P, E, P], BF16)
        g["w_in"] = keep.sem("w_in")
        constants(nc, keep, g)

        spent = []

        def phase(f, tag, *args, **kw):
            with ExitStack() as own:
                f(nc, Mem(nc, own, tag, spent, whole), g, *args, **kw)

        phase(project_qkv, "a1_", a["x"], qk_dram, v_dram)
        phase(attend_a, "a2_", qk_dram, v_dram, o_dram)
        g["w1"] = keep.sb("w1", [P, E, KD, 2 * I])
        g["w2"] = keep.sb("w2", [P, E, KI, D])
        phase(project_out, "a3_", o_dram)
        phase(route, "r1_", t_dram)
        phase(experts, "e1_", t_dram, y_dram)
        phase(combine, "c1_", y_dram)
        phase(attend_b, "b_", spent)
        phase(add_b, "ab_")
        phase(route, "r2_", t_dram)
        phase(experts, "e2_", t_dram, y_dram)
        phase(combine, "c2_", y_dram, out=out)


def laid_out(inputs):
    import numpy as np
    v = {k.split("_", 1)[1]: np.asarray(a) for k, a in inputs.items()}
    c = np.ascontiguousarray

    def by_dim(w):
        return c(w.reshape(D, D // (HG * DK), HG, DK).transpose(0, 1, 3, 2).reshape(D, D))
    m1 = v["ffn_mlp1_w"]
    b1 = v["ffn_mlp1_b"]
    return {
        "x": v["attn_a_x"].reshape(T, D),
        "WqT": by_dim(v["attn_a_Wq"].T), "WkT": by_dim(v["attn_a_Wk"].T), "WvT": c(v["attn_a_Wv"].T), "WoT": c(v["attn_a_Wo"].T),
        "w_qkv": c(v["attn_b_w_qkv"]), "w_fcT": c(v["attn_b_w_fc"].T),
        "b_fc": v["attn_b_b_fc"], "gamma": v["attn_b_gamma"], "beta": v["attn_b_beta"],
        "scale": v["ffn_norm_scale"], "gate_w": v["ffn_gate_w"], "gate_b": v["ffn_gate_b"],
        "mlp1": c(m1.reshape(E, D, I, 2).transpose(0, 1, 3, 2).reshape(E, D, 2 * I)),
        "mlp1_b": c(b1.reshape(E, I, 2).transpose(0, 2, 1).reshape(E, 2 * I)),
        "mlp2": c(v["ffn_mlp2_w"]), "mlp2_b": v["ffn_mlp2_b"],
    }


def kernel(**inputs):
    import concourse.bacc as bacc
    from concourse.bass_utils import run_bass_kernel_spmd

    nc = bacc.Bacc("TRN2", target_bir_lowering=False, num_devices=1)
    arrays = laid_out(inputs)
    aps = {k: nc.dram_tensor(f"in_{k}", a.shape, mybir.dt.from_np(a.dtype), kind="ExternalInput").ap()
           for k, a in arrays.items()}
    out = nc.dram_tensor("out", (T, D), F32, kind="ExternalOutput").ap()
    program(nc, aps, out)
    r = run_bass_kernel_spmd(nc, [{f"in_{k}": a for k, a in arrays.items()}], core_ids=[0])
    return r.results[0]["out"].reshape(B, S, D)
```
